# Optimizing a Trainium2 kernel written in Bass

```python
import numpy as np
import jax
import jax.numpy as jnp

def _softmax(x, axis=-1):
    return jax.nn.softmax(x, axis=axis)

def _gelu(x):
    return jax.nn.gelu(x, approximate=True)

def _silu(x):
    return jax.nn.silu(x)

def _sigmoid(x):
    return jax.nn.sigmoid(x)

def _layernorm(x, axis=-1, eps=1e-05):
    m = jnp.mean(x, axis=axis, keepdims=True)
    v = jnp.var(x, axis=axis, keepdims=True)
    return (x - m) / jnp.sqrt(v + eps)

def _scatter_add(tgt, idx, src, axis=0):
    return tgt.at[idx].add(src)

def _segment_sum(src, seg, n):
    return jax.ops.segment_sum(src, seg, n)
kernel_name = 'mk_early_fusion_d4_tok_img256_r4_555438'

def setup_inputs(seed: int=0):
    np.random.seed(seed)
    _w = jnp.asarray

    def _rec_inputs():
        import jax
        import jax.numpy as jnp
        _rk = jax.random.key(seed)
        x = -0.000392918 + 0.999932 * jax.random.normal(jax.random.fold_in(_rk, 1), (4, 1, 128, 512), jnp.float32)
        txt = 6.72731e-05 + 1.00306 * jax.random.normal(jax.random.fold_in(_rk, 2), (4, 512, 64), jnp.float32)
        return (x, txt)
    x, txt = _rec_inputs()

    def _L0_tok_setup():
        import jax, jax.numpy as jnp
        import numpy as np
        PATCH = 8
        EMBED = 64
        N_MELS = 128
        N_FRAMES = 512
        BATCH = 64
        NUM_PATCHES = N_MELS // PATCH * (N_FRAMES // PATCH)
        key = jax.random.key(seed)
        k1, k2, k3, k4 = jax.random.split(key, 4)
        x = jax.random.normal(k1, (BATCH, 1, N_MELS, N_FRAMES), dtype=jnp.float32)
        W = jax.random.normal(k2, (EMBED, PATCH * PATCH), dtype=jnp.float32) * (1.0 / np.sqrt(PATCH * PATCH))
        b = jax.random.normal(k3, (EMBED,), dtype=jnp.float32) * 0.01
        pos_embed = jax.random.normal(k4, (1, NUM_PATCHES, EMBED), dtype=jnp.float32) * 0.02
        return {'x': x, 'W': W, 'b': b, 'pos_embed': pos_embed}
    _L0_tok_all = _L0_tok_setup()
    _L0_tok_in = {k: v for k, v in _L0_tok_all.items() if k in ('W', 'b', 'pos_embed')}
    del _L0_tok_all

    def _L0_attn_setup():
        import jax, jax.numpy as jnp
        import numpy as np
        B, N, H = (4, 1024, 64)
        key = jax.random.key(seed)
        ks = jax.random.split(key, 7)
        s = 1.0 / np.sqrt(H)
        return {'x': jax.random.normal(ks[0], (B, N, H), dtype=jnp.float32), 'Wq': jax.random.uniform(ks[1], (H, H), jnp.float32, -s, s), 'bq': jax.random.uniform(ks[2], (H,), jnp.float32, -s, s), 'Wk': jax.random.uniform(ks[3], (H, H), jnp.float32, -s, s), 'bk': jax.random.uniform(ks[4], (H,), jnp.float32, -s, s), 'Wv': jax.random.uniform(ks[5], (H, H), jnp.float32, -s, s), 'bv': jax.random.uniform(ks[6], (H,), jnp.float32, -s, s)}
    _L0_attn_all = _L0_attn_setup()
    _L0_attn_in = {k: v for k, v in _L0_attn_all.items() if k in ('Wq', 'bq', 'Wk', 'bk', 'Wv', 'bv')}
    del _L0_attn_all

    def _L0_ffn_setup():
        import math
        import jax, jax.numpy as jnp
        import numpy as np
        CAPACITY_FACTOR = 1.25
        TOP_K = 2
        LN_EPS = 1e-05

        def _layer_norm(x, gamma, beta):
            mu = jnp.mean(x, axis=-1, keepdims=True)
            var = jnp.var(x, axis=-1, keepdims=True)
            return (x - mu) * jax.lax.rsqrt(var + LN_EPS) * gamma + beta
        key = jax.random.key(seed)
        ks = jax.random.split(key, 4)
        B, S, D, F, E = (8, 1024, 64, 128, 8)
        x = jax.random.normal(ks[0], (B, S, D), dtype=jnp.float32)
        Wr = jax.random.normal(ks[1], (D, E), dtype=jnp.float32) / np.sqrt(D)
        br = jnp.zeros((E,), jnp.float32)
        W1 = jax.random.normal(ks[2], (E, D, F), dtype=jnp.float32) / np.sqrt(D)
        b1 = jnp.zeros((E, F), jnp.float32)
        W2 = jax.random.normal(ks[3], (E, F, D), dtype=jnp.float32) / np.sqrt(F)
        b2 = jnp.zeros((E, D), jnp.float32)
        gamma = jnp.ones((D,), jnp.float32)
        beta = jnp.zeros((D,), jnp.float32)
        return {'x': x, 'Wr': Wr, 'br': br, 'W1': W1, 'b1': b1, 'W2': W2, 'b2': b2, 'gamma': gamma, 'beta': beta}
    _L0_ffn_all = _L0_ffn_setup()
    _L0_ffn_in = {k: v for k, v in _L0_ffn_all.items() if k in ('Wr', 'br', 'W1', 'b1', 'W2', 'b2', 'gamma', 'beta')}
    del _L0_ffn_all

    def _L1_attn_setup():
        import jax, jax.numpy as jnp
        import numpy as np
        DIM = 64
        DIM_HEAD = 32
        NUM_HEADS = DIM // DIM_HEAD
        SCALE = DIM_HEAD ** (-0.5)
        key = jax.random.key(seed)
        ks = jax.random.split(key, 5)
        B, L, C = (4, 512, DIM)
        x = jax.random.normal(ks[0], (B, L, C), dtype=jnp.float32)
        w_qkv = jax.random.normal(ks[1], (3 * C, C), dtype=jnp.float32) * C ** (-0.5)
        b_qkv = jax.random.normal(ks[2], (3 * C,), dtype=jnp.float32) * 0.02
        w_proj = jax.random.normal(ks[3], (C, C), dtype=jnp.float32) * C ** (-0.5)
        b_proj = jax.random.normal(ks[4], (C,), dtype=jnp.float32) * 0.02
        return {'x': x, 'w_qkv': w_qkv, 'b_qkv': b_qkv, 'w_proj': w_proj, 'b_proj': b_proj}
    _L1_attn_all = _L1_attn_setup()
    _L1_attn_in = {k: v for k, v in _L1_attn_all.items() if k in ('w_qkv', 'b_qkv', 'w_proj', 'b_proj')}
    del _L1_attn_all

    def _L1_ffn_setup():
        import jax, jax.numpy as jnp
        import numpy as np
        B, T, IN_DIM = (64, 64, 64)
        HID, OUT_DIM = (128, 64)
        N_LAYERS, N_EXPERTS, N_SHARED = (2, 16, 1)
        key = jax.random.key(seed)
        ks = jax.random.split(key, 10)
        s = 0.02
        x = jax.random.normal(ks[0], (B, T, IN_DIM), dtype=jnp.float32)
        route_id = jax.random.randint(ks[1], (B,), 0, N_EXPERTS)
        Wi = jax.random.normal(ks[2], (HID, IN_DIM), dtype=jnp.float32) * s
        bi = jnp.zeros((HID,), dtype=jnp.float32)
        Wr = jax.random.normal(ks[3], (N_LAYERS, N_EXPERTS, HID, HID), dtype=jnp.float32) * s
        br = jax.random.normal(ks[4], (N_LAYERS, N_EXPERTS, HID), dtype=jnp.float32) * s
        Ws = jax.random.normal(ks[5], (N_LAYERS, N_SHARED, HID, HID), dtype=jnp.float32) * s
        bs = jax.random.normal(ks[6], (N_LAYERS, N_SHARED, HID), dtype=jnp.float32) * s
        Wo = jax.random.normal(ks[7], (OUT_DIM, HID), dtype=jnp.float32) * s
        bo = jnp.zeros((OUT_DIM,), dtype=jnp.float32)
        return {'x': x, 'route_id': route_id, 'Wi': Wi, 'bi': bi, 'Wr': Wr, 'br': br, 'Ws': Ws, 'bs': bs, 'Wo': Wo, 'bo': bo}
    _L1_ffn_all = _L1_ffn_setup()
    _L1_ffn_in = {k: v for k, v in _L1_ffn_all.items() if k in ('route_id', 'Wi', 'bi', 'Wr', 'br', 'Ws', 'bs', 'Wo', 'bo')}
    del _L1_ffn_all

    def _L2_attn_setup():
        import jax, jax.numpy as jnp
        import numpy as np
        B, N, D, TOP_K = (4, 1024, 64, 64)
        EPS = 1e-12
        key = jax.random.key(seed)
        kx, kw, kb = jax.random.split(key, 3)
        x = jax.random.normal(kx, (B, N, D), dtype=jnp.float32)
        lim = 1.0 / np.sqrt(D)
        W = jax.random.uniform(kw, (D, D), dtype=jnp.float32, minval=-lim, maxval=lim)
        b = jax.random.uniform(kb, (D,), dtype=jnp.float32, minval=-lim, maxval=lim)
        return {'x': x, 'W': W, 'b': b}
    _L2_attn_all = _L2_attn_setup()
    _L2_attn_in = {k: v for k, v in _L2_attn_all.items() if k in ('W', 'b')}
    del _L2_attn_all

    def _L2_ffn_setup():
        import jax, jax.numpy as jnp
        import numpy as np
        B, K, D = (128, 16, 64)
        E = 32
        H = int(D * 0.25)
        key = jax.random.key(seed)
        ks = jax.random.split(key, 7)
        d_rs = D ** (-0.5)
        h_rs = H ** (-0.5)
        x = jax.random.normal(ks[0], (B, K, D), dtype=jnp.float32)
        router_w = jax.random.uniform(ks[1], (E, D), jnp.float32, -d_rs, d_rs)
        router_b = jax.random.uniform(ks[2], (E,), jnp.float32, -d_rs, d_rs)
        W1 = jax.random.uniform(ks[3], (E, D, H), jnp.float32, -h_rs, h_rs)
        b1 = jax.random.uniform(ks[4], (E, H), jnp.float32, -h_rs, h_rs)
        W2 = jax.random.uniform(ks[5], (E, H, D), jnp.float32, -d_rs, d_rs)
        b2 = jax.random.uniform(ks[6], (E, D), jnp.float32, -d_rs, d_rs)
        return {'x': x, 'router_w': router_w, 'router_b': router_b, 'W1': W1, 'b1': b1, 'W2': W2, 'b2': b2}
    _L2_ffn_all = _L2_ffn_setup()
    _L2_ffn_in = {k: v for k, v in _L2_ffn_all.items() if k in ('router_w', 'router_b', 'W1', 'b1', 'W2', 'b2')}
    del _L2_ffn_all

    def _L3_attn_setup():
        import jax, jax.numpy as jnp
        import numpy as np
        NUM_HEADS = 4
        LN_EPS = 1e-05

        def positional_encoding(length, d_model):
            pos = jnp.arange(length, dtype=jnp.float32)[:, None]
            div = jnp.exp(jnp.arange(0, d_model, 2, dtype=jnp.float32) * (-np.log(10000.0) / d_model))
            pe = jnp.zeros((length, d_model), dtype=jnp.float32)
            pe = pe.at[:, 0::2].set(jnp.sin(pos * div))
            pe = pe.at[:, 1::2].set(jnp.cos(pos * div))
            return pe

        def rel_shift(pos_score):
            B, H, S, _ = pos_score.shape
            padded = jnp.pad(pos_score, ((0, 0), (0, 0), (0, 0), (1, 0)))
            padded = padded.reshape(B, H, S + 1, S)
            return padded[:, :, 1:].reshape(B, H, S, S)
        key = jax.random.key(seed)
        ks = jax.random.split(key, 8)
        B, S, D, H = (8, 512, 64, NUM_HEADS)
        dh = D // H
        s = 0.02
        return {'inputs': jax.random.normal(ks[0], (B, S, D), dtype=jnp.float32), 'ln_gamma': jnp.ones((D,), jnp.float32), 'ln_beta': jnp.zeros((D,), jnp.float32), 'Wq': jax.random.normal(ks[1], (D, D), jnp.float32) * s, 'bq': jnp.zeros((D,), jnp.float32), 'Wk': jax.random.normal(ks[2], (D, D), jnp.float32) * s, 'bk': jnp.zeros((D,), jnp.float32), 'Wv': jax.random.normal(ks[3], (D, D), jnp.float32) * s, 'bv': jnp.zeros((D,), jnp.float32), 'Wpos': jax.random.normal(ks[4], (D, D), jnp.float32) * s, 'u_bias': jax.random.normal(ks[5], (H, dh), jnp.float32) * s, 'v_bias': jax.random.normal(ks[6], (H, dh), jnp.float32) * s, 'Wout': jax.random.normal(ks[7], (D, D), jnp.float32) * s, 'bout': jnp.zeros((D,), jnp.float32)}
    _L3_attn_all = _L3_attn_setup()
    _L3_attn_in = {k: v for k, v in _L3_attn_all.items() if k in ('ln_gamma', 'ln_beta', 'Wq', 'bq', 'Wk', 'bk', 'Wv', 'bv', 'Wpos', 'u_bias', 'v_bias', 'Wout', 'bout')}
    del _L3_attn_all

    def _L3_ffn_setup():
        import jax, jax.numpy as jnp
        import numpy as np
        B, T, C = (64, 96, 64)
        NH, NKV = (4, 2)
        HD = C // NH
        NREP = NH // NKV
        NE, TOPK = (8, 2)
        HID = int(8 / 3 * C)
        EPS_RMS = 1e-06

        def _rope_tables(t_len):
            inv_freq = 1.0 / 10000.0 ** (np.arange(0, HD, 2, dtype=np.float32) / HD)
            t = np.arange(t_len, dtype=np.float32)
            freqs = np.outer(t, inv_freq)
            emb = np.concatenate([freqs, freqs], axis=-1)
            return (jnp.asarray(np.cos(emb)), jnp.asarray(np.sin(emb)))

        def _rotate_half(x):
            h = x.shape[-1] // 2
            return jnp.concatenate([-x[..., h:], x[..., :h]], axis=-1)

        def _rmsnorm(v, w):
            return v * jax.lax.rsqrt(jnp.mean(v * v, axis=-1, keepdims=True) + EPS_RMS) * w
        key = jax.random.key(seed)
        ks = jax.random.split(key, 10)
        s = lambda k, shape: jax.random.normal(k, shape, jnp.float32) * 0.02
        return {'x': jax.random.normal(ks[0], (B, T, C), jnp.float32), 'ln1_w': jnp.ones((C,), jnp.float32), 'ln2_w': jnp.ones((C,), jnp.float32), 'wq': s(ks[1], (NH * HD, C)), 'wk': s(ks[2], (NKV * HD, C)), 'wv': s(ks[3], (NKV * HD, C)), 'wo': s(ks[4], (C, C)), 'router_w': s(ks[5], (NE, C)), 'w1': s(ks[6], (NE, HID, C)), 'w2': s(ks[7], (NE, C, HID)), 'w3': s(ks[8], (NE, HID, C))}
    _L3_ffn_all = _L3_ffn_setup()
    _L3_ffn_in = {k: v for k, v in _L3_ffn_all.items() if k in ('ln1_w', 'ln2_w', 'wq', 'wk', 'wv', 'wo', 'router_w', 'w1', 'w2', 'w3')}
    del _L3_ffn_all
    return {'x': x, 'txt': txt, 'L0_tok_W': _L0_tok_in['W'], 'L0_tok_b': _L0_tok_in['b'], 'L0_tok_pos_embed': _L0_tok_in['pos_embed'], 'L0_attn_Wq': _L0_attn_in['Wq'], 'L0_attn_bq': _L0_attn_in['bq'], 'L0_attn_Wk': _L0_attn_in['Wk'], 'L0_attn_bk': _L0_attn_in['bk'], 'L0_attn_Wv': _L0_attn_in['Wv'], 'L0_attn_bv': _L0_attn_in['bv'], 'L0_ffn_Wr': _L0_ffn_in['Wr'], 'L0_ffn_br': _L0_ffn_in['br'], 'L0_ffn_W1': _L0_ffn_in['W1'], 'L0_ffn_b1': _L0_ffn_in['b1'], 'L0_ffn_W2': _L0_ffn_in['W2'], 'L0_ffn_b2': _L0_ffn_in['b2'], 'L0_ffn_gamma': _L0_ffn_in['gamma'], 'L0_ffn_beta': _L0_ffn_in['beta'], 'L1_attn_w_qkv': _L1_attn_in['w_qkv'], 'L1_attn_b_qkv': _L1_attn_in['b_qkv'], 'L1_attn_w_proj': _L1_attn_in['w_proj'], 'L1_attn_b_proj': _L1_attn_in['b_proj'], 'L1_ffn_route_id': _L1_ffn_in['route_id'], 'L1_ffn_Wi': _L1_ffn_in['Wi'], 'L1_ffn_bi': _L1_ffn_in['bi'], 'L1_ffn_Wr': _L1_ffn_in['Wr'], 'L1_ffn_br': _L1_ffn_in['br'], 'L1_ffn_Ws': _L1_ffn_in['Ws'], 'L1_ffn_bs': _L1_ffn_in['bs'], 'L1_ffn_Wo': _L1_ffn_in['Wo'], 'L1_ffn_bo': _L1_ffn_in['bo'], 'L2_attn_W': _L2_attn_in['W'], 'L2_attn_b': _L2_attn_in['b'], 'L2_ffn_router_w': _L2_ffn_in['router_w'], 'L2_ffn_router_b': _L2_ffn_in['router_b'], 'L2_ffn_W1': _L2_ffn_in['W1'], 'L2_ffn_b1': _L2_ffn_in['b1'], 'L2_ffn_W2': _L2_ffn_in['W2'], 'L2_ffn_b2': _L2_ffn_in['b2'], 'L3_attn_ln_gamma': _L3_attn_in['ln_gamma'], 'L3_attn_ln_beta': _L3_attn_in['ln_beta'], 'L3_attn_Wq': _L3_attn_in['Wq'], 'L3_attn_bq': _L3_attn_in['bq'], 'L3_attn_Wk': _L3_attn_in['Wk'], 'L3_attn_bk': _L3_attn_in['bk'], 'L3_attn_Wv': _L3_attn_in['Wv'], 'L3_attn_bv': _L3_attn_in['bv'], 'L3_attn_Wpos': _L3_attn_in['Wpos'], 'L3_attn_u_bias': _L3_attn_in['u_bias'], 'L3_attn_v_bias': _L3_attn_in['v_bias'], 'L3_attn_Wout': _L3_attn_in['Wout'], 'L3_attn_bout': _L3_attn_in['bout'], 'L3_ffn_ln1_w': _L3_ffn_in['ln1_w'], 'L3_ffn_ln2_w': _L3_ffn_in['ln2_w'], 'L3_ffn_wq': _L3_ffn_in['wq'], 'L3_ffn_wk': _L3_ffn_in['wk'], 'L3_ffn_wv': _L3_ffn_in['wv'], 'L3_ffn_wo': _L3_ffn_in['wo'], 'L3_ffn_router_w': _L3_ffn_in['router_w'], 'L3_ffn_w1': _L3_ffn_in['w1'], 'L3_ffn_w2': _L3_ffn_in['w2'], 'L3_ffn_w3': _L3_ffn_in['w3']}

def reference(x, txt, L0_tok_W, L0_tok_b, L0_tok_pos_embed, L0_attn_Wq, L0_attn_bq, L0_attn_Wk, L0_attn_bk, L0_attn_Wv, L0_attn_bv, L0_ffn_Wr, L0_ffn_br, L0_ffn_W1, L0_ffn_b1, L0_ffn_W2, L0_ffn_b2, L0_ffn_gamma, L0_ffn_beta, L1_attn_w_qkv, L1_attn_b_qkv, L1_attn_w_proj, L1_attn_b_proj, L1_ffn_route_id, L1_ffn_Wi, L1_ffn_bi, L1_ffn_Wr, L1_ffn_br, L1_ffn_Ws, L1_ffn_bs, L1_ffn_Wo, L1_ffn_bo, L2_attn_W, L2_attn_b, L2_ffn_router_w, L2_ffn_router_b, L2_ffn_W1, L2_ffn_b1, L2_ffn_W2, L2_ffn_b2, L3_attn_ln_gamma, L3_attn_ln_beta, L3_attn_Wq, L3_attn_bq, L3_attn_Wk, L3_attn_bk, L3_attn_Wv, L3_attn_bv, L3_attn_Wpos, L3_attn_u_bias, L3_attn_v_bias, L3_attn_Wout, L3_attn_bout, L3_ffn_ln1_w, L3_ffn_ln2_w, L3_ffn_wq, L3_ffn_wk, L3_ffn_wv, L3_ffn_wo, L3_ffn_router_w, L3_ffn_w1, L3_ffn_w2, L3_ffn_w3):
    import jax
    import jax.numpy as jnp

    def _L0_tok_ref(x, W, b, pos_embed):
        import jax, jax.numpy as jnp
        import numpy as np
        PATCH = 8
        EMBED = 64
        N_MELS = 128
        N_FRAMES = 512
        BATCH = 64
        NUM_PATCHES = N_MELS // PATCH * (N_FRAMES // PATCH)
        B = x.shape[0]
        mp, fp = (N_MELS // PATCH, N_FRAMES // PATCH)
        xs = x[:, 0]
        patches = xs.reshape(B, mp, PATCH, fp, PATCH).transpose(0, 1, 3, 2, 4).reshape(B, mp * fp, PATCH * PATCH)
        emb = jnp.einsum('bnk,ek->bne', patches, W) + b
        return emb + pos_embed

    def _L0_attn_ref(x, Wq, bq, Wk, bk, Wv, bv):
        import jax, jax.numpy as jnp
        import numpy as np
        B, N, H = (4, 1024, 64)
        q = jnp.einsum('bnh,oh->bno', x, Wq) + bq
        k = jnp.einsum('bnh,oh->bno', x, Wk) + bk
        v = jnp.einsum('bnh,oh->bno', x, Wv) + bv
        scores = jnp.einsum('bik,bjk->bij', q, k)
        attention = jax.nn.softmax(scores, axis=-1)
        attended = jnp.einsum('bij,bjk->bik', attention, v)
        return attended

    def _L0_ffn_ref(x, Wr, br, W1, b1, W2, b2, gamma, beta):
        import math
        import jax, jax.numpy as jnp
        import numpy as np
        CAPACITY_FACTOR = 1.25
        TOP_K = 2
        LN_EPS = 1e-05

        def _layer_norm(x, gamma, beta):
            mu = jnp.mean(x, axis=-1, keepdims=True)
            var = jnp.var(x, axis=-1, keepdims=True)
            return (x - mu) * jax.lax.rsqrt(var + LN_EPS) * gamma + beta
        B, S, D = x.shape
        E = Wr.shape[1]
        N = B * S
        K = TOP_K
        logits = jnp.mean(x, axis=1) @ Wr + br
        routing_weights = jax.nn.softmax(logits, axis=-1)
        capacity = float(math.ceil(N * CAPACITY_FACTOR / E))
        expected_loads = routing_weights.sum(axis=0) * (N / B)
        scale = jnp.where(expected_loads > capacity, capacity / expected_loads, 1.0)
        routing_weights = jax.nn.softmax(routing_weights * scale, axis=-1)
        rw_tok = jnp.broadcast_to(routing_weights[:, None, :], (B, S, E)).reshape(N, E)
        top_w, top_i = jax.lax.top_k(rw_tok, K)
        top_w = jax.nn.softmax(top_w, axis=-1)
        xf = x.reshape(N, D)
        h = jax.nn.gelu(jnp.einsum('nd,edf->enf', xf, W1) + b1[:, None, :], approximate=False)
        y = jnp.einsum('enf,efd->end', h, W2) + b2[:, None, :]
        w_dense = jnp.zeros((N, E), x.dtype).at[jnp.arange(N)[:, None], top_i].add(top_w)
        out = jnp.einsum('ne,end->nd', w_dense, y).reshape(B, S, D)
        out = _layer_norm(out + x, gamma, beta)
        return out

    def _L1_attn_ref(x, w_qkv, b_qkv, w_proj, b_proj):
        import jax, jax.numpy as jnp
        import numpy as np
        DIM = 64
        DIM_HEAD = 32
        NUM_HEADS = DIM // DIM_HEAD
        SCALE = DIM_HEAD ** (-0.5)
        B, L, C = x.shape
        H, D = (NUM_HEADS, DIM_HEAD)
        qkv = x @ w_qkv.T + b_qkv
        qkv = qkv.reshape(B, L, H, 3 * D).transpose(0, 2, 1, 3)
        q, k, v = jnp.split(qkv, 3, axis=-1)
        attn = jnp.einsum('bhld,bhmd->bhlm', q, k) * SCALE
        attn = jax.nn.softmax(attn, axis=-1)
        out = jnp.einsum('bhlm,bhmd->bhld', attn, v)
        out = out.transpose(0, 2, 1, 3).reshape(B, L, C)
        return out @ w_proj.T + b_proj

    def _L1_ffn_ref(x, route_id, Wi, bi, Wr, br, Ws, bs, Wo, bo):
        import jax, jax.numpy as jnp
        import numpy as np
        B, T, IN_DIM = (64, 64, 64)
        HID, OUT_DIM = (128, 64)
        N_LAYERS, N_EXPERTS, N_SHARED = (2, 16, 1)
        flat = x.reshape(-1, x.shape[-1])
        n_tok = flat.shape[0]
        route = jnp.repeat(route_id, n_tok // route_id.shape[0])
        h = jax.nn.relu(flat @ Wi.T + bi)
        n_layers, n_experts = (Wr.shape[0], Wr.shape[1])
        for l in range(n_layers):
            shared = (jnp.einsum('nd,shd->snh', h, Ws[l]) + bs[l][:, None, :]).mean(axis=0)
            routed = jnp.zeros_like(h)
            for e in range(n_experts):
                ye = h @ Wr[l, e].T + br[l, e]
                routed = routed + jnp.where((route == e)[:, None], ye, 0.0)
            h = jax.nn.relu(shared + routed + h)
        out = h @ Wo.T + bo
        return out.reshape(*x.shape[:-1], out.shape[-1])

    def _L2_attn_ref(x, W, b):
        import jax, jax.numpy as jnp
        import numpy as np
        B, N, D, TOP_K = (4, 1024, 64, 64)
        EPS = 1e-12
        value = jnp.einsum('bnd,ed->bne', x, W) + b
        norm = jnp.linalg.norm(x, axis=-1, keepdims=True)
        normed_x = x / jnp.maximum(norm, EPS)
        cos_sim = jnp.einsum('bnd,bmd->bnm', normed_x, normed_x)
        topk_vals, topk_inds = jax.lax.top_k(cos_sim, TOP_K)
        b_idx = jnp.arange(x.shape[0])[:, None, None]
        n_idx = jnp.arange(x.shape[1])[None, :, None]
        attn_sparse = jnp.zeros_like(cos_sim).at[b_idx, n_idx, topk_inds].set(topk_vals)
        attn = jax.nn.softmax(attn_sparse, axis=-1)
        return jnp.einsum('bnm,bmd->bnd', attn, value)

    def _L2_ffn_ref(x, router_w, router_b, W1, b1, W2, b2):
        import jax, jax.numpy as jnp
        import numpy as np
        B, K, D = (128, 16, 64)
        E = 32
        H = int(D * 0.25)
        xf = x.reshape(-1, D)
        logits = xf @ router_w.T + router_b
        idx = jnp.argmax(logits, axis=-1)
        w1t = jnp.take(W1, idx, axis=0)
        h = jnp.einsum('nd,ndh->nh', xf, w1t) + jnp.take(b1, idx, axis=0)
        h = jax.nn.relu(h)
        w2t = jnp.take(W2, idx, axis=0)
        out = jnp.einsum('nh,nhd->nd', h, w2t) + jnp.take(b2, idx, axis=0)
        out = jax.nn.relu(out)
        return out.reshape(x.shape)

    def _L3_attn_ref(inputs, ln_gamma, ln_beta, Wq, bq, Wk, bk, Wv, bv, Wpos, u_bias, v_bias, Wout, bout):
        import jax, jax.numpy as jnp
        import numpy as np
        NUM_HEADS = 4
        LN_EPS = 1e-05

        def positional_encoding(length, d_model):
            pos = jnp.arange(length, dtype=jnp.float32)[:, None]
            div = jnp.exp(jnp.arange(0, d_model, 2, dtype=jnp.float32) * (-np.log(10000.0) / d_model))
            pe = jnp.zeros((length, d_model), dtype=jnp.float32)
            pe = pe.at[:, 0::2].set(jnp.sin(pos * div))
            pe = pe.at[:, 1::2].set(jnp.cos(pos * div))
            return pe

        def rel_shift(pos_score):
            B, H, S, _ = pos_score.shape
            padded = jnp.pad(pos_score, ((0, 0), (0, 0), (0, 0), (1, 0)))
            padded = padded.reshape(B, H, S + 1, S)
            return padded[:, :, 1:].reshape(B, H, S, S)
        B, S, D = inputs.shape
        H = NUM_HEADS
        dh = D // H
        mu = jnp.mean(inputs, axis=-1, keepdims=True)
        var = jnp.mean(jnp.square(inputs - mu), axis=-1, keepdims=True)
        x = (inputs - mu) / jnp.sqrt(var + LN_EPS) * ln_gamma + ln_beta
        pe = positional_encoding(S, D)
        q = (x @ Wq + bq).reshape(B, S, H, dh)
        k = (x @ Wk + bk).reshape(B, S, H, dh)
        v = (x @ Wv + bv).reshape(B, S, H, dh)
        p = (pe @ Wpos).reshape(S, H, dh)
        content_score = jnp.einsum('bshd,bthd->bhst', q + u_bias, k)
        pos_score = jnp.einsum('bshd,thd->bhst', q + v_bias, p)
        pos_score = rel_shift(pos_score)
        score = (content_score + pos_score) / np.sqrt(D).astype(np.float32)
        attn = jax.nn.softmax(score, axis=-1)
        ctx = jnp.einsum('bhst,bthd->bshd', attn, v).reshape(B, S, D)
        return ctx @ Wout + bout

    def _L3_ffn_ref(x, ln1_w, ln2_w, wq, wk, wv, wo, router_w, w1, w2, w3):
        import jax, jax.numpy as jnp
        import numpy as np
        B, T, C = (64, 96, 64)
        NH, NKV = (4, 2)
        HD = C // NH
        NREP = NH // NKV
        NE, TOPK = (8, 2)
        HID = int(8 / 3 * C)
        EPS_RMS = 1e-06

        def _rope_tables(t_len):
            inv_freq = 1.0 / 10000.0 ** (np.arange(0, HD, 2, dtype=np.float32) / HD)
            t = np.arange(t_len, dtype=np.float32)
            freqs = np.outer(t, inv_freq)
            emb = np.concatenate([freqs, freqs], axis=-1)
            return (jnp.asarray(np.cos(emb)), jnp.asarray(np.sin(emb)))

        def _rotate_half(x):
            h = x.shape[-1] // 2
            return jnp.concatenate([-x[..., h:], x[..., :h]], axis=-1)

        def _rmsnorm(v, w):
            return v * jax.lax.rsqrt(jnp.mean(v * v, axis=-1, keepdims=True) + EPS_RMS) * w
        Bx, Tx, Cx = x.shape
        h = _rmsnorm(x, ln1_w)
        q = (h @ wq.T).reshape(Bx, Tx, NH, HD).transpose(0, 2, 1, 3)
        k = (h @ wk.T).reshape(Bx, Tx, NKV, HD).transpose(0, 2, 1, 3)
        v = (h @ wv.T).reshape(Bx, Tx, NKV, HD).transpose(0, 2, 1, 3)
        cos, sin = _rope_tables(Tx)
        cos, sin = (cos[None, None], sin[None, None])
        q = q * cos + _rotate_half(q) * sin
        k = k * cos + _rotate_half(k) * sin
        k = jnp.repeat(k, NREP, axis=1)
        v = jnp.repeat(v, NREP, axis=1)
        scores = jnp.einsum('bhtd,bhsd->bhts', q, k) / jnp.sqrt(jnp.float32(HD))
        causal = jnp.tril(jnp.ones((Tx, Tx), dtype=bool))
        scores = jnp.where(causal[None, None], scores, jnp.float32(-1e+30))
        att = jax.nn.softmax(scores, axis=-1)
        y = jnp.einsum('bhts,bhsd->bhtd', att, v).transpose(0, 2, 1, 3).reshape(Bx, Tx, Cx)
        x = x + y @ wo.T
        flat = _rmsnorm(x, ln2_w).reshape(-1, Cx)
        probs = jax.nn.softmax(flat @ router_w.T, axis=-1)
        tp, ti = jax.lax.top_k(probs, TOPK)
        tp = tp / (jnp.sum(tp, axis=-1, keepdims=True) + 1e-09)
        weights = jnp.sum(tp[..., None] * jax.nn.one_hot(ti, NE, dtype=flat.dtype), axis=1)
        out = jnp.zeros_like(flat)
        for e in range(NE):
            hh = jax.nn.silu(flat @ w1[e].T) * (flat @ w3[e].T)
            out = out + weights[:, e:e + 1] * (hh @ w2[e].T)
        return x + out.reshape(Bx, Tx, Cx)
    h = _L0_tok_ref(x, L0_tok_W, L0_tok_b, L0_tok_pos_embed)
    h = jnp.concatenate([h, txt], axis=1)
    h = h + _L0_attn_ref(_layernorm(h, axis=-1), L0_attn_Wq, L0_attn_bq, L0_attn_Wk, L0_attn_bk, L0_attn_Wv, L0_attn_bv)
    h = h + _L0_ffn_ref(_layernorm(h, axis=-1), L0_ffn_Wr, L0_ffn_br, L0_ffn_W1, L0_ffn_b1, L0_ffn_W2, L0_ffn_b2, L0_ffn_gamma, L0_ffn_beta)
    h = h + _L1_attn_ref(_layernorm(h, axis=-1), L1_attn_w_qkv, L1_attn_b_qkv, L1_attn_w_proj, L1_attn_b_proj)
    h = h + _L1_ffn_ref(_layernorm(h, axis=-1), L1_ffn_route_id, L1_ffn_Wi, L1_ffn_bi, L1_ffn_Wr, L1_ffn_br, L1_ffn_Ws, L1_ffn_bs, L1_ffn_Wo, L1_ffn_bo)
    h = h + _L2_attn_ref(_layernorm(h, axis=-1), L2_attn_W, L2_attn_b)
    h = h + _L2_ffn_ref(_layernorm(h, axis=-1), L2_ffn_router_w, L2_ffn_router_b, L2_ffn_W1, L2_ffn_b1, L2_ffn_W2, L2_ffn_b2)
    h = h + _L3_attn_ref(_layernorm(h, axis=-1), L3_attn_ln_gamma, L3_attn_ln_beta, L3_attn_Wq, L3_attn_bq, L3_attn_Wk, L3_attn_bk, L3_attn_Wv, L3_attn_bv, L3_attn_Wpos, L3_attn_u_bias, L3_attn_v_bias, L3_attn_Wout, L3_attn_bout)
    h = h + _L3_ffn_ref(_layernorm(h, axis=-1), L3_ffn_ln1_w, L3_ffn_ln2_w, L3_ffn_wq, L3_ffn_wk, L3_ffn_wv, L3_ffn_wo, L3_ffn_router_w, L3_ffn_w1, L3_ffn_w2, L3_ffn_w3)
    return h

_drawn_inputs = setup_inputs


def setup_inputs(seed=0):
    import zlib

    import numpy as np

    out = dict(_drawn_inputs(seed))
    spreads = {'L0_ffn_br': (0.0, 0.1),
     'L0_ffn_b1': (0.0, 0.323),
     'L0_ffn_b2': (0.0, 0.1),
     'L0_ffn_gamma': (1.0, 0.2),
     'L0_ffn_beta': (0.0, 0.1),
     'L1_ffn_bi': (0.0, 0.734),
     'L1_ffn_bo': (0.0, 0.1),
     'L3_attn_ln_gamma': (1.0, 0.6),
     'L3_attn_ln_beta': (0.0, 0.8),
     'L3_attn_bq': (0.0, 0.8),
     'L3_attn_bk': (0.0, 2.0),
     'L3_attn_bv': (0.0, 0.8),
     'L3_attn_bout': (0.0, 0.1),
     'L3_ffn_ln1_w': (1.0, 0.6),
     'L3_ffn_ln2_w': (1.0, 0.6)}
    factors = {'L0_tok_b': 4.514,
     'L0_tok_pos_embed': 2.807,
     'L0_attn_bk': 64.0,
     'L0_ffn_Wr': 8.0,
     'L1_attn_b_qkv': 3.984,
     'L1_attn_b_proj': 4.392,
     'L1_ffn_Wi': 4.421,
     'L1_ffn_Wr': 8.0,
     'L1_ffn_br': 8.0,
     'L1_ffn_Ws': 8.0,
     'L1_ffn_bs': 8.0,
     'L1_ffn_Wo': 2.787,
     'L2_ffn_b1': 6.146,
     'L3_attn_Wq': 8.0,
     'L3_attn_Wk': 8.0,
     'L3_attn_Wv': 8.0,
     'L3_attn_Wpos': 8.0,
     'L3_attn_u_bias': 8.0,
     'L3_attn_v_bias': 23.991,
     'L3_attn_Wout': 8.0,
     'L3_ffn_wq': 8.0,
     'L3_ffn_wk': 8.0,
     'L3_ffn_wv': 8.0,
     'L3_ffn_wo': 8.0,
     'L3_ffn_router_w': 8.0,
     'L3_ffn_w1': 8.0,
     'L3_ffn_w2': 8.0,
     'L3_ffn_w3': 8.0}
    for name, (base, spread) in spreads.items():
        noise = np.random.default_rng([zlib.crc32(name.encode()), seed]).standard_normal(out[name].shape)
        drawn = base * np.exp(spread * noise) if base else spread * noise
        out[name] = jnp.asarray(drawn.astype(out[name].dtype))
    for name, factor in factors.items():
        out[name] = (out[name] * factor).astype(out[name].dtype)
    return out
```

```python
import concourse.bass as bass
from concourse import mybir
from contextlib import ExitStack
import numpy as np

F32 = mybir.dt.float32
I32 = mybir.dt.int32
ALU = mybir.AluOpType
ACT = mybir.ActivationFunctionType
AX = mybir.AxisListType

B, D, P = 4, 64, 128
NP_, NT = 1024, 512
S = NP_ + NT
T = S // P
TP = NP_ // P
NB = S // 512
E0, F0 = 8, 128
E1, HID1, GRP = 16, 128, 96
NG = S // GRP
GPB = 4
E2, H2 = 32, 16
C2 = E2 * H2 // P
HEADS, DH = 4, 16
E3, HC3 = 8, 85
TOPK = 64
BIG = float(2.0 ** 100)
NEG = -4e30
LN_EPS, RMS_EPS = 1e-5, 1e-6
CAP0 = float(-(-(B * S * 5 // 4) // E0))

ENGINES = 4

SIGNALS = {
    "embed": {"rstd_ready": 1, "xt_copied": 3, "emb_psum": 1, "xt_psum": 3, "q_psum": 3, "k_psum": 3, "v_psum": 2,
        "vec_step": 7, "var_ready": 1, "normed": 1},
    "attn0": {"probs_ready": 12, "pt_by_act": 24, "scores_ready": 12, "pt_psum": 36, "ctx_ready": 12,
        "max_ready": 12, "pt_by_vec": 12, "vec_step": 12, "ctx_copied": 12},
    "mean0": {"rstd_ready": 1, "mean_psum": 1, "logit_psum": 1, "vec_step": 6, "var_ready": 1, "normed": 1,
        "mean_ready": 1},
    "route0": {"exp_out": 3, "vec_step": 33, "exp_in": 3},
    "moe0": {"rstd_ready": 2, "xt_copied": 3, "hid_ready": 6, "xt_psum": 3, "hid_psum": 6, "out_psum": 2,
        "vec_step": 31, "var_ready": 2, "normed": 1, "weights_ready": 1},
    "qkv1": {"rstd_ready": 1, "xt_copied": 3, "xt_psum": 3, "q_psum": 3, "k_psum": 3, "v_psum": 2, "vec_step": 6,
        "var_ready": 1, "normed": 1},
    "attn1": {"probs_ready": 24, "pt_by_act": 48, "scores_ready": 24, "pt_psum": 72, "ctx_ready": 24,
        "max_ready": 24, "pt_by_vec": 24, "vec_step": 24, "ctx_copied": 24},
    "moe1": {"rstd_ready": 1, "xt_copied": 6, "hid_ready": 3, "expert_ready": 8, "xt_psum": 6, "proj_psum": 2,
        "hid_psum": 3, "expert_psum": 8, "out_psum": 2, "bias_ready": 1, "vec_step": 9, "var_ready": 1, "normed": 1},
    "sim2": {"rstd_ready": 2, "xt_copied": 6, "xt_psum": 6, "v_psum": 2, "vec_step": 10, "var_ready": 2, "normed": 2},
    "attn2": {"probs_ready": 12, "pt_by_act": 24, "scores_ready": 12, "pt_psum": 36, "ctx_ready": 12,
        "vec_step": 204, "sparse_ready": 12, "pt_by_vec": 12, "ctx_copied": 12},
    "moe2": {"rstd_ready": 1, "xt_copied": 6, "hid_ready": 12, "xt_psum": 6, "logit_psum": 1, "hid_psum": 12,
        "out_psum": 2, "vec_step": 12, "var_ready": 1, "normed": 2},
    "rel3a": {"rstd_ready": 2, "pool_step": 13, "rot_used": 6, "xt_copied": 3, "qv_ready": 6, "content_ready": 6,
        "k_copied": 6, "xt_psum": 3, "v_psum": 2, "q_psum": 6, "k_psum": 6, "rot_psum": 6, "vec_step": 15,
        "bias_ready": 1, "var_ready": 2, "normed": 1, "v_copied": 1, "rot_ready": 6},
    "attn3a": {"probs_ready": 24, "pt_by_act": 48, "scores_ready": 24, "side_ready": 24, "pt_psum": 72,
        "ctx_ready": 24, "vec_step": 48, "side_read": 24, "max_ready": 24, "pt_by_vec": 24, "ctx_copied": 24},
    "rel3b": {"pool_step": 12, "rot_used": 6, "qv_ready": 6, "content_ready": 6, "k_copied": 6, "q_psum": 6,
        "k_psum": 6, "rot_psum": 6, "rot_ready": 6},
    "attn3b": {"probs_ready": 24, "pt_by_act": 48, "scores_ready": 24, "side_ready": 24, "pt_psum": 72,
        "ctx_ready": 24, "vec_step": 48, "side_read": 24, "max_ready": 24, "pt_by_vec": 24, "ctx_copied": 24},
    "rope4": {"rstd_ready": 2, "rope_used": 6, "xt_copied": 6, "xt_psum": 6, "proj_psum": 2, "v_psum": 1,
        "rope_psum": 6, "vec_step": 12, "var_ready": 2, "normed": 1, "rope_ready": 6},
    "attn4": {"probs_ready": 48, "pt_by_act": 48, "scores_ready": 48, "pt_psum": 96, "ctx_ready": 48,
        "vec_step": 144, "max_ready": 48, "pt_by_vec": 48, "ctx_copied": 48},
    "moe4": {"rstd_ready": 1, "xt_copied": 6, "exp_out": 1, "silu_ready": 48, "xt_psum": 6, "proj_psum": 2,
        "logit_psum": 1, "gate_psum": 48, "up_psum": 48, "down_psum": 24, "proj_read": 1, "vec_step": 50,
        "var_ready": 1, "normed": 1, "exp_in": 1, "gated": 48, "mixed": 12},
}


def const_layout():
    return [
        ("ident", P, P), ("mask_low", P, P), ("mask_line", P, P + 1), ("mask_future", P, P), ("neg", P, P),
        ("mean", P, P), ("half", P, 2 * T), ("iota8", P, 8), ("iota32", P, 32),
        ("tok_w", 65, D), ("pos", P, TP * D),
        ("q0", 65, D), ("k0", 65, D), ("v0", 65, D),
        ("wr0", 65, E0), ("w1_0", 65, E0 * F0), ("w2_0", P, E0 * D), ("b2_0", P, E0 * D), ("gamma0", P, D), ("beta0", P, D),
        ("q1", 65, D), ("k1", 65, D), ("v1", 65, D), ("proj1", 65, D),
        ("wi1", 65, HID1), ("ws1", P, 2 * HID1), ("bs1", P, 2), ("wo1", P, D), ("bo1", P, D),
        ("w2a", 65, D), ("rw2", 65, E2), ("w1_2", P, C2 * P), ("w2_2", P, C2 * D), ("b2_2", P, D),
        ("gamma3", P, D), ("beta3", P, D), ("wq3", 64, HEADS * 80), ("bq3", 80, HEADS), ("uv3", 80, HEADS),
        ("wk3", 65, HEADS * DH), ("v3", 65, D), ("wpos3", DH, HEADS * 2 * D), ("wout3", 65, D),
        ("rot_c", 64, S), ("rot_s", 64, S),
        ("rms1", P, D), ("rms2", P, D), ("wq4", 64, 2 * P), ("wk4", 64, 2 * P), ("wv4", 64, 32), ("wo4", 64, D),
        ("rope_c", P, S), ("rope_s", P, S),
        ("rt4", 64, E3), ("w1_4", 64, E3 * 2 * HC3), ("w3_4", 64, E3 * 2 * HC3), ("w2_4", HC3, E3 * 2 * D),
    ]


CONST_AT = {}
_at = 0
for _name, _rows, _cols in const_layout():
    CONST_AT[_name] = (_rows, _at, _cols)
    _at += _cols
CONST_COLS = _at


class Ledger:

    def __init__(self, nc, ctx):
        self.nc, self.seen = nc, {}
        names = ["phase_left", "res_free"] + sorted({n for p in SIGNALS.values() for n in p})
        self.sems = {n: ctx.enter_context(nc.semaphore(n)) for n in names}
        self.pass_ended, self.pass_opened, self.turn = (ctx.enter_context(nc.semaphore(n))
                                                        for n in ("pass_ended", "pass_opened", "turn"))

    def phases(self, phase):
        return [p for p in PLAN if phase in p][0]

    def before(self, phase, name):
        phases = self.phases(phase)
        return sum(SIGNALS[p].get(name, 0) for p in phases[:phases.index(phase)])

    def ended(self, phase):
        return (self.phases(phase).index(phase) + 1) * ENGINES

    def end_pass(self, eng, passes):
        eng.drain().then_inc(self.pass_ended, 1)
        if eng is self.nc.gpsimd:
            eng.wait_ge(self.pass_ended, passes * (ENGINES + 1))
            eng.sem_inc(self.turn, 1)
            nums = sorted(s.num for s in self.sems.values())
            assert nums == list(range(nums[0], nums[0] + len(nums)))
            eng.sem_clear(range(nums[0], nums[0] + len(nums)))
            eng.drain().then_inc(self.pass_opened, 1)
        else:
            eng.wait_ge(self.pass_opened, passes)
            eng.sem_inc(self.turn, 1)


class Phase:

    def __init__(self, ledger, name):
        self.led, self.name, self.mine = ledger, name, {}

    def mark(self, name):
        self.mine[name] = self.mine.get(name, 0) + 1
        seen = self.led.seen.setdefault(self.name, {})
        seen[name] = seen.get(name, 0) + 1
        return self.led.sems[name], 1

    def after(self, name, k):
        return self.led.sems[name], self.led.before(self.name, name) + k

    def own(self, name):
        return self.after(name, self.mine[name])

    def leave(self, eng):
        eng.drain().then_inc(self.led.sems["phase_left"], 1)
        eng.wait_ge(self.led.sems["phase_left"], self.led.ended(self.name))


PLAN = [
    ["embed", "attn0", "mean0"],
    ["route0"],
    ["moe0", "qkv1", "attn1", "moe1", "sim2", "attn2", "moe2", "rel3a", "attn3a", "rel3b", "attn3b",
     "rope4", "attn4", "moe4"],
]


def units_of(kind):
    heads = {"attn0": [0], "attn1": [0, 1], "attn2": [0], "attn3a": [0, 1], "attn3b": [2, 3], "attn4": [0, 1, 2, 3]}[kind]
    return [(h, q) for h in heads for q in range(T)]


def build(nc, consts, patches, txt, route, w_route, pe_low, pe_up, out):
    with ExitStack() as ctx:
        def sb(name, shape, dt=F32):
            return ctx.enter_context(nc.sbuf_tensor(name, shape, dt))

        cst = sb("cst", [P, CONST_COLS])
        h = sb("h", [P, T, D])
        x = sb("x", [P, T, D])
        y = sb("y", [P, T, D])
        sq = sb("sq", [P, T, D])
        ctxt = sb("ctxt", [P, T, D])
        res = sb("res", [P, T, D])
        v = sb("v", [P, T, D])
        hall = sb("hall", [P, B, T * D])
        xt = sb("xt", [65, S])
        qlo = sb("qlo", [P, 2, S])
        qup = sb("qup", [P, 2, S])
        klo = sb("klo", [80, 2, S])
        kup = sb("kup", [80, 2, S])
        big = sb("big", [P, 4 * S])
        rw = sb("rw", [P, 2, NG, HID1 + 1])
        st = sb("st", [P, 16, T])
        negmax = sb("negmax", [P, 48])
        rowsum = sb("rowsum", [P, 48])
        rinv = sb("rinv", [P, 48])
        top8 = sb("top8", [P, 8 * T, 8])
        lg0 = sb("lg0", [P, B, E0])
        r0 = sb("r0", [P, 8, B, E0])
        r0s = sb("r0s", [P, 8, B])
        oh0 = sb("oh0", [P, B, 2 * E0])
        wt0 = sb("wt0", [P, B, 2 * E0])
        ohb = sb("ohb", [P, 2 * E0])
        wtb = sb("wtb", [P, 2 * E0])
        mean_t = sb("mean_t", [65, P])
        w1s = sb("w1s", [65, 2, F0])
        w2s = sb("w2s", [P, 2, D])
        b2s = sb("b2s", [P, 2, D])
        wsi = sb("wsi", [P, 2, HID1])
        bias1 = sb("bias1", [P, 2, NG])
        bias3 = sb("bias3", [80, HEADS])
        lg = sb("lg", [P, 5, T * E3])
        wt4 = sb("wt4", [P, T, E3])
        route_sb = sb("route_sb", [1, B * NG], I32)
        ps = ctx.enter_context(nc.psum_tensor("ps", [P, 8, 512], F32))

        xp = qup[0:65, 0, 0:NP_]
        txt_in = qup[:, 1, 0:(T - TP) * D].rearrange("p (t d) -> p t d", d=D)
        prob = big[:, 0:2 * S].rearrange("p (s n) -> p s n", s=2)
        pt = big[:, 2 * S:4 * S].rearrange("p (s g n) -> p s g n", s=2, g=NB)
        hid = big[:, :].rearrange("p (c n) -> p c n", c=4)
        xt2 = qup[:, 0, :]
        xa = big[:, 0:S].rearrange("p (t n) -> p t n", n=P)
        work = qup[:, 0, :]
        sparse = qup[:, 1, :]
        qt = qlo[:, 0, :]
        kt = qlo[:, 1, :]
        qv = big[0:DH, 0:2 * 512].rearrange("p (s n) -> p s n", s=2)
        rt1 = big[0:D, 1024:2048].rearrange("p (s n) -> p s n", s=2)
        rt2 = big[0:D, 2048:3072].rearrange("p (s n) -> p s n", s=2)
        rp1 = big[:, 0:S]
        rp2 = big[:, S:2 * S]
        sg = big[0:HC3, 0:1024].rearrange("p (s n) -> p s n", s=2)
        hh = big[0:HC3, 1024:1024 + 2048].rearrange("p (s c n) -> p s c n", s=2, c=2)
        moe_w = big[:, 4096:4096 + 512]

        def K(name):
            rows, at, cols = CONST_AT[name]
            return cst[0:rows, at:at + cols]

        ident = K("ident")
        led = Ledger(nc, ctx)

        def dsem(name):
            return ctx.enter_context(nc.semaphore(name))

        consts_in = dsem("consts_in")
        patches_in = dsem("patches_in")
        route_in = dsem("route_in")
        weights_in = dsem("weights_in")
        stored = dsem("stored")
        CONST_DMAS = 16 * 6


        def chain(ph, eng):
            def link(ins):
                ins.then_inc(*ph.mark("vec_step"))
                eng.wait_ge(*ph.own("vec_step"))
            return link

        def pool_chain(ph, pool):
            def link(ins):
                ins.then_inc(*ph.mark("pool_step"))
                pool.wait_ge(*ph.own("pool_step"))
            return link

        def bc(ap, shape):
            return ap.unsqueeze(2).to_broadcast(shape)

        def per_token(ap):
            return ap.unsqueeze(1).to_broadcast([P, T, D])

        def norm_vec(ph, dve, src, dst, n, centre=True, eps=LN_EPS, tail=None):
            link = chain(ph, dve)
            xc = src
            if centre:
                link(nc.vector.tensor_reduce(st[:, 0, :], src, AX.X, ALU.add))
                link(nc.vector.tensor_scalar(st[:, 1, :], st[:, 0, :], -1.0 / D, None, ALU.mult))
                link(nc.vector.tensor_tensor(dst, src, bc(st[:, 1, :], [P, T, D]), ALU.add))
                xc = dst
            link(nc.vector.tensor_tensor(sq[:, :, :], xc, xc, ALU.mult))
            link(nc.vector.tensor_reduce(st[:, 2, :], sq[:, :, :], AX.X, ALU.add))
            nc.vector.tensor_scalar(st[:, 3, :], st[:, 2, :], 1.0 / D, eps, ALU.mult, ALU.add)\
                .then_inc(*ph.mark("var_ready"))
            dve.wait_ge(*ph.after("rstd_ready", n))
            link(nc.vector.tensor_tensor(dst, xc, bc(st[:, 4, :], [P, T, D]), ALU.mult))

        def norm_pool(ph, pool, n, power=-0.5):
            pool.wait_ge(*ph.after("var_ready", n))
            e = K("half")[:, 0:T] if power < 0 else K("half")[:, T:2 * T]
            nc.gpsimd.tensor_tensor(st[:, 4, :], st[:, 3, :], e, ALU.pow).then_inc(*ph.mark("rstd_ready"))
            pool.wait_ge(*ph.own("rstd_ready"))

        def ready_vec(ph, dve, name="normed"):
            nc.vector.tensor_copy(st[:, 15, 0:1], st[:, 4, 0:1]).then_inc(*ph.mark(name))

        def transpose_pe(ph, src, banks, width=D):
            for t in range(T):
                ins = nc.tensor.transpose(ps[0:width, banks[t // 4], (t % 4) * P:(t % 4 + 1) * P], src[:, t, :], ident)
                if t % 4 == 3:
                    ins.then_inc(*ph.mark("xt_psum"))

        def transpose_act(ph, act, dst, banks, n0=0, width=D):
            for j in range(NB):
                act.wait_ge(*ph.after("xt_psum", n0 + j + 1))
                nc.scalar.copy(dst[0:width, 512 * j:512 * (j + 1)], ps[0:width, banks[j], :]).then_inc(*ph.mark("xt_copied"))

        def rows_pe(ph, w, src, banks, name, n=D, rows=65):
            for t in range(T):
                ins = nc.tensor.matmul(ps[:, banks[t // 6], (t % 6) * n:(t % 6 + 1) * n], src[0:rows, t * P:(t + 1) * P], w,
                                       start=True, stop=True)
                if t % 6 == 5:
                    ins.then_inc(*ph.mark(name))

        def rows_bank(banks, i, n=D):
            return ps[:, banks[i], 0:6 * n].rearrange("p (t d) -> p t d", d=n)

        def qkv_pe(ph, pe, wq, wk, wv):
            pe.wait_ge(*ph.after("normed", 1))
            transpose_pe(ph, x, [0, 1, 2])
            for j in range(NB):
                pe.wait_ge(*ph.after("xt_copied", j + 1))
                nc.tensor.matmul(ps[0:D, 3 + j, :], K(wq), xt[:, 512 * j:512 * (j + 1)], start=True, stop=True)\
                    .then_inc(*ph.mark("q_psum"))
            for j in range(NB):
                nc.tensor.matmul(ps[0:D, (6 + j) % 8, :], K(wk), xt[:, 512 * j:512 * (j + 1)], start=True, stop=True)\
                    .then_inc(*ph.mark("k_psum"))
            rows_pe(ph, K(wv), xt, [1, 2], "v_psum")

        def qkv_act(ph, act):
            transpose_act(ph, act, xt, [0, 1, 2])
            for j in range(NB):
                act.wait_ge(*ph.after("k_psum", j + 1))
                nc.scalar.copy(kt[0:D, 512 * j:512 * (j + 1)], ps[0:D, (6 + j) % 8, :])

        def qkv_vec(ph, dve, scale):
            for j in range(NB):
                dve.wait_ge(*ph.after("q_psum", j + 1))
                nc.vector.tensor_scalar(qt[0:D, 512 * j:512 * (j + 1)], ps[0:D, 3 + j, :], scale, None, ALU.mult)
            for i in range(2):
                dve.wait_ge(*ph.after("v_psum", i + 1))
                nc.vector.tensor_copy(v[:, 6 * i:6 * i + 6, :], rows_bank([1, 2], i))


        def tiles(kind, q):
            return q + 1 if kind == "attn4" else T

        def groups(kind, q):
            return -(-tiles(kind, q) // 4)

        def before_groups(kind, u):
            return sum(groups(kind, q) for _, q in units_of(kind)[:u])

        def vec_groups(kind, u):
            return u

        def act_groups(kind, u):
            return before_groups(kind, u) - u

        def width(kind):
            return {"attn0": D, "attn1": 32, "attn2": D}.get(kind, DH)

        def v_of(kind, hd, t):
            if kind in ("attn0", "attn2"):
                return v[:, t, :]
            if kind == "attn1":
                return v[:, t, 32 * hd:32 * hd + 32]
            if kind == "attn4":
                return v[:, t, DH * (hd // 2):DH * (hd // 2) + DH]
            return v[:, t, DH * hd:DH * hd + DH]

        def attn_pe(ph, pe, kind):
            units = units_of(kind)

            def scores(u, j):
                hd, q = units[u]
                if u >= len(units) or 4 * j >= tiles(kind, q):
                    return
                if j == 0 and u >= 2:
                    pe.wait_ge(*ph.after("probs_ready", u - 1))
                bank = ps[:, 3 * (u % 2) + j, :]
                lo, hi = 4 * j, min(4 * j + 4, tiles(kind, q))
                qs = slice(q * P, (q + 1) * P)
                if kind.startswith("attn3"):
                    s = hd % 2
                    cut = min(max(q, lo), hi)
                    parts = [(lo, cut, qlo, klo), (cut, hi, qup, kup)]
                    parts = [(a, b, qq, kk) for a, b, qq, kk in parts if a < b]
                    for a, b, qq, kk in parts:
                        ins = nc.tensor.matmul(bank[:, (a - lo) * P:(b - lo) * P], qq[0:80, s, qs], kk[:, s, a * P:b * P],
                                               start=True, stop=True)
                else:
                    r = {"attn1": 32, "attn4": 32}.get(kind, D)
                    base = r * hd if r == 32 else 0
                    ins = nc.tensor.matmul(bank[:, 0:(hi - lo) * P], qt[base:base + r, qs], kt[base:base + r, lo * P:hi * P],
                                           start=True, stop=True)
                if hi == tiles(kind, q):
                    ins.then_inc(*ph.mark("scores_ready"))

            def side(u):
                hd, q = units[u]
                s = hd % 2
                if u >= 2:
                    pe.wait_ge(*ph.after("ctx_copied", u - 1))
                qs = slice(q * P, (q + 1) * P)
                n = min(P + 1, S - q * P)
                nc.tensor.matmul(ps[:, 7, 0:P], qlo[0:80, s, qs], klo[:, s, qs], start=True, stop=True)
                nc.tensor.matmul(ps[:, 7, P:P + n], qlo[64:80, s, qs], klo[64:80, s, q * P:q * P + n], start=True, stop=True)\
                    .then_inc(*ph.mark("side_ready"))

            def turn(u, g):
                if g == 0:
                    pe.wait_ge(*ph.after("probs_ready", u + 1))
                if g == 0 and u > 0:
                    if groups(kind, units[u - 1][1]) > 1:
                        pe.wait_ge(*ph.after("pt_by_act", act_groups(kind, u)))
                    else:
                        pe.wait_ge(*ph.after("pt_by_vec", vec_groups(kind, u)))
                if g == 1:
                    pe.wait_ge(*ph.after("pt_by_vec", vec_groups(kind, u) + 1))
                if g == 2:
                    pe.wait_ge(*ph.after("pt_by_act", act_groups(kind, u) + 1))
                n = min(4, tiles(kind, units[u][1]) - 4 * g)
                for i in range(n):
                    ins = nc.tensor.transpose(ps[:, 6, i * P:(i + 1) * P], prob[:, u % 2, (4 * g + i) * P:(4 * g + i + 1) * P],
                                              ident)
                ins.then_inc(*ph.mark("pt_psum"))

            def context(u, g):
                hd, q = units[u]
                if g == 0:
                    pe.wait_ge(*ph.after("pt_by_vec", vec_groups(kind, u) + 1))
                    if u > 0:
                        pe.wait_ge(*ph.after("ctx_copied", u))
                    if kind.startswith("attn3") and u + 1 < len(units):
                        pe.wait_ge(*ph.after("side_read", u + 2))
                else:
                    pe.wait_ge(*ph.after("pt_by_act", act_groups(kind, u) + g))
                n = tiles(kind, q)
                for i in range(4 * g, min(4 * g + 4, n)):
                    ins = nc.tensor.matmul(ps[:, 7, 448:448 + width(kind)], pt[:, u % 2, g, (i % 4) * P:(i % 4 + 1) * P],
                                           v_of(kind, hd, i), start=(i == 0), stop=(i == n - 1))
                if g == groups(kind, q) - 1:
                    ins.then_inc(*ph.mark("ctx_ready"))

            for u in (0, 1):
                for j in range(NB):
                    scores(u, j)
            if kind.startswith("attn3"):
                side(0)
            for u in range(len(units)):
                more = groups(kind, units[u][1])
                ahead = u + 2 < len(units)
                turn(u, 0)
                if kind.startswith("attn3") and u + 1 < len(units):
                    if u == 0:
                        pe.wait_ge(*ph.after("side_read", 1))
                    else:
                        pe.wait_ge(*ph.after("ctx_copied", u))
                    side(u + 1)
                if ahead:
                    scores(u + 2, 0)
                if more > 1:
                    turn(u, 1)
                context(u, 0)
                if ahead:
                    scores(u + 2, 1)
                if more > 2:
                    turn(u, 2)
                if more > 1:
                    context(u, 1)
                if ahead:
                    scores(u + 2, 2)
                if more > 2:
                    context(u, 2)

        def attn_act(ph, act, kind):
            units = units_of(kind)

            def exps(u):
                q = units[u][1]
                n = tiles(kind, q) * P
                if kind == "attn2":
                    act.wait_ge(*ph.after("sparse_ready", u + 1))
                    src, bias = sparse, 0.0
                else:
                    act.wait_ge(*ph.after("max_ready", u + 1))
                    src = ps[:, 3 * (u % 2):3 * (u % 2) + NB, :].rearrange("p b n -> p (b n)")[:, 0:n]
                    bias = negmax[:, u:u + 1]
                if u >= 2:
                    act.wait_ge(*ph.after("pt_psum", before_groups(kind, u - 1)))
                scale = 0.25 if kind == "attn4" else 1.0
                nc.scalar.activation(prob[:, u % 2, 0:n], src, ACT.Exp, bias=bias, scale=scale,
                                     accum_out=rowsum[:, u:u + 1]).then_inc(*ph.mark("probs_ready"))

            exps(0)
            for u in range(len(units)):
                for g in range(1, groups(kind, units[u][1])):
                    n = min(4, tiles(kind, units[u][1]) - 4 * g) * P
                    act.wait_ge(*ph.after("pt_psum", before_groups(kind, u) + g + 1))
                    if u >= 2:
                        act.wait_ge(*ph.after("ctx_ready", u - 1))
                    nc.scalar.copy(pt[:, u % 2, g, 0:n], ps[:, 6, 0:n]).then_inc(*ph.mark("pt_by_act"))
                if u + 1 < len(units):
                    exps(u + 1)

        def attn_vec(ph, dve, kind, dest):
            units = units_of(kind)
            link = chain(ph, dve)

            def maxima(u):
                hd, q = units[u]
                n = tiles(kind, q) * P
                flat = ps[:, 3 * (u % 2):3 * (u % 2) + NB, :].rearrange("p b n -> p (b n)")
                dve.wait_ge(*ph.after("scores_ready", u + 1))
                if kind.startswith("attn3"):
                    dve.wait_ge(*ph.after("side_ready", u + 1))
                    m = min(P + 1, S - q * P)
                    link(nc.vector.copy_predicated(flat[:, q * P:(q + 1) * P], K("mask_low").bitcast(I32), ps[:, 7, 0:P]))
                    ins = nc.vector.copy_predicated(flat[:, q * P:q * P + m], K("mask_line")[:, 0:m].bitcast(I32),
                                                    ps[:, 7, P:P + m])
                    ins.then_inc(*ph.mark("side_read"))
                    dve.wait_ge(*ph.own("side_read"))
                if kind == "attn4":
                    link(nc.vector.copy_predicated(flat[:, q * P:(q + 1) * P], K("mask_future").bitcast(I32), K("neg")))
                if kind == "attn2":
                    if u >= 1:
                        dve.wait_ge(*ph.after("probs_ready", u))
                    src = flat[:, 0:S]
                    for r in range(TOPK // 8):
                        link(nc.vector.max(top8[:, 8 * q + r, :], src))
                        link(nc.vector.match_replace(work, top8[:, 8 * q + r, :], src, -4.0))
                        src = work
                    nc.vector.scalar_tensor_tensor(sparse, work, -3.0, flat[:, 0:S], ALU.is_lt, ALU.mult)\
                        .then_inc(*ph.mark("sparse_ready"))
                    return
                if kind == "attn4":
                    link(nc.vector.tensor_reduce(st[:, 14, u % T:u % T + 1], flat[:, 0:n], AX.X, ALU.max, negate=True))
                    nc.vector.tensor_scalar(negmax[:, u:u + 1], st[:, 14, u % T:u % T + 1], 0.25, None, ALU.mult)\
                        .then_inc(*ph.mark("max_ready"))
                else:
                    nc.vector.tensor_reduce(negmax[:, u:u + 1], flat[:, 0:n], AX.X, ALU.max, negate=True)\
                        .then_inc(*ph.mark("max_ready"))

            maxima(0)
            for u in range(len(units)):
                hd, q = units[u]
                n = min(4, tiles(kind, q)) * P
                dve.wait_ge(*ph.after("pt_psum", before_groups(kind, u) + 1))
                if u >= 2:
                    dve.wait_ge(*ph.after("ctx_ready", u - 1))
                nc.vector.tensor_copy(pt[:, u % 2, 0, 0:n], ps[:, 6, 0:n]).then_inc(*ph.mark("pt_by_vec"))
                link(nc.vector.reciprocal(rinv[:, u:u + 1], rowsum[:, u:u + 1]))
                if u + 1 < len(units) and kind != "attn2":
                    maxima(u + 1)
                dve.wait_ge(*ph.after("ctx_ready", u + 1))
                dest(u, hd, q, ps[:, 7, 448:448 + width(kind)], rinv[:, u:u + 1]).then_inc(*ph.mark("ctx_copied"))
                if u + 1 < len(units) and kind == "attn2":
                    maxima(u + 1)

        def add_to_h(u, hd, q, o, r):
            return nc.vector.scalar_tensor_tensor(h[:, q, :], o, r, h[:, q, :], ALU.mult, ALU.add)

        def to_ctxt(w):
            def put(u, hd, q, o, r):
                return nc.vector.tensor_scalar(ctxt[:, q, w * hd:w * hd + w], o, r, None, ALU.mult)
            return put

        def top2_onehots(link, src, oh1, oh2, tmp, m, iota, shape):
            for oh, s in ((oh1, src), (oh2, tmp)):
                link(nc.vector.tensor_reduce(m, s, AX.X, ALU.max))
                link(nc.vector.tensor_tensor(oh, s, bc(m, shape), ALU.is_equal))
                link(nc.vector.tensor_tensor(oh, oh, iota, ALU.mult))
                link(nc.vector.tensor_reduce(m, oh, AX.X, ALU.max))
                link(nc.vector.tensor_tensor(oh, oh, bc(m, shape), ALU.is_equal))
                if oh is oh1 and oh2 is not None:
                    link(nc.vector.scalar_tensor_tensor(tmp, oh, -BIG, src, ALU.mult, ALU.add))
                if oh2 is None:
                    return

        block = ctx.enter_context(nc.Block())

        @block.sync
        def _(sp):
            half = CONST_COLS // 2
            sp.dma_start(cst[:, 0:half], consts[:, 0:half]).then_inc(consts_in, 16)
            sp.dma_start(cst[:, half:CONST_COLS], consts[:, half:CONST_COLS]).then_inc(consts_in, 16)
            sp.dma_start(route_sb[:, :], route).then_inc(route_in, 16)
            for s in range(2):
                sp.dma_start(klo[0:D, s, :], pe_low).then_inc(consts_in, 16)
            sp.dma_start(kup[0:D, 0, :], pe_up).then_inc(consts_in, 16)
            sp.dma_start(kup[0:D, 1, :], pe_up).then_inc(consts_in, 16)

            def load_tokens(b):
                sp.dma_start(xp, patches[bass.ds(b, 1), :, :].rearrange("a p n -> (a p) n")).then_inc(patches_in, 16)
                sp.dma_start(txt_in, txt[bass.ds(b, 1), :, :].rearrange("a (t p) d -> (a p) t d", p=P)).then_inc(patches_in, 16)

            def load_experts(b):
                for g in range(NG):
                    e = sp.value_load(route_sb[0:1, bass.ds(b * NG + g, 1)], min_val=0, max_val=E1 - 1)
                    for layer in range(2):
                        sp.dma_start(rw[:, layer, g, :], w_route[layer, bass.ds(e, 1), :, :].rearrange("a p n -> (a p) n"))\
                            .then_inc(weights_in, 16)

            load_tokens(0)
            with sp.Fori(0, B - 1) as b:
                sp.wait_ge(led.sems["phase_left"], led.ended("embed"))
                load_tokens(b + 1)
                sp.wait_ge(led.sems["phase_left"], led.ended("mean0"))
                led.end_pass(sp, b + 1)
            sp.wait_ge(led.sems["phase_left"], led.ended("mean0"))
            led.end_pass(sp, B)
            sp.wait_ge(route_in, 16)
            load_experts(0)
            sp.wait_ge(led.sems["phase_left"], led.ended("route0"))
            led.end_pass(sp, B + 1)

            sp.sem_inc(led.sems["res_free"], 1)

            def store_row(b):
                sp.wait_ge(led.sems["phase_left"], led.ended("moe4"))
                sp.dma_start(out[bass.ds(b, 1), :, :].rearrange("a (t p) d -> (a p) t d", p=P), res[:, :, :])\
                    .then_inc(stored, 16)

            with sp.Fori(0, B - 1) as b:
                sp.wait_ge(led.sems["phase_left"], led.ended("moe1"))
                load_experts(b + 1)
                store_row(b)
                led.end_pass(sp, b + (B + 2))
                sp.wait_ge(stored, 16 * (b + 1))
                sp.sem_inc(led.sems["res_free"], 1)
            store_row(B - 1)
            led.end_pass(sp, 2 * B + 1)
            sp.wait_ge(stored, 16 * B)

        @block.gpsimd
        def _(pool):
            with pool.Fori(0, B) as b:
                ph = Phase(led, "embed")
                pool.wait_ge(consts_in, CONST_DMAS)
                norm_pool(ph, pool, 1)
                ph.leave(pool)
                Phase(led, "attn0").leave(pool)
                ph = Phase(led, "mean0")
                norm_pool(ph, pool, 1)
                ph.leave(pool)
                led.end_pass(pool, b + 1)
            Phase(led, "route0").leave(pool)
            led.end_pass(pool, B + 1)
            with pool.Fori(0, B) as b:
                ph = Phase(led, "moe0")
                norm_pool(ph, pool, 1)
                norm_pool(ph, pool, 2)
                ph.leave(pool)
                ph = Phase(led, "qkv1")
                norm_pool(ph, pool, 1)
                ph.leave(pool)
                Phase(led, "attn1").leave(pool)
                ph = Phase(led, "moe1")
                norm_pool(ph, pool, 1)
                ph.leave(pool)
                ph = Phase(led, "sim2")
                norm_pool(ph, pool, 1)
                norm_pool(ph, pool, 2, power=0.5)
                ph.leave(pool)
                Phase(led, "attn2").leave(pool)
                ph = Phase(led, "moe2")
                norm_pool(ph, pool, 1)
                ph.leave(pool)
                for half, name in enumerate(("rel3a", "rel3b")):
                    ph = Phase(led, name)
                    link = pool_chain(ph, pool)
                    if half == 0:
                        norm_pool(ph, pool, 1)
                        norm_pool(ph, pool, 2)
                        link(nc.gpsimd.memset(qup[0:D, :, S - 1:S], 0.0))
                    for i in range(2 * NB):
                        s, j = i // NB, i % NB
                        c = 512 * j
                        pool.wait_ge(*ph.after("rot_ready", i + 1))
                        link(nc.gpsimd.tensor_tensor(qlo[0:D, s, c:c + 512], rt1[:, i % 2, :], rt2[:, i % 2, :], ALU.add))
                        o = 1 if j == 0 else 0
                        nc.gpsimd.tensor_tensor(qup[0:D, s, c - 1 + o:c + 511], rt1[:, i % 2, o:512], rt2[:, i % 2, o:512],
                                                ALU.add).then_inc(*ph.mark("rot_used"))
                        pool.wait_ge(*ph.own("rot_used"))
                        pool.wait_ge(*ph.after("content_ready", i + 1))
                        link(nc.gpsimd.tensor_copy(qup[64:80, s, c:c + 512], qlo[64:80, s, c:c + 512]))
                    ph.leave(pool)
                    Phase(led, "attn3" + "ab"[half]).leave(pool)
                ph = Phase(led, "rope4")
                norm_pool(ph, pool, 1)
                norm_pool(ph, pool, 2)
                for i in range(2 * NB):
                    j = i // 2
                    dst = (qt, kt)[i % 2]
                    cols = slice(512 * j, 512 * (j + 1))
                    pool.wait_ge(*ph.after("rope_ready", i + 1))
                    nc.gpsimd.tensor_tensor(dst[:, cols], rp1[:, (i % 2) * 512:(i % 2) * 512 + 512],
                                            rp2[:, (i % 2) * 512:(i % 2) * 512 + 512], ALU.add).then_inc(*ph.mark("rope_used"))
                    pool.wait_ge(*ph.own("rope_used"))
                ph.leave(pool)
                Phase(led, "attn4").leave(pool)
                ph = Phase(led, "moe4")
                norm_pool(ph, pool, 1)
                ph.leave(pool)
                led.end_pass(pool, b + (B + 2))

        @block.scalar
        def _(act):
            with act.Fori(0, B) as b:
                ph = Phase(led, "embed")
                qkv_act(ph, act)
                ph.leave(act)
                ph = Phase(led, "attn0")
                attn_act(ph, act, "attn0")
                ph.leave(act)
                Phase(led, "mean0").leave(act)
                led.end_pass(act, b + 1)
            ph = Phase(led, "route0")
            for n in (1, 2):
                act.wait_ge(*ph.after("exp_in", n))
                nc.scalar.activation(r0[:, 1, :, :], r0[:, 0, :, :], ACT.Exp).then_inc(*ph.mark("exp_out"))
            act.wait_ge(*ph.after("exp_in", 3))
            nc.scalar.activation(r0s[:, 3, :], r0s[:, 2, :], ACT.Exp).then_inc(*ph.mark("exp_out"))
            ph.leave(act)
            led.end_pass(act, B + 1)
            with act.Fori(0, B) as b:
                ph = Phase(led, "moe0")
                transpose_act(ph, act, xt, [0, 1, 2])
                for i in range(2 * NB):
                    k, j = i // NB, i % NB
                    act.wait_ge(*ph.after("hid_psum", i + 1))
                    nc.scalar.activation(hid[:, k, 512 * j:512 * (j + 1)], ps[:, 3 + i % 3, :], ACT.Gelu)\
                        .then_inc(*ph.mark("hid_ready"))
                ph.leave(act)
                ph = Phase(led, "qkv1")
                qkv_act(ph, act)
                ph.leave(act)
                ph = Phase(led, "attn1")
                attn_act(ph, act, "attn1")
                ph.leave(act)
                ph = Phase(led, "moe1")
                transpose_act(ph, act, xt, [0, 1, 2])
                transpose_act(ph, act, xt, [0, 1, 2], n0=NB)
                for j in range(NB):
                    act.wait_ge(*ph.after("hid_psum", j + 1))
                    nc.scalar.activation(hid[:, 0, 512 * j:512 * (j + 1)], ps[:, 5 + j, :], ACT.Relu)\
                        .then_inc(*ph.mark("hid_ready"))
                act.wait_ge(*ph.after("bias_ready", 1))
                for layer in range(2):
                    for j in range(NG // GPB):
                        act.wait_ge(*ph.after("expert_psum", layer * (NG // GPB) + j + 1))
                        for i in range(GPB):
                            g = GPB * j + i
                            ins = nc.scalar.activation(hid[:, 1 - layer, GRP * g:GRP * (g + 1)],
                                                       ps[:, 4 * layer + j, GRP * i:GRP * (i + 1)], ACT.Relu,
                                                       bias=bias1[:, layer, g:g + 1])
                        ins.then_inc(*ph.mark("expert_ready"))
                ph.leave(act)
                ph = Phase(led, "sim2")
                transpose_act(ph, act, xt, [0, 1, 2])
                transpose_act(ph, act, qt, [5, 6, 7], n0=NB)
                ph.leave(act)
                ph = Phase(led, "attn2")
                attn_act(ph, act, "attn2")
                ph.leave(act)
                ph = Phase(led, "moe2")
                transpose_act(ph, act, xt, [0, 1, 2])
                transpose_act(ph, act, xt2, [4, 5, 6], n0=NB, width=P)
                for i in range(NB * C2):
                    j, c = i // C2, i % C2
                    act.wait_ge(*ph.after("hid_psum", i + 1))
                    nc.scalar.activation(hid[:, c, 512 * j:512 * (j + 1)], ps[:, i % 4, :], ACT.Relu)\
                        .then_inc(*ph.mark("hid_ready"))
                ph.leave(act)
                for half, name in enumerate(("rel3a", "rel3b")):
                    ph = Phase(led, name)
                    if half == 0:
                        transpose_act(ph, act, xt, [0, 1, 2])
                        act.wait_ge(*ph.after("bias_ready", 1))
                    for i in range(2 * NB):
                        s, j = i // NB, i % NB
                        hd = 2 * half + s
                        bank, cols = 4 * (i % 2), slice(512 * j, 512 * (j + 1))
                        act.wait_ge(*ph.after("q_psum", i + 1))
                        if i >= 2:
                            act.wait_ge(*ph.after("rot_psum", i - 1))
                        nc.scalar.activation(qv[:, i % 2, :], ps[0:DH, bank, :], ACT.Identity,
                                             bias=bias3[0:DH, hd:hd + 1], scale=0.125).then_inc(*ph.mark("qv_ready"))
                        nc.scalar.activation(qlo[64:80, s, cols], ps[64:80, bank, :], ACT.Identity,
                                             bias=bias3[64:80, hd:hd + 1], scale=0.125).then_inc(*ph.mark("content_ready"))
                        act.wait_ge(*ph.after("k_psum", i + 1))
                        nc.scalar.copy(klo[64:80, s, cols], ps[64:80, bank + 1, :])
                        nc.scalar.copy(kup[64:80, s, cols], ps[64:80, bank + 1, :]).then_inc(*ph.mark("k_copied"))
                    ph.leave(act)
                    ph = Phase(led, "attn3" + "ab"[half])
                    attn_act(ph, act, "attn3" + "ab"[half])
                    ph.leave(act)
                ph = Phase(led, "rope4")
                transpose_act(ph, act, xt, [0, 1, 2])
                transpose_act(ph, act, xt, [0, 1, 2], n0=NB)
                act.wait_ge(*ph.after("v_psum", 1))
                nc.scalar.copy(v[:, :, 0:32], ps[:, 3, 0:T * 32].rearrange("p (t d) -> p t d", d=32))
                ph.leave(act)
                ph = Phase(led, "attn4")
                attn_act(ph, act, "attn4")
                ph.leave(act)
                ph = Phase(led, "moe4")
                transpose_act(ph, act, xt, [0, 1, 2])
                transpose_act(ph, act, xt, [0, 1, 2], n0=NB)
                act.wait_ge(*ph.after("exp_in", 1))
                nc.scalar.activation(lg[:, 1, :], lg[:, 0, :], ACT.Exp).then_inc(*ph.mark("exp_out"))
                for i in range(NB * E3 * 2):
                    act.wait_ge(*ph.after("gate_psum", i + 1))
                    if i >= 2:
                        act.wait_ge(*ph.after("gated", i - 1))
                    nc.scalar.activation(sg[:, i % 2, :], ps[0:HC3, 2 * (i % 2), :], ACT.Silu).then_inc(*ph.mark("silu_ready"))
                ph.leave(act)
                led.end_pass(act, b + (B + 2))

        @block.tensor
        def _(pe):
            with pe.Fori(0, B) as b:
                ph = Phase(led, "embed")
                pe.wait_ge(consts_in, CONST_DMAS)
                pe.wait_ge(patches_in, 32 * (b + 1))
                for t in range(TP):
                    ins = nc.tensor.matmul(ps[:, 0, t * D:(t + 1) * D], xp[:, t * P:(t + 1) * P], K("tok_w"), start=True, stop=True)
                ins.then_inc(*ph.mark("emb_psum"))
                qkv_pe(ph, pe, "q0", "k0", "v0")
                ph.leave(pe)
                ph = Phase(led, "attn0")
                attn_pe(ph, pe, "attn0")
                ph.leave(pe)
                ph = Phase(led, "mean0")
                pe.wait_ge(*ph.after("normed", 1))
                for t in range(T):
                    ins = nc.tensor.matmul(ps[0:D, 0, 0:P], x[:, t, :], K("mean"), start=(t == 0), stop=(t == T - 1))
                ins.then_inc(*ph.mark("mean_psum"))
                pe.wait_ge(*ph.after("mean_ready", 1))
                nc.tensor.matmul(ps[:, 1, 0:E0], mean_t[:, :], K("wr0"), start=True, stop=True).then_inc(*ph.mark("logit_psum"))
                ph.leave(pe)
                led.end_pass(pe, b + 1)
            Phase(led, "route0").leave(pe)
            led.end_pass(pe, B + 1)
            with pe.Fori(0, B) as b:
                ph = Phase(led, "moe0")
                pe.wait_ge(*ph.after("normed", 1))
                transpose_pe(ph, x, [0, 1, 2])
                pe.wait_ge(*ph.after("weights_ready", 1))
                for i in range(2 * NB):
                    k, j = i // NB, i % NB
                    if k == 0:
                        pe.wait_ge(*ph.after("xt_copied", j + 1))
                    if i >= 3:
                        pe.wait_ge(*ph.after("hid_ready", i - 2))
                    nc.tensor.matmul(ps[:, 3 + i % 3, :], w1s[:, k, :], xt[:, 512 * j:512 * (j + 1)], start=True, stop=True)\
                        .then_inc(*ph.mark("hid_psum"))
                pe.wait_ge(*ph.after("hid_ready", 2 * NB))
                for t in range(T):
                    for k in range(2):
                        ins = nc.tensor.matmul(ps[:, 6 + t // 6, (t % 6) * D:(t % 6 + 1) * D], hid[:, k, t * P:(t + 1) * P],
                                               w2s[:, k, :], start=(k == 0), stop=(k == 1))
                    if t % 6 == 5:
                        ins.then_inc(*ph.mark("out_psum"))
                ph.leave(pe)
                ph = Phase(led, "qkv1")
                qkv_pe(ph, pe, "q1", "k1", "v1")
                ph.leave(pe)
                ph = Phase(led, "attn1")
                attn_pe(ph, pe, "attn1")
                ph.leave(pe)
                ph = Phase(led, "moe1")
                transpose_pe(ph, ctxt, [0, 1, 2])
                pe.wait_ge(*ph.after("xt_copied", NB))
                rows_pe(ph, K("proj1"), xt, [3, 4], "proj_psum")
                pe.wait_ge(*ph.after("normed", 1))
                transpose_pe(ph, x, [0, 1, 2])
                for j in range(NB):
                    pe.wait_ge(*ph.after("xt_copied", NB + j + 1))
                    nc.tensor.matmul(ps[:, 5 + j, :], K("wi1"), xt[:, 512 * j:512 * (j + 1)], start=True, stop=True)\
                        .then_inc(*ph.mark("hid_psum"))
                pe.wait_ge(*ph.after("bias_ready", 1))
                pe.wait_ge(weights_in, (b + 1) * (16 * 2 * NG))
                for layer in range(2):
                    if layer == 0:
                        pe.wait_ge(*ph.after("hid_ready", NB))
                    else:
                        pe.wait_ge(*ph.after("expert_ready", NG // GPB))
                    for j in range(NG // GPB):
                        bank = ps[:, 4 * layer + j, :]
                        w = GRP * GPB
                        nc.tensor.matmul(bank[:, 0:w], wsi[:, layer, :], hid[:, layer, w * j:w * (j + 1)], start=True, stop=False,
                                         skip_group_check=True)
                        for i in range(GPB):
                            g = GPB * j + i
                            ins = nc.tensor.matmul(bank[:, GRP * i:GRP * (i + 1)], rw[:, layer, g, 0:HID1],
                                                   hid[:, layer, GRP * g:GRP * (g + 1)], start=False, stop=(i == GPB - 1),
                                                   skip_group_check=True)
                        ins.then_inc(*ph.mark("expert_psum"))
                pe.wait_ge(*ph.after("expert_ready", 2 * (NG // GPB)))
                rows_pe(ph, K("wo1"), hid[:, 0, :], [0, 1], "out_psum", rows=P)
                ph.leave(pe)
                ph = Phase(led, "sim2")
                pe.wait_ge(*ph.after("normed", 1))
                transpose_pe(ph, x, [0, 1, 2])
                pe.wait_ge(*ph.after("xt_copied", NB))
                rows_pe(ph, K("w2a"), xt, [3, 4], "v_psum")
                pe.wait_ge(*ph.after("normed", 2))
                transpose_pe(ph, y, [5, 6, 7])
                ph.leave(pe)
                ph = Phase(led, "attn2")
                attn_pe(ph, pe, "attn2")
                ph.leave(pe)
                ph = Phase(led, "moe2")
                pe.wait_ge(*ph.after("normed", 1))
                transpose_pe(ph, xa[:, :, 0:D], [0, 1, 2])
                pe.wait_ge(*ph.after("xt_copied", NB))
                for t in range(T):
                    ins = nc.tensor.matmul(ps[:, 3, t * E2:(t + 1) * E2], xt[:, t * P:(t + 1) * P], K("rw2"), start=True, stop=True)
                ins.then_inc(*ph.mark("logit_psum"))
                pe.wait_ge(*ph.after("normed", 2))
                transpose_pe(ph, xa, [4, 5, 6], width=P)
                for i in range(NB * C2):
                    j, c = i // C2, i % C2
                    if c == 0:
                        pe.wait_ge(*ph.after("xt_copied", NB + j + 1))
                    if i >= 4:
                        pe.wait_ge(*ph.after("hid_ready", i - 3))
                    nc.tensor.matmul(ps[:, i % 4, :], K("w1_2")[:, c * P:(c + 1) * P], xt2[:, 512 * j:512 * (j + 1)],
                                     start=True, stop=True).then_inc(*ph.mark("hid_psum"))
                pe.wait_ge(*ph.after("hid_ready", NB * C2))
                for t in range(T):
                    o = ps[:, 4 + t // 6, (t % 6) * D:(t % 6 + 1) * D]
                    for c in range(C2):
                        nc.tensor.matmul(o, hid[:, c, t * P:(t + 1) * P], K("w2_2")[:, c * D:(c + 1) * D], start=(c == 0), stop=False)
                    ins = nc.tensor.matmul(o, xt2[64:96, t * P:(t + 1) * P], K("b2_2")[64:96, :], start=False, stop=True)
                    if t % 6 == 5:
                        ins.then_inc(*ph.mark("out_psum"))
                ph.leave(pe)
                for half, name in enumerate(("rel3a", "rel3b")):
                    ph = Phase(led, name)
                    if half == 0:
                        pe.wait_ge(*ph.after("normed", 1))
                        transpose_pe(ph, x, [0, 1, 2])
                        pe.wait_ge(*ph.after("xt_copied", NB))
                        rows_pe(ph, K("v3"), xt, [6, 7], "v_psum")
                        pe.wait_ge(*ph.after("v_copied", 1))
                    for i in range(2 * NB):
                        s, j = i // NB, i % NB
                        hd = 2 * half + s
                        bank, cols = 4 * (i % 2), slice(512 * j, 512 * (j + 1))
                        if i >= 2:
                            pe.wait_ge(*ph.after("k_copied", i - 1))
                            pe.wait_ge(*ph.after("rot_ready", i - 1))
                        nc.tensor.matmul(ps[0:80, bank, :], K("wq3")[:, 80 * hd:80 * hd + 80], xt[0:D, cols], start=True, stop=True)\
                            .then_inc(*ph.mark("q_psum"))
                        nc.tensor.matmul(ps[64:80, bank + 1, :], K("wk3")[:, DH * hd:DH * hd + DH], xt[:, cols], start=True, stop=True)\
                            .then_inc(*ph.mark("k_psum"))
                        pe.wait_ge(*ph.after("qv_ready", i + 1))
                        for r in range(2):
                            w = K("wpos3")[:, (2 * hd + r) * D:(2 * hd + r + 1) * D]
                            ins = nc.tensor.matmul(ps[0:D, bank + 2 + r, :], w, qv[:, i % 2, :], start=True, stop=True)
                        ins.then_inc(*ph.mark("rot_psum"))
                    ph.leave(pe)
                    ph = Phase(led, "attn3" + "ab"[half])
                    attn_pe(ph, pe, "attn3" + "ab"[half])
                    ph.leave(pe)
                ph = Phase(led, "rope4")
                transpose_pe(ph, ctxt, [0, 1, 2])
                pe.wait_ge(*ph.after("xt_copied", NB))
                rows_pe(ph, K("wout3"), xt, [3, 4], "proj_psum")
                pe.wait_ge(*ph.after("normed", 1))
                transpose_pe(ph, x, [0, 1, 2])
                pe.wait_ge(*ph.after("xt_copied", 2 * NB))
                for t in range(T):
                    ins = nc.tensor.matmul(ps[:, 3, t * 32:(t + 1) * 32], xt[0:D, t * P:(t + 1) * P], K("wv4"), start=True, stop=True)
                ins.then_inc(*ph.mark("v_psum"))
                for i in range(2 * NB):
                    j, w = i // 2, ("wq4", "wk4")[i % 2]
                    bank = 4 + 2 * (i % 2)
                    if i >= 2:
                        pe.wait_ge(*ph.after("rope_ready", i - 1))
                    for r in range(2):
                        ins = nc.tensor.matmul(ps[:, bank + r, :], K(w)[:, r * P:(r + 1) * P], xt[0:D, 512 * j:512 * (j + 1)],
                                               start=True, stop=True)
                    ins.then_inc(*ph.mark("rope_psum"))
                ph.leave(pe)
                ph = Phase(led, "attn4")
                attn_pe(ph, pe, "attn4")
                ph.leave(pe)
                ph = Phase(led, "moe4")
                transpose_pe(ph, ctxt, [0, 1, 2])
                pe.wait_ge(*ph.after("xt_copied", NB))
                rows_pe(ph, K("wo4"), xt, [3, 4], "proj_psum", rows=D)
                pe.wait_ge(*ph.after("normed", 1))
                transpose_pe(ph, x, [0, 1, 2])
                pe.wait_ge(*ph.after("xt_copied", 2 * NB))
                for t in range(T):
                    ins = nc.tensor.matmul(ps[:, 3, t * E3:(t + 1) * E3], xt[0:D, t * P:(t + 1) * P], K("rt4"), start=True, stop=True)
                ins.then_inc(*ph.mark("logit_psum"))
                pe.wait_ge(*ph.after("exp_in", 1))
                pe.wait_ge(*ph.after("proj_read", 1))

                def down(n):
                    j, e = n // E3, n % E3
                    pe.wait_ge(*ph.after("gated", 2 * n + 2))
                    if e == 0 and j > 0:
                        pe.wait_ge(*ph.after("mixed", 4 * j))
                    for t in range(4):
                        for c in range(2):
                            ins = nc.tensor.matmul(ps[:, 4 + t, e * D:(e + 1) * D], hh[:, n % 2, c, t * P:(t + 1) * P],
                                                   K("w2_4")[:, (2 * e + c) * D:(2 * e + c + 1) * D], start=(c == 0), stop=(c == 1))
                    ins.then_inc(*ph.mark("down_psum"))

                for n in range(NB * E3):
                    j, e = n // E3, n % E3
                    for c in range(2):
                        i = 2 * n + c
                        if i >= 2:
                            pe.wait_ge(*ph.after("gated", i - 1))
                        w = slice((2 * e + c) * HC3, (2 * e + c + 1) * HC3)
                        xs = xt[0:D, 512 * j:512 * (j + 1)]
                        nc.tensor.matmul(ps[0:HC3, 2 * (i % 2), :], K("w1_4")[:, w], xs, start=True, stop=True)\
                            .then_inc(*ph.mark("gate_psum"))
                        nc.tensor.matmul(ps[0:HC3, 2 * (i % 2) + 1, :], K("w3_4")[:, w], xs, start=True, stop=True)\
                            .then_inc(*ph.mark("up_psum"))
                    if n > 0:
                        down(n - 1)
                down(NB * E3 - 1)
                ph.leave(pe)
                led.end_pass(pe, b + (B + 2))

        @block.vector
        def _(dve):
            dve.wait_ge(consts_in, CONST_DMAS)
            for layer in range(2):
                nc.vector.tensor_tensor(wsi[:, layer, :], K("ws1")[:, layer * HID1:(layer + 1) * HID1], ident, ALU.add)
            nc.vector.memset(xt[64:65, :], 1.0)
            nc.vector.memset(mean_t[64:65, :], 1.0)
            with dve.Fori(0, B) as b:
                ph = Phase(led, "embed")
                link = chain(ph, dve)
                dve.wait_ge(patches_in, 32 * (b + 1))
                nc.vector.tensor_copy(h[:, TP:T, :], txt_in)
                dve.wait_ge(*ph.after("emb_psum", 1))
                link(nc.vector.tensor_tensor(h[:, 0:TP, :].rearrange("p t d -> p (t d)"), ps[:, 0, :], K("pos"), ALU.add))
                norm_vec(ph, dve, h[:, :, :], x[:, :, :], 1)
                ready_vec(ph, dve)
                qkv_vec(ph, dve, 1.0)
                ph.leave(dve)
                ph = Phase(led, "attn0")
                attn_vec(ph, dve, "attn0", add_to_h)
                ph.leave(dve)
                ph = Phase(led, "mean0")
                link = chain(ph, dve)
                norm_vec(ph, dve, h[:, :, :], x[:, :, :], 1)
                ready_vec(ph, dve)
                nc.vector.tensor_copy(hall[:, bass.ds(b, 1), :], h[:, :, :].rearrange("p t d -> p (t d)").unsqueeze(1))
                dve.wait_ge(*ph.after("mean_psum", 1))
                nc.vector.tensor_copy(mean_t[0:D, :], ps[0:D, 0, 0:P]).then_inc(*ph.mark("mean_ready"))
                dve.wait_ge(*ph.after("logit_psum", 1))
                nc.vector.tensor_copy(lg0[:, bass.ds(b, 1), :], ps[:, 1, 0:E0].unsqueeze(1))
                ph.leave(dve)
                led.end_pass(dve, b + 1)

            ph = Phase(led, "route0")
            link = chain(ph, dve)
            shape = [P, B, E0]
            src = lg0[:, :, :]
            for n in (1, 2):
                link(nc.vector.tensor_reduce(r0s[:, 0, :], src, AX.X, ALU.max))
                nc.vector.tensor_tensor(r0[:, 0, :, :], src, bc(r0s[:, 0, :], shape), ALU.subtract).then_inc(*ph.mark("exp_in"))
                dve.wait_ge(*ph.after("exp_out", n))
                link(nc.vector.tensor_reduce(r0s[:, 0, :], r0[:, 1, :, :], AX.X, ALU.add))
                link(nc.vector.reciprocal(r0s[:, 1, :], r0s[:, 0, :]))
                link(nc.vector.tensor_tensor(r0[:, 2, :, :], r0[:, 1, :, :], bc(r0s[:, 1, :], shape), ALU.mult))
                if n == 1:
                    load = r0[:, 3, 0, :]
                    link(nc.vector.tensor_reduce(load, r0[:, 2, :, :].rearrange("p b e -> p e b"), AX.X, ALU.add))
                    link(nc.vector.tensor_scalar(load, load, float(S), None, ALU.mult))
                    link(nc.vector.reciprocal(r0[:, 3, 1, :], load))
                    link(nc.vector.tensor_scalar(r0[:, 3, 1, :], r0[:, 3, 1, :], CAP0, 1.0, ALU.mult, ALU.min))
                    link(nc.vector.tensor_tensor(r0[:, 4, :, :], r0[:, 2, :, :],
                                                 r0[:, 3, 1, :].unsqueeze(1).to_broadcast(shape), ALU.mult))
                    src = r0[:, 4, :, :]
            iota = K("iota8").unsqueeze(1).to_broadcast(shape)
            oh1, oh2 = oh0[:, :, 0:E0], oh0[:, :, E0:2 * E0]
            top2_onehots(link, r0[:, 2, :, :], oh1, oh2, r0[:, 5, :, :], r0s[:, 0, :], iota, shape)
            for k, oh in enumerate((oh1, oh2)):
                link(nc.vector.tensor_tensor(r0[:, 6, :, :], oh, r0[:, 2, :, :], ALU.mult))
                link(nc.vector.tensor_reduce(r0s[:, 4 + k, :], r0[:, 6, :, :], AX.X, ALU.add))
            nc.vector.tensor_tensor(r0s[:, 2, :], r0s[:, 5, :], r0s[:, 4, :], ALU.subtract).then_inc(*ph.mark("exp_in"))
            dve.wait_ge(*ph.after("exp_out", 3))
            link(nc.vector.tensor_scalar(r0s[:, 4, :], r0s[:, 3, :], 1.0, None, ALU.add))
            link(nc.vector.reciprocal(r0s[:, 5, :], r0s[:, 4, :]))
            link(nc.vector.tensor_tensor(r0s[:, 6, :], r0s[:, 3, :], r0s[:, 5, :], ALU.mult))
            for k, oh in enumerate((oh1, oh2)):
                link(nc.vector.tensor_tensor(wt0[:, :, k * E0:(k + 1) * E0], oh, bc(r0s[:, 5 + k, :], shape), ALU.mult))
            ph.leave(dve)
            led.end_pass(dve, B + 1)

            with dve.Fori(0, B) as b:
                ph = Phase(led, "moe0")
                link = chain(ph, dve)
                nc.vector.tensor_copy(ohb[:, :].unsqueeze(1), oh0[:, bass.ds(b, 1), :])
                nc.vector.tensor_copy(wtb[:, :].unsqueeze(1), wt0[:, bass.ds(b, 1), :])
                link(nc.vector.tensor_copy(h[:, :, :].rearrange("p t d -> p (t d)").unsqueeze(1), hall[:, bass.ds(b, 1), :]))
                norm_vec(ph, dve, h[:, :, :], x[:, :, :], 1)
                ready_vec(ph, dve)
                for k in range(2):
                    sel = big[0:65, 0:E0 * F0].rearrange("p (f e) -> p f e", e=E0)
                    link(nc.vector.tensor_tensor(sel, K("w1_0").rearrange("p (e f) -> p f e", e=E0),
                                                 ohb[0:65, k * E0:(k + 1) * E0].unsqueeze(1).to_broadcast([65, F0, E0]), ALU.mult))
                    link(nc.vector.tensor_reduce(w1s[:, k, :], sel, AX.X, ALU.add))
                    for table, dst in (("w2_0", w2s), ("b2_0", b2s)):
                        sel = big[:, 0:E0 * D].rearrange("p (f e) -> p f e", e=E0)
                        link(nc.vector.tensor_tensor(sel, K(table).rearrange("p (e f) -> p f e", e=E0),
                                                     wtb[:, k * E0:(k + 1) * E0].unsqueeze(1).to_broadcast([P, D, E0]), ALU.mult))
                        link(nc.vector.tensor_reduce(dst[:, k, :], sel, AX.X, ALU.add))
                nc.vector.tensor_tensor(b2s[:, 0, :], b2s[:, 0, :], b2s[:, 1, :], ALU.add).then_inc(*ph.mark("weights_ready"))
                dve.wait_ge(*ph.own("weights_ready"))
                for i in range(2):
                    dve.wait_ge(*ph.after("out_psum", i + 1))
                    link(nc.vector.tensor_tensor(y[:, 6 * i:6 * i + 6, :], rows_bank([6, 7], i), x[:, 6 * i:6 * i + 6, :], ALU.add))
                link(nc.vector.tensor_tensor(y[:, :, :], y[:, :, :], per_token(b2s[:, 0, :]), ALU.add))
                norm_vec(ph, dve, y[:, :, :], x[:, :, :], 2)
                link(nc.vector.tensor_tensor(x[:, :, :], x[:, :, :], per_token(K("gamma0")), ALU.mult))
                link(nc.vector.tensor_tensor(x[:, :, :], x[:, :, :], per_token(K("beta0")), ALU.add))
                link(nc.vector.tensor_tensor(h[:, :, :], h[:, :, :], x[:, :, :], ALU.add))
                ph.leave(dve)

                ph = Phase(led, "qkv1")
                norm_vec(ph, dve, h[:, :, :], x[:, :, :], 1)
                ready_vec(ph, dve)
                qkv_vec(ph, dve, float(32 ** -0.5))
                ph.leave(dve)
                ph = Phase(led, "attn1")
                attn_vec(ph, dve, "attn1", to_ctxt(32))
                ph.leave(dve)

                ph = Phase(led, "moe1")
                link = chain(ph, dve)
                dve.wait_ge(weights_in, (b + 1) * (16 * 2 * NG))
                for layer in range(2):
                    ins = nc.vector.tensor_scalar(bias1[:, layer, :], rw[:, layer, :, HID1], K("bs1")[:, layer:layer + 1], None, ALU.add)
                ins.then_inc(*ph.mark("bias_ready"))
                for i in range(2):
                    dve.wait_ge(*ph.after("proj_psum", i + 1))
                    link(nc.vector.tensor_tensor(h[:, 6 * i:6 * i + 6, :], rows_bank([3, 4], i), h[:, 6 * i:6 * i + 6, :], ALU.add))
                norm_vec(ph, dve, h[:, :, :], x[:, :, :], 1)
                ready_vec(ph, dve)
                link(nc.vector.tensor_tensor(h[:, :, :], h[:, :, :], per_token(K("bo1")), ALU.add))
                for i in range(2):
                    dve.wait_ge(*ph.after("out_psum", i + 1))
                    nc.vector.tensor_tensor(h[:, 6 * i:6 * i + 6, :], rows_bank([0, 1], i), h[:, 6 * i:6 * i + 6, :], ALU.add)
                ph.leave(dve)

                ph = Phase(led, "sim2")
                link = chain(ph, dve)
                norm_vec(ph, dve, h[:, :, :], x[:, :, :], 1)
                ready_vec(ph, dve)
                link(nc.vector.tensor_tensor(sq[:, :, :], x[:, :, :], x[:, :, :], ALU.mult))
                nc.vector.tensor_reduce(st[:, 3, :], sq[:, :, :], AX.X, ALU.add).then_inc(*ph.mark("var_ready"))
                dve.wait_ge(*ph.after("rstd_ready", 2))
                link(nc.vector.tensor_scalar(st[:, 5, :], st[:, 4, :], 1e-12, None, ALU.max))
                link(nc.vector.reciprocal(st[:, 6, :], st[:, 5, :]))
                link(nc.vector.tensor_tensor(y[:, :, :], x[:, :, :], bc(st[:, 6, :], [P, T, D]), ALU.mult))
                ready_vec(ph, dve)
                for i in range(2):
                    dve.wait_ge(*ph.after("v_psum", i + 1))
                    nc.vector.tensor_copy(v[:, 6 * i:6 * i + 6, :], rows_bank([3, 4], i))
                for j in range(NB):
                    dve.wait_ge(*ph.after("xt_copied", NB + j + 1))
                    nc.vector.tensor_copy(kt[0:D, 512 * j:512 * (j + 1)], qt[0:D, 512 * j:512 * (j + 1)])
                ph.leave(dve)
                ph = Phase(led, "attn2")
                attn_vec(ph, dve, "attn2", add_to_h)
                ph.leave(dve)

                ph = Phase(led, "moe2")
                link = chain(ph, dve)
                norm_vec(ph, dve, h[:, :, :], xa[:, :, 0:D], 1)
                ready_vec(ph, dve)
                dve.wait_ge(*ph.after("logit_psum", 1))
                logits = ps[:, 3, 0:T * E2].rearrange("p (t e) -> p t e", e=E2)
                oh = xa[:, :, D:D + E2]
                iota = K("iota32").unsqueeze(1).to_broadcast([P, T, E2])
                top2_onehots(link, logits, oh, None, None, st[:, 7, :], iota, [P, T, E2])
                link(nc.vector.tensor_scalar(xa[:, :, D + E2:P], oh, -1.0, None, ALU.add))
                ready_vec(ph, dve)
                for i in range(2):
                    dve.wait_ge(*ph.after("out_psum", i + 1))
                    nc.vector.scalar_tensor_tensor(h[:, 6 * i:6 * i + 6, :], rows_bank([4, 5], i), 0.0, h[:, 6 * i:6 * i + 6, :],
                                                   ALU.max, ALU.add)
                ph.leave(dve)

                for half, name in enumerate(("rel3a", "rel3b")):
                    ph = Phase(led, name)
                    link = chain(ph, dve)
                    if half == 0:
                        link(nc.vector.tensor_tensor(bias3[:, :], K("bq3"), K("uv3"), ALU.add))
                        nc.vector.tensor_scalar(bias3[:, :], bias3[:, :], 0.125, None, ALU.mult).then_inc(*ph.mark("bias_ready"))
                        norm_vec(ph, dve, h[:, :, :], x[:, :, :], 1)
                        norm_vec(ph, dve, x[:, :, :], y[:, :, :], 2)
                        link(nc.vector.tensor_tensor(y[:, :, :], y[:, :, :], per_token(K("gamma3")), ALU.mult))
                        link(nc.vector.tensor_tensor(x[:, :, :], y[:, :, :], per_token(K("beta3")), ALU.add))
                        ready_vec(ph, dve)
                        for i in range(2):
                            dve.wait_ge(*ph.after("v_psum", i + 1))
                            ins = nc.vector.tensor_copy(v[:, 6 * i:6 * i + 6, :], rows_bank([6, 7], i))
                        ins.then_inc(*ph.mark("v_copied"))
                    for i in range(2 * NB):
                        j = i % NB
                        bank, cols = 4 * (i % 2), slice(512 * j, 512 * (j + 1))
                        dve.wait_ge(*ph.after("rot_psum", i + 1))
                        if i >= 2:
                            dve.wait_ge(*ph.after("rot_used", i - 1))
                        nc.vector.tensor_tensor(rt1[:, i % 2, :], ps[0:D, bank + 2, :], K("rot_c")[:, cols], ALU.mult)
                        nc.vector.tensor_tensor(rt2[:, i % 2, :], ps[0:D, bank + 3, :], K("rot_s")[:, cols], ALU.mult)\
                            .then_inc(*ph.mark("rot_ready"))
                    ph.leave(dve)
                    ph = Phase(led, "attn3" + "ab"[half])
                    attn_vec(ph, dve, "attn3" + "ab"[half], to_ctxt(DH))
                    ph.leave(dve)

                ph = Phase(led, "rope4")
                link = chain(ph, dve)
                for i in range(2):
                    dve.wait_ge(*ph.after("proj_psum", i + 1))
                    link(nc.vector.tensor_tensor(h[:, 6 * i:6 * i + 6, :], rows_bank([3, 4], i), h[:, 6 * i:6 * i + 6, :], ALU.add))
                norm_vec(ph, dve, h[:, :, :], y[:, :, :], 1)
                norm_vec(ph, dve, y[:, :, :], x[:, :, :], 2, centre=False, eps=RMS_EPS)
                link(nc.vector.tensor_tensor(x[:, :, :], x[:, :, :], per_token(K("rms1")), ALU.mult))
                ready_vec(ph, dve)
                for i in range(2 * NB):
                    j = i // 2
                    bank, o, cols = 4 + 2 * (i % 2), (i % 2) * 512, slice(512 * j, 512 * (j + 1))
                    dve.wait_ge(*ph.after("rope_psum", i + 1))
                    if i >= 2:
                        dve.wait_ge(*ph.after("rope_used", i - 1))
                    nc.vector.tensor_tensor(rp1[:, o:o + 512], ps[:, bank, :], K("rope_c")[:, cols], ALU.mult)
                    nc.vector.tensor_tensor(rp2[:, o:o + 512], ps[:, bank + 1, :], K("rope_s")[:, cols], ALU.mult)\
                        .then_inc(*ph.mark("rope_ready"))
                ph.leave(dve)
                ph = Phase(led, "attn4")
                attn_vec(ph, dve, "attn4", to_ctxt(DH))
                ph.leave(dve)

                ph = Phase(led, "moe4")
                link = chain(ph, dve)
                for i in range(2):
                    dve.wait_ge(*ph.after("proj_psum", i + 1))
                    ins = nc.vector.tensor_tensor(y[:, 6 * i:6 * i + 6, :], rows_bank([3, 4], i), y[:, 6 * i:6 * i + 6, :], ALU.add)
                ins.then_inc(*ph.mark("proj_read"))
                dve.wait_ge(*ph.own("proj_read"))
                norm_vec(ph, dve, y[:, :, :], x[:, :, :], 1, centre=False, eps=RMS_EPS)
                link(nc.vector.tensor_tensor(x[:, :, :], x[:, :, :], per_token(K("rms2")), ALU.mult))
                ready_vec(ph, dve)
                link(nc.vector.tensor_tensor(y[:, :, :], y[:, :, :], h[:, :, :], ALU.add))
                dve.wait_ge(*ph.after("logit_psum", 1))
                shape = [P, T, E3]
                L = [lg[:, i, :].rearrange("p (t e) -> p t e", e=E3) for i in range(5)]
                logits = ps[:, 3, 0:T * E3].rearrange("p (t e) -> p t e", e=E3)
                link(nc.vector.tensor_reduce(st[:, 7, :], logits, AX.X, ALU.max))
                nc.vector.tensor_tensor(L[0], logits, bc(st[:, 7, :], shape), ALU.subtract).then_inc(*ph.mark("exp_in"))
                dve.wait_ge(*ph.after("exp_out", 1))
                link(nc.vector.tensor_reduce(st[:, 7, :], L[1], AX.X, ALU.add))
                link(nc.vector.reciprocal(st[:, 8, :], st[:, 7, :]))
                link(nc.vector.tensor_tensor(L[1], L[1], bc(st[:, 8, :], shape), ALU.mult))
                iota = K("iota8").unsqueeze(1).to_broadcast(shape)
                top2_onehots(link, L[1], L[2], L[3], L[4], st[:, 7, :], iota, shape)
                link(nc.vector.tensor_tensor(L[2], L[2], L[3], ALU.add))
                link(nc.vector.tensor_tensor(L[2], L[2], L[1], ALU.mult))
                link(nc.vector.tensor_reduce(st[:, 7, :], L[2], AX.X, ALU.add))
                link(nc.vector.tensor_scalar(st[:, 8, :], st[:, 7, :], 1e-9, None, ALU.add))
                link(nc.vector.reciprocal(st[:, 9, :], st[:, 8, :]))
                link(nc.vector.tensor_tensor(wt4[:, :, :], L[2], bc(st[:, 9, :], shape), ALU.mult))
                dve.wait_ge(led.sems["res_free"], 1)
                for n in range(NB * E3):
                    j, e = n // E3, n % E3
                    for c in range(2):
                        i = 2 * n + c
                        dve.wait_ge(*ph.after("silu_ready", i + 1))
                        dve.wait_ge(*ph.after("up_psum", i + 1))
                        if n >= 2:
                            dve.wait_ge(*ph.after("down_psum", n - 1))
                        nc.vector.tensor_tensor(hh[:, n % 2, c, :], sg[:, i % 2, :], ps[0:HC3, 2 * (i % 2) + 1, :], ALU.mult)\
                            .then_inc(*ph.mark("gated"))
                    if e == E3 - 1:
                        dve.wait_ge(*ph.after("down_psum", n + 1))
                        for t in range(4):
                            tt = 4 * j + t
                            link(nc.vector.tensor_tensor(moe_w.rearrange("p (e d) -> p e d", e=E3),
                                                         ps[:, 4 + t, :].rearrange("p (e d) -> p e d", e=E3),
                                                         bc(wt4[:, tt, :], [P, E3, D]), ALU.mult))
                            link(nc.vector.tensor_reduce(sq[:, tt, :], moe_w.rearrange("p (e d) -> p d e", e=E3), AX.X, ALU.add))
                            nc.vector.tensor_tensor(res[:, tt, :], sq[:, tt, :], y[:, tt, :], ALU.add).then_inc(*ph.mark("mixed"))
                ph.leave(dve)
                led.end_pass(dve, b + (B + 2))

        return led



def _tables():
    c = {}
    i = np.arange(P)
    c["ident"] = np.eye(P)
    c["mask_low"] = (i[None, :] <= i[:, None]).astype(np.int32)
    c["mask_line"] = (np.arange(P + 1)[None, :] == i[:, None] + 1).astype(np.int32)
    c["mask_future"] = (i[None, :] > i[:, None]).astype(np.int32)
    c["neg"] = np.full((P, P), NEG)
    c["mean"] = np.full((P, P), 1.0 / S)
    c["half"] = np.repeat(np.array([[-0.5] * T + [0.5] * T]), P, 0)
    c["iota8"] = np.repeat(np.arange(8, 0, -1)[None].astype(float), P, 0)
    c["iota32"] = np.repeat(np.arange(32, 0, -1)[None].astype(float), P, 0)
    w = np.exp(np.arange(0, D, 2) * (-np.log(10000.0) / D))
    m = np.arange(S)

    def pe(pos):
        t = np.zeros((D, len(pos)))
        t[0::2], t[1::2] = np.sin(w[:, None] * pos), np.cos(w[:, None] * pos)
        return t
    a = -(m + 1.0)
    c["rot_c"] = np.repeat(np.cos(w[:, None] * a), 2, 0)
    s = np.sin(w[:, None] * a)
    c["rot_s"] = np.stack([-s, s], 1).reshape(D, S)
    inv = 1.0 / 10000.0 ** (np.arange(0, DH, 2) / DH)
    f = np.outer(np.concatenate([inv, inv]), m)
    c["rope_c"], c["rope_s"] = np.zeros((P, S)), np.zeros((P, S))
    for hd in range(HEADS):
        c["rope_c"][32 * hd:32 * hd + DH] = np.cos(f)
        c["rope_s"][32 * hd:32 * hd + DH] = np.sin(f) * np.where(np.arange(DH) < DH // 2, -1.0, 1.0)[:, None]
    return c, pe(m + S).astype(np.float32), pe(m).astype(np.float32)


def _layout(a):
    c, pe_low, pe_up = _tables()

    def aug(w, bias):
        return np.concatenate([w.T, bias[None, :]], 0)

    def rep(vec):
        return np.repeat(vec.reshape(1, -1), P, 0)
    c["tok_w"] = aug(a["L0_tok_W"], a["L0_tok_b"])
    c["pos"] = a["L0_tok_pos_embed"][0].reshape(TP, P, D).transpose(1, 0, 2).reshape(P, TP * D)
    for n in "qkv":
        c[n + "0"] = aug(a["L0_attn_W" + n], a["L0_attn_b" + n])
    c["wr0"] = np.concatenate([a["L0_ffn_Wr"], a["L0_ffn_br"][None]], 0)
    c["w1_0"] = np.concatenate([a["L0_ffn_W1"], a["L0_ffn_b1"][:, None, :]], 1).transpose(1, 0, 2).reshape(65, E0 * F0)
    c["w2_0"] = a["L0_ffn_W2"].transpose(1, 0, 2).reshape(P, E0 * D)
    c["b2_0"] = rep(a["L0_ffn_b2"])
    c["gamma0"], c["beta0"] = rep(a["L0_ffn_gamma"]), rep(a["L0_ffn_beta"])
    wq, bq = a["L1_attn_w_qkv"].reshape(2, 3, 32, D), a["L1_attn_b_qkv"].reshape(2, 3, 32)
    for i, n in enumerate("qkv"):
        c[n + "1"] = aug(wq[:, i].reshape(D, D), bq[:, i].reshape(D))
    c["proj1"] = aug(a["L1_attn_w_proj"], a["L1_attn_b_proj"])
    c["wi1"] = aug(a["L1_ffn_Wi"], a["L1_ffn_bi"])
    c["ws1"] = a["L1_ffn_Ws"][:, 0].transpose(2, 0, 1).reshape(P, 2 * HID1)
    c["bs1"] = a["L1_ffn_bs"][:, 0].T
    c["wo1"], c["bo1"] = a["L1_ffn_Wo"].T, rep(a["L1_ffn_bo"])
    c["w2a"] = aug(a["L2_attn_W"], a["L2_attn_b"])
    c["rw2"] = aug(a["L2_ffn_router_w"], a["L2_ffn_router_b"])
    c["w1_2"] = np.zeros((P, E2 * H2), np.float32)
    c["w1_2"][0:D] = a["L2_ffn_W1"].transpose(1, 0, 2).reshape(D, E2 * H2)
    for e in range(E2):
        c["w1_2"][D + e, H2 * e:H2 * (e + 1)] = a["L2_ffn_b1"][e]
        c["w1_2"][D + E2 + e, H2 * e:H2 * (e + 1)] = BIG
    c["w2_2"] = a["L2_ffn_W2"].reshape(C2, P, D).transpose(1, 0, 2).reshape(P, C2 * D)
    c["b2_2"] = np.zeros((P, D), np.float32)
    c["b2_2"][D:D + E2] = a["L2_ffn_b2"]
    c["gamma3"], c["beta3"] = rep(a["L3_attn_ln_gamma"]), rep(a["L3_attn_ln_beta"])
    c["wq3"], c["bq3"], c["uv3"] = np.zeros((D, HEADS, 80), np.float32), np.zeros((80, HEADS), np.float32), np.zeros((80, HEADS), np.float32)
    for hd in range(HEADS):
        sl = slice(DH * hd, DH * hd + DH)
        for r in (0, 64):
            c["wq3"][:, hd, r:r + DH] = a["L3_attn_Wq"][:, sl]
            c["bq3"][r:r + DH, hd] = a["L3_attn_bq"][sl]
        c["uv3"][0:DH, hd] = a["L3_attn_v_bias"][hd]
        c["uv3"][64:80, hd] = a["L3_attn_u_bias"][hd]
    c["wq3"] = c["wq3"].reshape(D, HEADS * 80)
    c["wk3"] = np.concatenate([a["L3_attn_Wk"], a["L3_attn_bk"][None]], 0)
    c["v3"] = np.concatenate([a["L3_attn_Wv"], a["L3_attn_bv"][None]], 0)
    swap = np.arange(D) ^ 1
    wp = a["L3_attn_Wpos"].reshape(D, HEADS, DH).transpose(2, 1, 0)
    c["wpos3"] = np.stack([wp, wp[:, :, swap]], 2).reshape(DH, HEADS * 2 * D)
    c["wout3"] = np.concatenate([a["L3_attn_Wout"], a["L3_attn_bout"][None]], 0)
    c["rms1"], c["rms2"] = rep(a["L3_ffn_ln1_w"]), rep(a["L3_ffn_ln2_w"])
    turned = np.concatenate([np.arange(DH // 2, DH), np.arange(DH // 2)])
    for n, kv in (("wq", HEADS), ("wk", 2)):
        w = a["L3_ffn_" + n].reshape(kv, DH, D)
        w = np.repeat(w, HEADS // kv, 0)
        z = np.zeros((2, HEADS, 32, D), np.float32)
        z[0, :, 0:DH], z[1, :, 0:DH] = w, w[:, turned]
        c[n + "4"] = z.reshape(2 * P, D).T
    c["wv4"], c["wo4"] = a["L3_ffn_wv"].T, a["L3_ffn_wo"].T
    c["rt4"] = a["L3_ffn_router_w"].T
    for n in (1, 3):
        c[f"w{n}_4"] = a[f"L3_ffn_w{n}"].reshape(E3 * 2 * HC3, D).T
    c["w2_4"] = a["L3_ffn_w2"].reshape(E3, D, 2, HC3).transpose(3, 0, 2, 1).reshape(HC3, E3 * 2 * D)

    pack = np.zeros((P, CONST_COLS), np.float32)
    for name, (rows, at, cols) in CONST_AT.items():
        assert c[name].shape == (rows, cols), (name, c[name].shape)
        part = c[name]
        pack[0:rows, at:at + cols] = part.view(np.float32) if part.dtype == np.int32 else part
    x = a["x"][:, 0].reshape(B, P // 8, 8, 512 // 8, 8).transpose(0, 2, 4, 1, 3).reshape(B, D, NP_)
    patches = np.concatenate([x, np.ones((B, 1, NP_), np.float32)], 1)
    w_route = np.concatenate([a["L1_ffn_Wr"].transpose(0, 1, 3, 2), a["L1_ffn_br"][..., None]], 3)
    return {"consts": pack, "patches": patches, "txt": a["txt"], "route": a["L1_ffn_route_id"].reshape(1, B * NG),
            "w_route": w_route, "pe_low": pe_low, "pe_up": pe_up}


def kernel(**inputs):
    import numpy as _np
    import concourse.bacc as _bacc
    from concourse import mybir as _mybir
    from concourse.bass_utils import run_bass_kernel_spmd as _run

    arrays = _layout({k: _np.asarray(a) for k, a in inputs.items()})
    arrays = {f"in_{k}": _np.ascontiguousarray(a) for k, a in arrays.items()}
    nc = _bacc.Bacc("TRN2", target_bir_lowering=False, num_devices=1)
    args = {k[3:]: nc.dram_tensor(k, a.shape, _mybir.dt.from_np(a.dtype), kind="ExternalInput").ap() for k, a in arrays.items()}
    out = nc.dram_tensor("out_dram", (B, S, D), F32, kind="ExternalOutput").ap()
    build(nc, out=out, **args)
    r = _run(nc, [arrays], core_ids=[0])
    return r.results[0]["out_dram"]
```

```python
import concourse.bass as bass
from concourse import mybir
from contextlib import ExitStack
import numpy as np

F32 = mybir.dt.float32
I32 = mybir.dt.int32
ALU = mybir.AluOpType
ACT = mybir.ActivationFunctionType
AX = mybir.AxisListType

B, D, P = 4, 64, 128
NP_, NT = 1024, 512
S = NP_ + NT
T = S // P
TP = NP_ // P
NB = S // 512
E0, F0 = 8, 128
E1, HID1, GRP = 16, 128, 96
NG = S // GRP
GPB = 4
E2, H2 = 32, 16
C2 = E2 * H2 // P
HEADS, DH = 4, 16
E3, HC3 = 8, 85
TOPK = 64
CHUNKS, PER_CHUNK = 16, 16
BIG = float(2.0 ** 100)
NEG = -4e30
LN_EPS, RMS_EPS = 1e-5, 1e-6
CAP0 = float(-(-(B * S * 5 // 4) // E0))

ENGINES = 4

SIGNALS = {
    "embed": {"pool_step": 1, "rstd_ready": 1, "xt_copied": 3, "emb_psum": 1, "xt_psum": 3, "q_psum": 3, "k_psum": 3,
        "v_psum": 2, "vec_step": 7, "var_ready": 1, "normed": 1},
    "attn0": {"probs_ready": 12, "pt_by_act": 12, "scores_ready": 12, "pt_psum": 36, "ctx_ready": 12,
        "max_ready": 12, "pt_by_vec": 24, "vec_step": 12, "ctx_copied": 12},
    "mean0": {"rstd_ready": 1, "mean_psum": 1, "logit_psum": 1, "vec_step": 6, "var_ready": 1, "normed": 1,
        "mean_ready": 1},
    "route0": {"exp_out": 3, "vec_step": 33, "exp_in": 3},
    "moe0": {"rstd_ready": 2, "xt_copied": 3, "hid_ready": 6, "xt_psum": 3, "hid_psum": 6, "out_psum": 2,
        "vec_step": 31, "var_ready": 2, "normed": 1, "weights_ready": 1},
    "qkv1": {"pool_step": 1, "rstd_ready": 1, "xt_copied": 3, "xt_psum": 3, "q_psum": 3, "k_psum": 3, "v_psum": 2,
        "vec_step": 6, "var_ready": 1, "normed": 1},
    "attn1": {"queries_alone": 24, "probs_ready": 24, "pt_by_act": 24, "scores_ready": 24, "pt_psum": 72,
        "ctx_ready": 24, "max_ready": 24, "pt_by_vec": 48, "vec_step": 24, "ctx_copied": 24},
    "moe1": {"rstd_ready": 1, "xt_copied": 6, "hid_ready": 3, "expert_ready": 8, "xt_psum": 6, "proj_psum": 2,
        "hid_psum": 3, "expert_psum": 8, "out_psum": 2, "bias_ready": 1, "vec_step": 9, "var_ready": 1, "normed": 1},
    "sim2": {"pool_step": 1, "rstd_ready": 2, "xt_copied": 6, "xt_psum": 6, "v_psum": 2, "vec_step": 10,
        "var_ready": 2, "normed": 2},
    "attn2": {"row_copied": 12, "probs_ready": 12, "pt_by_act": 36, "scores_ready": 12, "unsure_summed": 12,
        "pt_psum": 36, "ctx_ready": 12, "vec_step": 300, "unsure_ready": 12, "sparse_ready": 12, "ctx_copied": 12},
    "moe2": {"rstd_ready": 1, "xt_copied": 6, "hid_ready": 12, "xt_psum": 6, "logit_psum": 1, "hid_psum": 12,
        "out_psum": 2, "vec_step": 12, "var_ready": 1, "normed": 2},
    "rel3a": {"pool_step": 7, "upper_cleared": 1, "rstd_ready": 2, "rot_used": 6, "xt_copied": 3, "qv_ready": 6,
        "content_ready": 6, "xt_psum": 3, "v_psum": 2, "q_psum": 6, "k_psum": 6, "rot_psum": 6, "vec_step": 15,
        "bias_ready": 1, "var_ready": 2, "normed": 1, "v_copied": 1, "k_copied": 6, "rot_ready": 6},
    "attn3a": {"queries_alone": 24, "probs_ready": 24, "pt_by_act": 24, "scores_ready": 24, "side_ready": 24,
        "pt_psum": 72, "ctx_ready": 24, "vec_step": 48, "side_read": 24, "max_ready": 24, "pt_by_vec": 48,
        "ctx_copied": 24},
    "rel3b": {"pool_step": 6, "rot_used": 6, "qv_ready": 6, "content_ready": 6, "q_psum": 6, "k_psum": 6,
        "rot_psum": 6, "k_copied": 6, "rot_ready": 6},
    "attn3b": {"queries_alone": 24, "probs_ready": 24, "pt_by_act": 24, "scores_ready": 24, "side_ready": 24,
        "pt_psum": 72, "ctx_ready": 24, "vec_step": 48, "side_read": 24, "max_ready": 24, "pt_by_vec": 48,
        "ctx_copied": 24},
    "rope4": {"rstd_ready": 2, "rope_used": 6, "xt_copied": 6, "xt_psum": 6, "proj_psum": 2, "v_psum": 1,
        "rope_psum": 6, "vec_step": 12, "var_ready": 2, "normed": 1, "rope_ready": 6},
    "attn4": {"queries_alone": 48, "probs_ready": 48, "pt_by_act": 48, "scores_ready": 48, "pt_psum": 96,
        "ctx_ready": 48, "vec_step": 144, "max_ready": 48, "ctx_copied": 48, "pt_by_vec": 48},
    "moe4": {"rstd_ready": 1, "xt_copied": 6, "exp_out": 1, "silu_ready": 48, "xt_psum": 6, "proj_psum": 2,
        "logit_psum": 1, "gate_psum": 48, "up_psum": 48, "down_psum": 24, "proj_read": 1, "vec_step": 50,
        "var_ready": 1, "normed": 1, "exp_in": 1, "gated": 48, "mixed": 12},
}


def const_layout():
    return [
        ("ident", P, P), ("mask_low", P, P), ("mask_line", P, P + 1), ("mask_future", P, P), ("neg", P, 1),
        ("mean", P, P), ("half", P, 2 * T), ("iota8", P, 8), ("iota32", P, 32),
        ("tok_w", 65, D), ("pos", P, TP * D),
        ("q0", 65, D), ("k0", 65, D), ("v0", 65, D),
        ("wr0", 65, E0), ("w1_0", 65, E0 * F0), ("w2_0", P, E0 * D), ("b2_0", P, E0 * D), ("gamma0", P, D), ("beta0", P, D),
        ("q1", 65, D), ("k1", 65, D), ("v1", 65, D), ("proj1", 65, D),
        ("wi1", 65, HID1), ("ws1", P, 2 * HID1), ("bs1", P, 2), ("wo1", P, D), ("bo1", P, D),
        ("w2a", 65, D), ("rw2", 65, E2), ("w1_2", P, C2 * P), ("w2_2", P, C2 * D), ("b2_2", P, D),
        ("gamma3", P, D), ("beta3", P, D), ("wq3", 64, HEADS * 80), ("bq3", 80, HEADS), ("uv3", 80, HEADS),
        ("v3", 65, D), ("wk3", 65, HEADS * DH), ("wpos3", DH, HEADS * 2 * D), ("wout3", 65, D),
        ("rot_c", 64, S), ("rot_s", 64, S),
        ("rms1", P, D), ("rms2", P, D), ("wq4", 64, 2 * P), ("wk4", 64, 2 * P), ("wv4", 64, 32), ("wo4", 64, D),
        ("rope_c", P, S), ("rope_s", P, S),
        ("rt4", 64, E3), ("w1_4", 64, E3 * 2 * HC3), ("w3_4", 64, E3 * 2 * HC3), ("w2_4", HC3, E3 * 2 * D),
    ]


CONST_AT = {}
_at = 0
for _name, _rows, _cols in const_layout():
    CONST_AT[_name] = (_rows, _at, _cols)
    _at += _cols
CONST_COLS = _at


class Ledger:

    def __init__(self, nc, ctx):
        self.nc, self.seen = nc, {}
        names = ["phase_left", "res_free"] + sorted({n for p in SIGNALS.values() for n in p})
        self.sems = {n: ctx.enter_context(nc.semaphore(n)) for n in names}
        self.pass_ended, self.pass_opened, self.turn = (ctx.enter_context(nc.semaphore(n))
                                                        for n in ("pass_ended", "pass_opened", "turn"))

    def phases(self, phase):
        return [p for p in PLAN if phase in p][0]

    def before(self, phase, name):
        phases = self.phases(phase)
        return sum(SIGNALS[p].get(name, 0) for p in phases[:phases.index(phase)])

    def ended(self, phase):
        return (self.phases(phase).index(phase) + 1) * ENGINES

    def end_pass(self, eng, passes):
        eng.drain().then_inc(self.pass_ended, 1)
        if eng is self.nc.gpsimd:
            eng.wait_ge(self.pass_ended, passes * (ENGINES + 1))
            eng.sem_inc(self.turn, 1)
            nums = sorted(s.num for s in self.sems.values())
            assert nums == list(range(nums[0], nums[0] + len(nums)))
            eng.sem_clear(range(nums[0], nums[0] + len(nums)))
            eng.drain().then_inc(self.pass_opened, 1)
        else:
            eng.wait_ge(self.pass_opened, passes)
            eng.sem_inc(self.turn, 1)


class Phase:

    def __init__(self, ledger, name):
        self.led, self.name, self.mine = ledger, name, {}

    def mark(self, name):
        self.mine[name] = self.mine.get(name, 0) + 1
        seen = self.led.seen.setdefault(self.name, {})
        seen[name] = seen.get(name, 0) + 1
        return self.led.sems[name], 1

    def after(self, name, k):
        return self.led.sems[name], self.led.before(self.name, name) + k

    def own(self, name):
        return self.after(name, self.mine[name])

    def leave(self, eng):
        eng.drain().then_inc(self.led.sems["phase_left"], 1)
        eng.wait_ge(self.led.sems["phase_left"], self.led.ended(self.name))


PLAN = [
    ["embed", "attn0", "mean0"],
    ["route0"],
    ["moe0", "qkv1", "attn1", "moe1", "sim2", "attn2", "moe2", "rel3a", "attn3a", "rel3b", "attn3b",
     "rope4", "attn4", "moe4"],
]


def units_of(kind):
    heads = {"attn0": [0], "attn1": [0, 1], "attn2": [0], "attn3a": [0, 1], "attn3b": [2, 3], "attn4": [0, 1, 2, 3]}[kind]
    return [(h, q) for h in heads for q in range(T)]


def build(nc, consts, patches, txt, route, w_route, pe_low, pe_up, out):
    with ExitStack() as ctx:
        def sb(name, shape, dt=F32):
            return ctx.enter_context(nc.sbuf_tensor(name, shape, dt))

        cst = sb("cst", [P, CONST_COLS])
        h = sb("h", [P, T, D])
        x = sb("x", [P, T, D])
        y = sb("y", [P, T, D])
        sq = sb("sq", [P, T, D])
        ctxt = sb("ctxt", [P, T, D])
        res = sb("res", [P, T, D])
        v = sb("v", [P, T, D])
        hall = sb("hall", [P, B, T * D])
        xt = sb("xt", [P, S])
        qlo = sb("qlo", [P, 2, S])
        qup = sb("qup", [P, 2, S])
        klo = sb("klo", [P, 2, S])
        kup = sb("kup", [P, 2, S])
        big = sb("big", [P, 4 * S])
        rw = sb("rw", [P, 2, NG, HID1 + 1])
        st = sb("st", [P, 16, T])
        negmax = sb("negmax", [P, 48])
        rowsum = sb("rowsum", [P, 48])
        qz = sb("qz", [P, HEADS, 2, P])
        rinv = sb("rinv", [P, 48])
        lg0 = sb("lg0", [P, B, E0])
        r0 = sb("r0", [P, 8, B, E0])
        r0s = sb("r0s", [P, 8, B])
        oh0 = sb("oh0", [P, B, 2 * E0])
        wt0 = sb("wt0", [P, B, 2 * E0])
        ohb = sb("ohb", [P, 2 * E0])
        wtb = sb("wtb", [P, 2 * E0])
        mean_t = sb("mean_t", [P, P])
        w1s = sb("w1s", [P, 2, F0])
        w2s = sb("w2s", [P, 2, D])
        b2s = sb("b2s", [P, 2, D])
        bias1 = sb("bias1", [P, 2, NG])
        bias3 = sb("bias3", [80, HEADS])
        lg = sb("lg", [P, 5, T * E3])
        wt4 = sb("wt4", [P, T, E3])
        route_sb = sb("route_sb", [1, B * NG], I32)
        ps = ctx.enter_context(nc.psum_tensor("ps", [P, 8, 512], F32))

        xp = qup[0:65, 0, 0:NP_]
        txt_in = qup[:, 1, 0:(T - TP) * D].rearrange("p (t d) -> p t d", d=D)
        prob = big[:, 0:2 * S].rearrange("p (s n) -> p s n", s=2)
        pt = big[:, 2 * S:4 * S].rearrange("p (s g n) -> p s g n", s=2, g=NB)
        hid = big[:, :].rearrange("p (c n) -> p c n", c=4)
        xt2 = qup[:, 0, :]
        xa = big[:, 0:S].rearrange("p (t n) -> p t n", n=P)
        work = qup[:, 0, :]
        row_copy = (big[:, S:2 * S], big[:, 3 * S:4 * S])
        sparse = qup[:, 1, :]
        qt = qlo[:, 0, :]
        kt = qlo[:, 1, :]
        qv = big[:, 0:2 * 512].rearrange("p (s n) -> p s n", s=2)
        rt1 = big[0:D, 1024:2048].rearrange("p (s n) -> p s n", s=2)
        rt2 = big[0:D, 2048:3072].rearrange("p (s n) -> p s n", s=2)
        rp1 = big[:, 0:S]
        rp2 = big[:, S:2 * S]
        sg = big[0:HC3, 0:1024].rearrange("p (s n) -> p s n", s=2)
        hh = big[0:HC3, 1024:1024 + 2048].rearrange("p (s c n) -> p s c n", s=2, c=2)
        moe_w = big[:, 4096:4096 + 512]

        def K(name):
            rows, at, cols = CONST_AT[name]
            return cst[0:rows, at:at + cols]

        def W(name):
            _, at, cols = CONST_AT[name]
            return cst[:, at:at + cols]

        ident = K("ident")
        wsi = K("ws1").rearrange("p (l n) -> p l n", l=2)
        spare = ctxt[:, :, :].rearrange("p t d -> p (t d)")
        n_cand = CHUNKS * PER_CHUNK
        cand, cand_left = spare[:, 0:n_cand], spare[:, n_cand:2 * n_cand]
        top8 = spare[:, 2 * n_cand:2 * n_cand + TOPK + 8].rearrange("p (r e) -> p r e", e=8)
        limit = spare[:, 2 * n_cand + TOPK + 8:2 * n_cand + TOPK + 9]
        unsure = spare[:, 2 * n_cand + TOPK + 9:2 * n_cand + TOPK + 10]
        unsure_any = spare[0:1, 2 * n_cand + TOPK + 10:2 * n_cand + TOPK + 11].bitcast(I32)
        led = Ledger(nc, ctx)

        def dsem(name):
            return ctx.enter_context(nc.semaphore(name))

        consts_in = dsem("consts_in")
        patches_in = dsem("patches_in")
        route_in = dsem("route_in")
        weights_in = dsem("weights_in")
        stored = dsem("stored")
        CONST_DMAS = 16 * 6


        def chain(ph, eng):
            def link(ins):
                ins.then_inc(*ph.mark("vec_step"))
                eng.wait_ge(*ph.own("vec_step"))
            return link

        def pool_chain(ph, pool):
            def link(ins):
                ins.then_inc(*ph.mark("pool_step"))
                pool.wait_ge(*ph.own("pool_step"))
            return link

        def bc(ap, shape):
            return ap.unsqueeze(2).to_broadcast(shape)

        def per_token(ap):
            return ap.unsqueeze(1).to_broadcast([P, T, D])

        def norm_vec(ph, dve, src, dst, n, centre=True, eps=LN_EPS, tail=None):
            link = chain(ph, dve)
            xc = src
            if centre:
                link(nc.vector.tensor_reduce(st[:, 0, :], src, AX.X, ALU.add))
                link(nc.vector.tensor_scalar(st[:, 1, :], st[:, 0, :], -1.0 / D, None, ALU.mult))
                link(nc.vector.tensor_tensor(dst, src, bc(st[:, 1, :], [P, T, D]), ALU.add))
                xc = dst
            link(nc.vector.tensor_tensor(sq[:, :, :], xc, xc, ALU.mult))
            link(nc.vector.tensor_reduce(st[:, 2, :], sq[:, :, :], AX.X, ALU.add))
            nc.vector.tensor_scalar(st[:, 3, :], st[:, 2, :], 1.0 / D, eps, ALU.mult, ALU.add)\
                .then_inc(*ph.mark("var_ready"))
            dve.wait_ge(*ph.after("rstd_ready", n))
            link(nc.vector.tensor_tensor(dst, xc, bc(st[:, 4, :], [P, T, D]), ALU.mult))

        def norm_pool(ph, pool, n, power=-0.5):
            pool.wait_ge(*ph.after("var_ready", n))
            e = K("half")[:, 0:T] if power < 0 else K("half")[:, T:2 * T]
            nc.gpsimd.tensor_tensor(st[:, 4, :], st[:, 3, :], e, ALU.pow).then_inc(*ph.mark("rstd_ready"))
            pool.wait_ge(*ph.own("rstd_ready"))

        def clear_upper(ph, pool):
            nc.gpsimd.memset(qlo[D:P, :, :], 0.0).then_inc(*ph.mark("pool_step"))
            pool.wait_ge(*ph.own("pool_step"))

        def ready_vec(ph, dve, name="normed"):
            nc.vector.tensor_copy(st[:, 15, 0:1], st[:, 4, 0:1]).then_inc(*ph.mark(name))

        def transpose_pe(ph, src, banks, width=D):
            for t in range(T):
                ins = nc.tensor.transpose(ps[0:width, banks[t // 4], (t % 4) * P:(t % 4 + 1) * P], src[:, t, :], ident)
                if t % 4 == 3:
                    ins.then_inc(*ph.mark("xt_psum"))

        def transpose_act(ph, act, dst, banks, n0=0, width=D):
            for j in range(NB):
                act.wait_ge(*ph.after("xt_psum", n0 + j + 1))
                nc.scalar.copy(dst[0:width, 512 * j:512 * (j + 1)], ps[0:width, banks[j], :]).then_inc(*ph.mark("xt_copied"))

        def rows_pe(ph, w, src, banks, name, n=D):
            for t in range(T):
                ins = nc.tensor.matmul(ps[:, banks[t // 6], (t % 6) * n:(t % 6 + 1) * n], src[:, t * P:(t + 1) * P], w,
                                       start=True, stop=True)
                if t % 6 == 5:
                    ins.then_inc(*ph.mark(name))

        def rows_bank(banks, i, n=D):
            return ps[:, banks[i], 0:6 * n].rearrange("p (t d) -> p t d", d=n)

        def qkv_pe(ph, pe, wq, wk, wv):
            pe.wait_ge(*ph.after("normed", 1))
            transpose_pe(ph, x, [0, 1, 2])
            for j in range(NB):
                pe.wait_ge(*ph.after("xt_copied", j + 1))
                nc.tensor.matmul(ps[0:D, 3 + j, :], W(wq), xt[:, 512 * j:512 * (j + 1)], start=True, stop=True)\
                    .then_inc(*ph.mark("q_psum"))
            for j in range(NB):
                nc.tensor.matmul(ps[0:D, (6 + j) % 8, :], W(wk), xt[:, 512 * j:512 * (j + 1)], start=True, stop=True)\
                    .then_inc(*ph.mark("k_psum"))
            rows_pe(ph, W(wv), xt, [1, 2], "v_psum")

        def qkv_act(ph, act):
            transpose_act(ph, act, xt, [0, 1, 2])
            for j in range(NB):
                act.wait_ge(*ph.after("k_psum", j + 1))
                nc.scalar.copy(kt[0:D, 512 * j:512 * (j + 1)], ps[0:D, (6 + j) % 8, :])

        def qkv_vec(ph, dve, scale):
            for j in range(NB):
                dve.wait_ge(*ph.after("q_psum", j + 1))
                nc.vector.tensor_scalar(qt[0:D, 512 * j:512 * (j + 1)], ps[0:D, 3 + j, :], scale, None, ALU.mult)
            for i in range(2):
                dve.wait_ge(*ph.after("v_psum", i + 1))
                nc.vector.tensor_copy(v[:, 6 * i:6 * i + 6, :], rows_bank([1, 2], i))


        def tiles(kind, q):
            return q + 1 if kind == "attn4" else T

        def groups(kind, q):
            return -(-tiles(kind, q) // 4)

        def before_groups(kind, u):
            return sum(groups(kind, q) for _, q in units_of(kind)[:u])

        def slot_of(kind, u):
            return 0 if kind == "attn2" else u % 2

        def copier(kind, g):
            return "pt_by_act" if kind == "attn2" or g == 0 else "pt_by_vec"

        def copied(kind, u, g):
            name = copier(kind, g)
            last = sum(copier(kind, i) == name for i in range(g + 1))
            return name, last + sum(copier(kind, i) == name for _, q in units_of(kind)[:u] for i in range(groups(kind, q)))

        def context_of(kind, hd):
            w, at = {"attn0": (D, 0), "attn1": (32, 32 * hd), "attn2": (D, 0), "attn4": (DH, DH * (hd // 2))}.get(
                kind, (DH, DH * hd))
            return ps[:, 7, 448 + at:448 + at + w]

        def alone(kind):
            return kind in ("attn1", "attn4") or kind.startswith("attn3")

        def head_rows(kind, hd):
            return (2, slice(64, 80)) if kind.startswith("attn3") else (hd, slice(32 * hd, 32 * hd + 32))

        def attn_pool(ph, pool, kind):
            link = pool_chain(ph, pool)
            for u, (hd, q) in enumerate(units_of(kind)):
                slot, rows = head_rows(kind, hd)
                if u >= 2:
                    pool.wait_ge(*ph.after("side_ready" if kind.startswith("attn3") else "scores_ready", u - 1))
                src = qlo[rows, hd % 2, :] if kind.startswith("attn3") else qt[rows, :]
                nc.gpsimd.tensor_copy(qz[rows, slot, u % 2, :], src[:, q * P:(q + 1) * P]).then_inc(*ph.mark("queries_alone"))
                pool.wait_ge(*ph.own("queries_alone"))

        def attn_pe(ph, pe, kind):
            units = units_of(kind)

            def scores(u, j):
                hd, q = units[u]
                if u >= len(units) or 4 * j >= tiles(kind, q):
                    return
                if j == 0 and u >= 2:
                    pe.wait_ge(*ph.after("probs_ready", u - 1))
                bank = ps[:, 3 * (u % 2) + j, :]
                lo, hi = 4 * j, min(4 * j + 4, tiles(kind, q))
                qs = slice(q * P, (q + 1) * P)
                if kind.startswith("attn3"):
                    s = hd % 2
                    cut = min(max(q, lo), hi)
                    parts = [(lo, cut, qlo, klo), (cut, hi, qup, kup)]
                    parts = [(a, b, qq, kk) for a, b, qq, kk in parts if a < b]
                    for a, b, qq, kk in parts:
                        ins = nc.tensor.matmul(bank[:, (a - lo) * P:(b - lo) * P], qq[:, s, qs], kk[:, s, a * P:b * P],
                                               start=True, stop=True)
                else:
                    qq = qt[:, qs]
                    if alone(kind):
                        pe.wait_ge(*ph.after("queries_alone", u + 1))
                        qq = qz[:, hd, u % 2, :]
                    ins = nc.tensor.matmul(bank[:, 0:(hi - lo) * P], qq, kt[:, lo * P:hi * P], start=True, stop=True)
                if hi == tiles(kind, q):
                    ins.then_inc(*ph.mark("scores_ready"))

            def side(u):
                hd, q = units[u]
                s = hd % 2
                if u >= 2:
                    pe.wait_ge(*ph.after("ctx_copied", u - 1))
                qs = slice(q * P, (q + 1) * P)
                n = min(P + 1, S - q * P)
                nc.tensor.matmul(ps[:, 7, 0:P], qlo[:, s, qs], klo[:, s, qs], start=True, stop=True)
                pe.wait_ge(*ph.after("queries_alone", u + 1))
                nc.tensor.matmul(ps[:, 7, P:P + n], qz[:, 2, u % 2, :], klo[:, s, q * P:q * P + n], start=True, stop=True)\
                    .then_inc(*ph.mark("side_ready"))

            def turn(u, g):
                if g == 0:
                    pe.wait_ge(*ph.after("probs_ready", u + 1))
                if g > 0:
                    pe.wait_ge(*ph.after(*copied(kind, u, g - 1)))
                elif u > 0:
                    pe.wait_ge(*ph.after(*copied(kind, u - 1, groups(kind, units[u - 1][1]) - 1)))
                n = min(4, tiles(kind, units[u][1]) - 4 * g)
                for i in range(n):
                    ins = nc.tensor.transpose(ps[:, 6, i * P:(i + 1) * P], prob[:, slot_of(kind, u), (4 * g + i) * P:(4 * g + i + 1) * P],
                                              ident)
                ins.then_inc(*ph.mark("pt_psum"))

            def context(u, g):
                hd, q = units[u]
                pe.wait_ge(*ph.after(*copied(kind, u, g)))
                if g == 0:
                    if u > 0:
                        pe.wait_ge(*ph.after("ctx_copied", u))
                    if kind.startswith("attn3") and u + 1 < len(units):
                        pe.wait_ge(*ph.after("side_read", u + 2))
                n = tiles(kind, q)
                for i in range(4 * g, min(4 * g + 4, n)):
                    ins = nc.tensor.matmul(ps[:, 7, 448:448 + D], pt[:, slot_of(kind, u), g, (i % 4) * P:(i % 4 + 1) * P],
                                           v[:, i, :], start=(i == 0), stop=(i == n - 1))
                if g == groups(kind, q) - 1:
                    ins.then_inc(*ph.mark("ctx_ready"))

            for u in (0, 1):
                for j in range(NB):
                    scores(u, j)
            if kind.startswith("attn3"):
                side(0)
            for u in range(len(units)):
                more = groups(kind, units[u][1])
                ahead = u + 2 < len(units)
                if kind == "attn2":
                    pe.wait_ge(*ph.after("unsure_ready", u + 1))
                    nc.tensor.matmul(ps[:, 7, 0:1], K("mean"), unsure, start=True, stop=True).then_inc(*ph.mark("unsure_summed"))
                turn(u, 0)
                if kind.startswith("attn3") and u + 1 < len(units):
                    if u == 0:
                        pe.wait_ge(*ph.after("side_read", 1))
                    else:
                        pe.wait_ge(*ph.after("ctx_copied", u))
                    side(u + 1)
                if ahead:
                    scores(u + 2, 0)
                if more > 1:
                    turn(u, 1)
                context(u, 0)
                if ahead:
                    scores(u + 2, 1)
                if more > 2:
                    turn(u, 2)
                if more > 1:
                    context(u, 1)
                if ahead:
                    scores(u + 2, 2)
                if more > 2:
                    context(u, 2)

        def copy_group(ph, eng, kind, u, g, copy):
            q = units_of(kind)[u][1]
            n = min(4, tiles(kind, q) - 4 * g) * P
            eng.wait_ge(*ph.after("pt_psum", before_groups(kind, u) + g + 1))
            if u >= 2 or (u == 1 and kind == "attn2"):
                eng.wait_ge(*ph.after("ctx_ready", u if kind == "attn2" else u - 1))
            copy(pt[:, slot_of(kind, u), g, 0:n], ps[:, 6, 0:n]).then_inc(*ph.mark(copier(kind, g)))

        def attn_act(ph, act, kind):
            units = units_of(kind)

            def exps(u):
                q = units[u][1]
                n = tiles(kind, q) * P
                if kind == "attn2":
                    act.wait_ge(*ph.after("sparse_ready", u + 1))
                    src, bias = sparse, 0.0
                else:
                    act.wait_ge(*ph.after("max_ready", u + 1))
                    src = ps[:, 3 * (u % 2):3 * (u % 2) + NB, :].rearrange("p b n -> p (b n)")[:, 0:n]
                    bias = negmax[:, u:u + 1]
                if kind == "attn2" and u >= 1:
                    act.wait_ge(*ph.after("pt_psum", before_groups(kind, u)))
                elif u >= 2:
                    act.wait_ge(*ph.after("pt_psum", before_groups(kind, u - 1)))
                scale = 0.25 if kind == "attn4" else 1.0
                nc.scalar.activation(prob[:, slot_of(kind, u), 0:n], src, ACT.Exp, bias=bias, scale=scale,
                                     accum_out=rowsum[:, u:u + 1]).then_inc(*ph.mark("probs_ready"))

            def copy_row(u):
                act.wait_ge(*ph.after("scores_ready", u + 1))
                if u >= 2:
                    act.wait_ge(*ph.after("sparse_ready", u - 1))
                nc.scalar.copy(row_copy[u % 2], ps[:, 3 * (u % 2):3 * (u % 2) + NB, :].rearrange("p b n -> p (b n)"))\
                    .then_inc(*ph.mark("row_copied"))

            if kind == "attn2":
                copy_row(0)
                copy_row(1)
            exps(0)
            for u in range(len(units)):
                for g in range(groups(kind, units[u][1])):
                    if copier(kind, g) == "pt_by_act":
                        copy_group(ph, act, kind, u, g, nc.scalar.copy)
                        if g == 0 and u + 1 < len(units) and kind != "attn2":
                            exps(u + 1)
                if kind == "attn2" and u + 2 < len(units):
                    copy_row(u + 2)
                if u + 1 < len(units) and kind == "attn2":
                    exps(u + 1)

        def attn_vec(ph, dve, kind, dest):
            units = units_of(kind)
            link = chain(ph, dve)

            def maxima(u):
                hd, q = units[u]
                n = tiles(kind, q) * P
                flat = ps[:, 3 * (u % 2):3 * (u % 2) + NB, :].rearrange("p b n -> p (b n)")
                if kind == "attn2":
                    dve.wait_ge(*ph.after("row_copied", u + 1))
                else:
                    dve.wait_ge(*ph.after("scores_ready", u + 1))
                if kind.startswith("attn3"):
                    dve.wait_ge(*ph.after("side_ready", u + 1))
                    m = min(P + 1, S - q * P)
                    link(nc.vector.copy_predicated(flat[:, q * P:(q + 1) * P], K("mask_low").bitcast(I32), ps[:, 7, 0:P]))
                    ins = nc.vector.copy_predicated(flat[:, q * P:q * P + m], K("mask_line")[:, 0:m].bitcast(I32),
                                                    ps[:, 7, P:P + m])
                    ins.then_inc(*ph.mark("side_read"))
                    dve.wait_ge(*ph.own("side_read"))
                if kind == "attn4":
                    link(nc.vector.copy_predicated(flat[:, q * P:(q + 1) * P], K("mask_future").bitcast(I32),
                                                   K("neg").to_broadcast([P, P])))
                if kind == "attn2":
                    if u >= 1:
                        dve.wait_ge(*ph.after("probs_ready", u))
                    row = row_copy[u % 2]
                    row_c = row.rearrange("p (n c) -> p c n", c=CHUNKS)
                    work_c = work.rearrange("p (n c) -> p c n", c=CHUNKS)
                    cand_c = cand.rearrange("p (c k) -> p c k", c=CHUNKS)
                    src = row_c
                    for r in range(PER_CHUNK // 8):
                        if r > 0:
                            for c in range(CHUNKS):
                                ins = nc.vector.match_replace(work_c[:, c, :], cand_c[:, c, 8 * r - 8:8 * r], src[:, c, :], -4.0)
                            link(ins)
                            src = work_c
                        for c in range(CHUNKS):
                            ins = nc.vector.max(cand_c[:, c, 8 * r:8 * r + 8], src[:, c, :])
                        link(ins)
                    src = cand
                    for r in range(TOPK // 8):
                        link(nc.vector.max(top8[:, r, :], src))
                        link(nc.vector.match_replace(cand_left, top8[:, r, :], src, -4.0))
                        src = cand_left
                    link(nc.vector.max(top8[:, TOPK // 8, :], src))
                    last = top8[:, TOPK // 8 - 1, 7:8]
                    link(nc.vector.tensor_reduce(limit, cand_c[:, :, PER_CHUNK - 1], AX.X, ALU.max))
                    link(nc.vector.tensor_tensor(limit, limit, top8[:, TOPK // 8, 0:1], ALU.max))
                    nc.vector.tensor_tensor(unsure, limit, last, ALU.is_ge).then_inc(*ph.mark("unsure_ready"))
                    link(nc.vector.scalar_tensor_tensor(sparse, row, last, row, ALU.is_ge, ALU.mult))
                    dve.wait_ge(*ph.after("unsure_summed", u + 1))
                    link(nc.vector.tensor_scalar(unsure_any, ps[0:1, 7, 0:1], 0.0, None, ALU.is_gt))
                    any_row = dve.value_load(unsure_any, min_val=0, max_val=1)
                    with dve.If(any_row > 0):
                        src = row
                        for r in range(TOPK // 8):
                            nc.vector.max(top8[:, r, :], src)
                            dve.drain()
                            nc.vector.match_replace(work, top8[:, r, :], src, -4.0)
                            dve.drain()
                            src = work
                        nc.vector.scalar_tensor_tensor(sparse, work, -3.0, row, ALU.is_lt, ALU.mult)
                        dve.drain()
                    nc.vector.tensor_copy(limit, last).then_inc(*ph.mark("sparse_ready"))
                    return
                if kind == "attn4":
                    link(nc.vector.tensor_reduce(st[:, 14, u % T:u % T + 1], flat[:, 0:n], AX.X, ALU.max, negate=True))
                    nc.vector.tensor_scalar(negmax[:, u:u + 1], st[:, 14, u % T:u % T + 1], 0.25, None, ALU.mult)\
                        .then_inc(*ph.mark("max_ready"))
                else:
                    nc.vector.tensor_reduce(negmax[:, u:u + 1], flat[:, 0:n], AX.X, ALU.max, negate=True)\
                        .then_inc(*ph.mark("max_ready"))

            maxima(0)
            for u in range(len(units)):
                hd, q = units[u]
                if u + 1 < len(units):
                    maxima(u + 1)
                for g in range(groups(kind, q)):
                    if copier(kind, g) == "pt_by_vec":
                        copy_group(ph, dve, kind, u, g, nc.vector.tensor_copy)
                dve.wait_ge(*ph.after("probs_ready", u + 1))
                link(nc.vector.reciprocal(rinv[:, u:u + 1], rowsum[:, u:u + 1]))
                dve.wait_ge(*ph.after("ctx_ready", u + 1))
                dest(u, hd, q, context_of(kind, hd), rinv[:, u:u + 1]).then_inc(*ph.mark("ctx_copied"))

        def add_to_h(u, hd, q, o, r):
            return nc.vector.scalar_tensor_tensor(h[:, q, :], o, r, h[:, q, :], ALU.mult, ALU.add)

        def to_ctxt(w):
            def put(u, hd, q, o, r):
                return nc.vector.tensor_scalar(ctxt[:, q, w * hd:w * hd + w], o, r, None, ALU.mult)
            return put

        def top2_onehots(link, src, oh1, oh2, tmp, m, iota, shape):
            for oh, s in ((oh1, src), (oh2, tmp)):
                link(nc.vector.tensor_reduce(m, s, AX.X, ALU.max))
                link(nc.vector.tensor_tensor(oh, s, bc(m, shape), ALU.is_equal))
                link(nc.vector.tensor_tensor(oh, oh, iota, ALU.mult))
                link(nc.vector.tensor_reduce(m, oh, AX.X, ALU.max))
                link(nc.vector.tensor_tensor(oh, oh, bc(m, shape), ALU.is_equal))
                if oh is oh1 and oh2 is not None:
                    link(nc.vector.scalar_tensor_tensor(tmp, oh, -BIG, src, ALU.mult, ALU.add))
                if oh2 is None:
                    return

        block = ctx.enter_context(nc.Block())

        @block.sync
        def _(sp):
            half = CONST_COLS // 2
            sp.dma_start(cst[:, 0:half], consts[:, 0:half]).then_inc(consts_in, 16)
            sp.dma_start(cst[:, half:CONST_COLS], consts[:, half:CONST_COLS]).then_inc(consts_in, 16)
            sp.dma_start(route_sb[:, :], route).then_inc(route_in, 16)
            for s in range(2):
                sp.dma_start(klo[0:D, s, :], pe_low).then_inc(consts_in, 16)
            sp.dma_start(kup[0:D, 0, :], pe_up).then_inc(consts_in, 16)
            sp.dma_start(kup[0:D, 1, :], pe_up).then_inc(consts_in, 16)

            def load_tokens(b):
                sp.dma_start(xp, patches[bass.ds(b, 1), :, :].rearrange("a p n -> (a p) n")).then_inc(patches_in, 16)
                sp.dma_start(txt_in, txt[bass.ds(b, 1), :, :].rearrange("a (t p) d -> (a p) t d", p=P)).then_inc(patches_in, 16)

            def load_experts(b):
                for g in range(NG):
                    e = sp.value_load(route_sb[0:1, bass.ds(b * NG + g, 1)], min_val=0, max_val=E1 - 1)
                    for layer in range(2):
                        sp.dma_start(rw[:, layer, g, :], w_route[layer, bass.ds(e, 1), :, :].rearrange("a p n -> (a p) n"))\
                            .then_inc(weights_in, 16)

            load_tokens(0)
            with sp.Fori(0, B - 1) as b:
                sp.wait_ge(led.sems["phase_left"], led.ended("embed"))
                load_tokens(b + 1)
                sp.wait_ge(led.sems["phase_left"], led.ended("mean0"))
                led.end_pass(sp, b + 1)
            sp.wait_ge(led.sems["phase_left"], led.ended("mean0"))
            led.end_pass(sp, B)
            sp.wait_ge(route_in, 16)
            load_experts(0)
            sp.wait_ge(led.sems["phase_left"], led.ended("route0"))
            led.end_pass(sp, B + 1)

            sp.sem_inc(led.sems["res_free"], 1)

            def store_row(b):
                sp.wait_ge(led.sems["phase_left"], led.ended("moe4"))
                sp.dma_start(out[bass.ds(b, 1), :, :].rearrange("a (t p) d -> (a p) t d", p=P), res[:, :, :])\
                    .then_inc(stored, 16)

            with sp.Fori(0, B - 1) as b:
                sp.wait_ge(led.sems["phase_left"], led.ended("moe1"))
                load_experts(b + 1)
                store_row(b)
                led.end_pass(sp, b + (B + 2))
                sp.wait_ge(stored, 16 * (b + 1))
                sp.sem_inc(led.sems["res_free"], 1)
            store_row(B - 1)
            led.end_pass(sp, 2 * B + 1)
            sp.wait_ge(stored, 16 * B)

        @block.gpsimd
        def _(pool):
            with pool.Fori(0, B) as b:
                ph = Phase(led, "embed")
                pool.wait_ge(consts_in, CONST_DMAS)
                clear_upper(ph, pool)
                norm_pool(ph, pool, 1)
                ph.leave(pool)
                Phase(led, "attn0").leave(pool)
                ph = Phase(led, "mean0")
                norm_pool(ph, pool, 1)
                ph.leave(pool)
                led.end_pass(pool, b + 1)
            Phase(led, "route0").leave(pool)
            led.end_pass(pool, B + 1)
            with pool.Fori(0, B) as b:
                ph = Phase(led, "moe0")
                norm_pool(ph, pool, 1)
                norm_pool(ph, pool, 2)
                ph.leave(pool)
                ph = Phase(led, "qkv1")
                clear_upper(ph, pool)
                norm_pool(ph, pool, 1)
                ph.leave(pool)
                ph = Phase(led, "attn1")
                attn_pool(ph, pool, "attn1")
                ph.leave(pool)
                ph = Phase(led, "moe1")
                norm_pool(ph, pool, 1)
                ph.leave(pool)
                ph = Phase(led, "sim2")
                clear_upper(ph, pool)
                norm_pool(ph, pool, 1)
                norm_pool(ph, pool, 2, power=0.5)
                ph.leave(pool)
                Phase(led, "attn2").leave(pool)
                ph = Phase(led, "moe2")
                norm_pool(ph, pool, 1)
                ph.leave(pool)
                for half, name in enumerate(("rel3a", "rel3b")):
                    ph = Phase(led, name)
                    link = pool_chain(ph, pool)
                    if half == 0:
                        link(nc.gpsimd.memset(qup[0:D, :, S - 1:S], 0.0))
                        nc.gpsimd.memset(qup[D:P, :, :], 0.0).then_inc(*ph.mark("upper_cleared"))
                        pool.wait_ge(*ph.own("upper_cleared"))
                        norm_pool(ph, pool, 1)
                        norm_pool(ph, pool, 2)
                    for i in range(2 * NB):
                        s, j = i // NB, i % NB
                        c = 512 * j
                        pool.wait_ge(*ph.after("rot_ready", i + 1))
                        link(nc.gpsimd.tensor_tensor(qlo[0:D, s, c:c + 512], rt1[:, i % 2, :], rt2[:, i % 2, :], ALU.add))
                        o = 1 if j == 0 else 0
                        nc.gpsimd.tensor_tensor(qup[0:D, s, c - 1 + o:c + 511], rt1[:, i % 2, o:512], rt2[:, i % 2, o:512],
                                                ALU.add).then_inc(*ph.mark("rot_used"))
                        pool.wait_ge(*ph.own("rot_used"))
                    ph.leave(pool)
                    ph = Phase(led, "attn3" + "ab"[half])
                    attn_pool(ph, pool, "attn3" + "ab"[half])
                    ph.leave(pool)
                ph = Phase(led, "rope4")
                norm_pool(ph, pool, 1)
                norm_pool(ph, pool, 2)
                for i in range(2 * NB):
                    j = i // 2
                    dst = (qt, kt)[i % 2]
                    cols = slice(512 * j, 512 * (j + 1))
                    pool.wait_ge(*ph.after("rope_ready", i + 1))
                    nc.gpsimd.tensor_tensor(dst[:, cols], rp1[:, (i % 2) * 512:(i % 2) * 512 + 512],
                                            rp2[:, (i % 2) * 512:(i % 2) * 512 + 512], ALU.add).then_inc(*ph.mark("rope_used"))
                    pool.wait_ge(*ph.own("rope_used"))
                ph.leave(pool)
                ph = Phase(led, "attn4")
                attn_pool(ph, pool, "attn4")
                ph.leave(pool)
                ph = Phase(led, "moe4")
                norm_pool(ph, pool, 1)
                ph.leave(pool)
                led.end_pass(pool, b + (B + 2))

        @block.scalar
        def _(act):
            with act.Fori(0, B) as b:
                ph = Phase(led, "embed")
                qkv_act(ph, act)
                ph.leave(act)
                ph = Phase(led, "attn0")
                attn_act(ph, act, "attn0")
                ph.leave(act)
                Phase(led, "mean0").leave(act)
                led.end_pass(act, b + 1)
            ph = Phase(led, "route0")
            for n in (1, 2):
                act.wait_ge(*ph.after("exp_in", n))
                nc.scalar.activation(r0[:, 1, :, :], r0[:, 0, :, :], ACT.Exp).then_inc(*ph.mark("exp_out"))
            act.wait_ge(*ph.after("exp_in", 3))
            nc.scalar.activation(r0s[:, 3, :], r0s[:, 2, :], ACT.Exp).then_inc(*ph.mark("exp_out"))
            ph.leave(act)
            led.end_pass(act, B + 1)
            with act.Fori(0, B) as b:
                ph = Phase(led, "moe0")
                transpose_act(ph, act, xt, [0, 1, 2])
                for i in range(2 * NB):
                    k, j = i // NB, i % NB
                    act.wait_ge(*ph.after("hid_psum", i + 1))
                    nc.scalar.activation(hid[:, k, 512 * j:512 * (j + 1)], ps[:, 3 + i % 3, :], ACT.Gelu)\
                        .then_inc(*ph.mark("hid_ready"))
                ph.leave(act)
                ph = Phase(led, "qkv1")
                qkv_act(ph, act)
                ph.leave(act)
                ph = Phase(led, "attn1")
                attn_act(ph, act, "attn1")
                ph.leave(act)
                ph = Phase(led, "moe1")
                transpose_act(ph, act, xt, [0, 1, 2])
                transpose_act(ph, act, xt, [0, 1, 2], n0=NB)
                for j in range(NB):
                    act.wait_ge(*ph.after("hid_psum", j + 1))
                    nc.scalar.activation(hid[:, 0, 512 * j:512 * (j + 1)], ps[:, 5 + j, :], ACT.Relu)\
                        .then_inc(*ph.mark("hid_ready"))
                act.wait_ge(*ph.after("bias_ready", 1))
                for layer in range(2):
                    for j in range(NG // GPB):
                        act.wait_ge(*ph.after("expert_psum", layer * (NG // GPB) + j + 1))
                        for i in range(GPB):
                            g = GPB * j + i
                            ins = nc.scalar.activation(hid[:, 1 - layer, GRP * g:GRP * (g + 1)],
                                                       ps[:, 4 * layer + j, GRP * i:GRP * (i + 1)], ACT.Relu,
                                                       bias=bias1[:, layer, g:g + 1])
                        ins.then_inc(*ph.mark("expert_ready"))
                ph.leave(act)
                ph = Phase(led, "sim2")
                transpose_act(ph, act, xt, [0, 1, 2])
                transpose_act(ph, act, qt, [5, 6, 7], n0=NB)
                ph.leave(act)
                ph = Phase(led, "attn2")
                attn_act(ph, act, "attn2")
                ph.leave(act)
                ph = Phase(led, "moe2")
                transpose_act(ph, act, xt, [0, 1, 2])
                transpose_act(ph, act, xt2, [4, 5, 6], n0=NB, width=P)
                for i in range(NB * C2):
                    j, c = i // C2, i % C2
                    act.wait_ge(*ph.after("hid_psum", i + 1))
                    nc.scalar.activation(hid[:, c, 512 * j:512 * (j + 1)], ps[:, i % 4, :], ACT.Relu)\
                        .then_inc(*ph.mark("hid_ready"))
                ph.leave(act)
                for half, name in enumerate(("rel3a", "rel3b")):
                    ph = Phase(led, name)
                    if half == 0:
                        transpose_act(ph, act, xt, [0, 1, 2])
                        act.wait_ge(*ph.after("bias_ready", 1))
                    for i in range(2 * NB):
                        s, j = i // NB, i % NB
                        hd = 2 * half + s
                        bank, cols = 4 * (i % 2), slice(512 * j, 512 * (j + 1))
                        act.wait_ge(*ph.after("q_psum", i + 1))
                        if i >= 2:
                            act.wait_ge(*ph.after("rot_psum", i - 1))
                        nc.scalar.activation(qv[0:DH, i % 2, :], ps[0:DH, bank, :], ACT.Identity,
                                             bias=bias3[0:DH, hd:hd + 1], scale=0.125).then_inc(*ph.mark("qv_ready"))
                        if half == 0 and i == 0:
                            act.wait_ge(*ph.after("upper_cleared", 1))
                        for content in (qlo, qup):
                            ins = nc.scalar.activation(content[64:80, s, cols], ps[64:80, bank, :], ACT.Identity,
                                                       bias=bias3[64:80, hd:hd + 1], scale=0.125)
                        ins.then_inc(*ph.mark("content_ready"))
                    ph.leave(act)
                    ph = Phase(led, "attn3" + "ab"[half])
                    attn_act(ph, act, "attn3" + "ab"[half])
                    ph.leave(act)
                ph = Phase(led, "rope4")
                transpose_act(ph, act, xt, [0, 1, 2])
                transpose_act(ph, act, xt, [0, 1, 2], n0=NB)
                act.wait_ge(*ph.after("v_psum", 1))
                nc.scalar.copy(v[:, :, 0:32], ps[:, 3, 0:T * 32].rearrange("p (t d) -> p t d", d=32))
                ph.leave(act)
                ph = Phase(led, "attn4")
                attn_act(ph, act, "attn4")
                ph.leave(act)
                ph = Phase(led, "moe4")
                transpose_act(ph, act, xt, [0, 1, 2])
                transpose_act(ph, act, xt, [0, 1, 2], n0=NB)
                act.wait_ge(*ph.after("exp_in", 1))
                nc.scalar.activation(lg[:, 1, :], lg[:, 0, :], ACT.Exp).then_inc(*ph.mark("exp_out"))
                for i in range(NB * E3 * 2):
                    act.wait_ge(*ph.after("gate_psum", i + 1))
                    if i >= 2:
                        act.wait_ge(*ph.after("gated", i - 1))
                    nc.scalar.activation(sg[:, i % 2, :], ps[0:HC3, 2 * (i % 2), :], ACT.Silu).then_inc(*ph.mark("silu_ready"))
                ph.leave(act)
                led.end_pass(act, b + (B + 2))

        @block.tensor
        def _(pe):
            with pe.Fori(0, B) as b:
                ph = Phase(led, "embed")
                pe.wait_ge(consts_in, CONST_DMAS)
                pe.wait_ge(patches_in, 32 * (b + 1))
                for t in range(TP):
                    ins = nc.tensor.matmul(ps[:, 0, t * D:(t + 1) * D], xp[:, t * P:(t + 1) * P], K("tok_w"), start=True, stop=True)
                ins.then_inc(*ph.mark("emb_psum"))
                qkv_pe(ph, pe, "q0", "k0", "v0")
                ph.leave(pe)
                ph = Phase(led, "attn0")
                attn_pe(ph, pe, "attn0")
                ph.leave(pe)
                ph = Phase(led, "mean0")
                pe.wait_ge(*ph.after("normed", 1))
                for t in range(T):
                    ins = nc.tensor.matmul(ps[0:D, 0, 0:P], x[:, t, :], K("mean"), start=(t == 0), stop=(t == T - 1))
                ins.then_inc(*ph.mark("mean_psum"))
                pe.wait_ge(*ph.after("mean_ready", 1))
                nc.tensor.matmul(ps[:, 1, 0:E0], mean_t[:, :], W("wr0"), start=True, stop=True).then_inc(*ph.mark("logit_psum"))
                ph.leave(pe)
                led.end_pass(pe, b + 1)
            Phase(led, "route0").leave(pe)
            led.end_pass(pe, B + 1)
            with pe.Fori(0, B) as b:
                ph = Phase(led, "moe0")
                pe.wait_ge(*ph.after("normed", 1))
                transpose_pe(ph, x, [0, 1, 2])
                pe.wait_ge(*ph.after("weights_ready", 1))
                for i in range(2 * NB):
                    k, j = i // NB, i % NB
                    if k == 0:
                        pe.wait_ge(*ph.after("xt_copied", j + 1))
                    if i >= 3:
                        pe.wait_ge(*ph.after("hid_ready", i - 2))
                    nc.tensor.matmul(ps[:, 3 + i % 3, :], w1s[:, k, :], xt[:, 512 * j:512 * (j + 1)], start=True, stop=True)\
                        .then_inc(*ph.mark("hid_psum"))
                pe.wait_ge(*ph.after("hid_ready", 2 * NB))
                for t in range(T):
                    for k in range(2):
                        ins = nc.tensor.matmul(ps[:, 6 + t // 6, (t % 6) * D:(t % 6 + 1) * D], hid[:, k, t * P:(t + 1) * P],
                                               w2s[:, k, :], start=(k == 0), stop=(k == 1))
                    if t % 6 == 5:
                        ins.then_inc(*ph.mark("out_psum"))
                ph.leave(pe)
                ph = Phase(led, "qkv1")
                qkv_pe(ph, pe, "q1", "k1", "v1")
                ph.leave(pe)
                ph = Phase(led, "attn1")
                attn_pe(ph, pe, "attn1")
                ph.leave(pe)
                ph = Phase(led, "moe1")
                transpose_pe(ph, ctxt, [0, 1, 2])
                pe.wait_ge(*ph.after("xt_copied", NB))
                rows_pe(ph, W("proj1"), xt, [3, 4], "proj_psum")
                pe.wait_ge(*ph.after("normed", 1))
                transpose_pe(ph, x, [0, 1, 2])
                for j in range(NB):
                    pe.wait_ge(*ph.after("xt_copied", NB + j + 1))
                    nc.tensor.matmul(ps[:, 5 + j, :], W("wi1"), xt[:, 512 * j:512 * (j + 1)], start=True, stop=True)\
                        .then_inc(*ph.mark("hid_psum"))
                pe.wait_ge(*ph.after("bias_ready", 1))
                pe.wait_ge(weights_in, (b + 1) * (16 * 2 * NG))
                for layer in range(2):
                    if layer == 0:
                        pe.wait_ge(*ph.after("hid_ready", NB))
                    else:
                        pe.wait_ge(*ph.after("expert_ready", NG // GPB))
                    for j in range(NG // GPB):
                        bank = ps[:, 4 * layer + j, :]
                        w = GRP * GPB
                        nc.tensor.matmul(bank[:, 0:w], wsi[:, layer, :], hid[:, layer, w * j:w * (j + 1)], start=True, stop=False,
                                         skip_group_check=True)
                        for i in range(GPB):
                            g = GPB * j + i
                            ins = nc.tensor.matmul(bank[:, GRP * i:GRP * (i + 1)], rw[:, layer, g, 0:HID1],
                                                   hid[:, layer, GRP * g:GRP * (g + 1)], start=False, stop=(i == GPB - 1),
                                                   skip_group_check=True)
                        ins.then_inc(*ph.mark("expert_psum"))
                pe.wait_ge(*ph.after("expert_ready", 2 * (NG // GPB)))
                rows_pe(ph, W("wo1"), hid[:, 0, :], [0, 1], "out_psum")
                ph.leave(pe)
                ph = Phase(led, "sim2")
                pe.wait_ge(*ph.after("normed", 1))
                transpose_pe(ph, x, [0, 1, 2])
                pe.wait_ge(*ph.after("xt_copied", NB))
                rows_pe(ph, W("w2a"), xt, [3, 4], "v_psum")
                pe.wait_ge(*ph.after("normed", 2))
                transpose_pe(ph, y, [5, 6, 7])
                ph.leave(pe)
                ph = Phase(led, "attn2")
                attn_pe(ph, pe, "attn2")
                ph.leave(pe)
                ph = Phase(led, "moe2")
                pe.wait_ge(*ph.after("normed", 1))
                transpose_pe(ph, xa[:, :, 0:D], [0, 1, 2])
                pe.wait_ge(*ph.after("xt_copied", NB))
                for t in range(T):
                    ins = nc.tensor.matmul(ps[:, 3, t * E2:(t + 1) * E2], xt[:, t * P:(t + 1) * P], W("rw2"), start=True, stop=True)
                ins.then_inc(*ph.mark("logit_psum"))
                pe.wait_ge(*ph.after("normed", 2))
                transpose_pe(ph, xa, [4, 5, 6], width=P)
                for i in range(NB * C2):
                    j, c = i // C2, i % C2
                    if c == 0:
                        pe.wait_ge(*ph.after("xt_copied", NB + j + 1))
                    if i >= 4:
                        pe.wait_ge(*ph.after("hid_ready", i - 3))
                    nc.tensor.matmul(ps[:, i % 4, :], K("w1_2")[:, c * P:(c + 1) * P], xt2[:, 512 * j:512 * (j + 1)],
                                     start=True, stop=True).then_inc(*ph.mark("hid_psum"))
                pe.wait_ge(*ph.after("hid_ready", NB * C2))
                for t in range(T):
                    o = ps[:, 4 + t // 6, (t % 6) * D:(t % 6 + 1) * D]
                    for c in range(C2):
                        nc.tensor.matmul(o, hid[:, c, t * P:(t + 1) * P], K("w2_2")[:, c * D:(c + 1) * D], start=(c == 0), stop=False)
                    ins = nc.tensor.matmul(o, xt2[64:96, t * P:(t + 1) * P], K("b2_2")[64:96, :], start=False, stop=True)
                    if t % 6 == 5:
                        ins.then_inc(*ph.mark("out_psum"))
                ph.leave(pe)
                for half, name in enumerate(("rel3a", "rel3b")):
                    ph = Phase(led, name)
                    if half == 0:
                        pe.wait_ge(*ph.after("normed", 1))
                        transpose_pe(ph, x, [0, 1, 2])
                        pe.wait_ge(*ph.after("xt_copied", NB))
                        rows_pe(ph, W("v3"), xt, [6, 7], "v_psum")
                        pe.wait_ge(*ph.after("v_copied", 1))
                    def content(i):
                        s, j = i // NB, i % NB
                        hd = 2 * half + s
                        bank, cols = 4 * (i % 2), slice(512 * j, 512 * (j + 1))
                        if i >= 2:
                            pe.wait_ge(*ph.after("k_copied", i - 1))
                            pe.wait_ge(*ph.after("content_ready", i - 1))
                        nc.tensor.matmul(ps[0:80, bank, :], W("wq3")[:, 80 * hd:80 * hd + 80], xt[:, cols], start=True, stop=True)\
                            .then_inc(*ph.mark("q_psum"))
                        at = CONST_AT["wk3"][1] + DH * hd
                        nc.tensor.matmul(ps[0:80, bank + 1, :], cst[:, at - D:at + DH], xt[:, cols], start=True, stop=True)\
                            .then_inc(*ph.mark("k_psum"))

                    content(0)
                    for i in range(2 * NB):
                        hd, bank = 2 * half + i // NB, 4 * (i % 2)
                        if i + 1 < 2 * NB:
                            content(i + 1)
                        pe.wait_ge(*ph.after("qv_ready", i + 1))
                        if i >= 2:
                            pe.wait_ge(*ph.after("rot_ready", i - 1))
                        for r in range(2):
                            w = W("wpos3")[:, (2 * hd + r) * D:(2 * hd + r + 1) * D]
                            ins = nc.tensor.matmul(ps[0:D, bank + 2 + r, :], w, qv[:, i % 2, :], start=True, stop=True)
                        ins.then_inc(*ph.mark("rot_psum"))
                    ph.leave(pe)
                    ph = Phase(led, "attn3" + "ab"[half])
                    attn_pe(ph, pe, "attn3" + "ab"[half])
                    ph.leave(pe)
                ph = Phase(led, "rope4")
                transpose_pe(ph, ctxt, [0, 1, 2])
                pe.wait_ge(*ph.after("xt_copied", NB))
                rows_pe(ph, W("wout3"), xt, [3, 4], "proj_psum")
                pe.wait_ge(*ph.after("normed", 1))
                transpose_pe(ph, x, [0, 1, 2])
                pe.wait_ge(*ph.after("xt_copied", 2 * NB))
                for t in range(T):
                    ins = nc.tensor.matmul(ps[:, 3, t * 32:(t + 1) * 32], xt[:, t * P:(t + 1) * P], W("wv4"), start=True, stop=True)
                ins.then_inc(*ph.mark("v_psum"))
                for i in range(2 * NB):
                    j, w = i // 2, ("wq4", "wk4")[i % 2]
                    bank = 4 + 2 * (i % 2)
                    if i >= 2:
                        pe.wait_ge(*ph.after("rope_ready", i - 1))
                    for r in range(2):
                        ins = nc.tensor.matmul(ps[:, bank + r, :], W(w)[:, r * P:(r + 1) * P], xt[:, 512 * j:512 * (j + 1)],
                                               start=True, stop=True)
                    ins.then_inc(*ph.mark("rope_psum"))
                ph.leave(pe)
                ph = Phase(led, "attn4")
                attn_pe(ph, pe, "attn4")
                ph.leave(pe)
                ph = Phase(led, "moe4")
                transpose_pe(ph, ctxt, [0, 1, 2])
                pe.wait_ge(*ph.after("xt_copied", NB))
                rows_pe(ph, W("wo4"), xt, [3, 4], "proj_psum")
                pe.wait_ge(*ph.after("normed", 1))
                transpose_pe(ph, x, [0, 1, 2])
                pe.wait_ge(*ph.after("xt_copied", 2 * NB))
                for t in range(T):
                    ins = nc.tensor.matmul(ps[:, 3, t * E3:(t + 1) * E3], xt[:, t * P:(t + 1) * P], W("rt4"), start=True, stop=True)
                ins.then_inc(*ph.mark("logit_psum"))
                pe.wait_ge(*ph.after("exp_in", 1))
                pe.wait_ge(*ph.after("proj_read", 1))

                def down(n):
                    j, e = n // E3, n % E3
                    pe.wait_ge(*ph.after("gated", 2 * n + 2))
                    if e == 0 and j > 0:
                        pe.wait_ge(*ph.after("mixed", 4 * j))
                    for t in range(4):
                        for c in range(2):
                            ins = nc.tensor.matmul(ps[:, 4 + t, e * D:(e + 1) * D], hh[:, n % 2, c, t * P:(t + 1) * P],
                                                   K("w2_4")[:, (2 * e + c) * D:(2 * e + c + 1) * D], start=(c == 0), stop=(c == 1))
                    ins.then_inc(*ph.mark("down_psum"))

                for n in range(NB * E3):
                    j, e = n // E3, n % E3
                    for c in range(2):
                        i = 2 * n + c
                        if i >= 2:
                            pe.wait_ge(*ph.after("gated", i - 1))
                        w = slice((2 * e + c) * HC3, (2 * e + c + 1) * HC3)
                        xs = xt[:, 512 * j:512 * (j + 1)]
                        nc.tensor.matmul(ps[0:HC3, 2 * (i % 2), :], W("w1_4")[:, w], xs, start=True, stop=True)\
                            .then_inc(*ph.mark("gate_psum"))
                        nc.tensor.matmul(ps[0:HC3, 2 * (i % 2) + 1, :], W("w3_4")[:, w], xs, start=True, stop=True)\
                            .then_inc(*ph.mark("up_psum"))
                    if n > 0:
                        down(n - 1)
                down(NB * E3 - 1)
                ph.leave(pe)
                led.end_pass(pe, b + (B + 2))

        @block.vector
        def _(dve):
            dve.wait_ge(consts_in, CONST_DMAS)
            for layer in range(2):
                nc.vector.tensor_tensor(wsi[:, layer, :], wsi[:, layer, :], ident, ALU.add)
            for rows in (xt[D:P, :], mean_t[D:P, :], w1s[D:P, :, :], klo[D:P, :, :], kup[D:P, :, :], qz[:, :, :, :]):
                nc.vector.memset(rows, 0.0)
            nc.vector.drain()
            nc.vector.memset(xt[D:D + 1, :], 1.0)
            nc.vector.memset(mean_t[D:D + 1, :], 1.0)
            with dve.Fori(0, B) as b:
                ph = Phase(led, "embed")
                link = chain(ph, dve)
                dve.wait_ge(patches_in, 32 * (b + 1))
                nc.vector.tensor_copy(h[:, TP:T, :], txt_in)
                dve.wait_ge(*ph.after("emb_psum", 1))
                link(nc.vector.tensor_tensor(h[:, 0:TP, :].rearrange("p t d -> p (t d)"), ps[:, 0, :], K("pos"), ALU.add))
                norm_vec(ph, dve, h[:, :, :], x[:, :, :], 1)
                ready_vec(ph, dve)
                qkv_vec(ph, dve, 1.0)
                ph.leave(dve)
                ph = Phase(led, "attn0")
                attn_vec(ph, dve, "attn0", add_to_h)
                ph.leave(dve)
                ph = Phase(led, "mean0")
                link = chain(ph, dve)
                norm_vec(ph, dve, h[:, :, :], x[:, :, :], 1)
                ready_vec(ph, dve)
                nc.vector.tensor_copy(hall[:, bass.ds(b, 1), :], h[:, :, :].rearrange("p t d -> p (t d)").unsqueeze(1))
                dve.wait_ge(*ph.after("mean_psum", 1))
                nc.vector.tensor_copy(mean_t[0:D, :], ps[0:D, 0, 0:P]).then_inc(*ph.mark("mean_ready"))
                dve.wait_ge(*ph.after("logit_psum", 1))
                nc.vector.tensor_copy(lg0[:, bass.ds(b, 1), :], ps[:, 1, 0:E0].unsqueeze(1))
                ph.leave(dve)
                led.end_pass(dve, b + 1)

            ph = Phase(led, "route0")
            link = chain(ph, dve)
            shape = [P, B, E0]
            src = lg0[:, :, :]
            for n in (1, 2):
                link(nc.vector.tensor_reduce(r0s[:, 0, :], src, AX.X, ALU.max))
                nc.vector.tensor_tensor(r0[:, 0, :, :], src, bc(r0s[:, 0, :], shape), ALU.subtract).then_inc(*ph.mark("exp_in"))
                dve.wait_ge(*ph.after("exp_out", n))
                link(nc.vector.tensor_reduce(r0s[:, 0, :], r0[:, 1, :, :], AX.X, ALU.add))
                link(nc.vector.reciprocal(r0s[:, 1, :], r0s[:, 0, :]))
                link(nc.vector.tensor_tensor(r0[:, 2, :, :], r0[:, 1, :, :], bc(r0s[:, 1, :], shape), ALU.mult))
                if n == 1:
                    load = r0[:, 3, 0, :]
                    link(nc.vector.tensor_reduce(load, r0[:, 2, :, :].rearrange("p b e -> p e b"), AX.X, ALU.add))
                    link(nc.vector.tensor_scalar(load, load, float(S), None, ALU.mult))
                    link(nc.vector.reciprocal(r0[:, 3, 1, :], load))
                    link(nc.vector.tensor_scalar(r0[:, 3, 1, :], r0[:, 3, 1, :], CAP0, 1.0, ALU.mult, ALU.min))
                    link(nc.vector.tensor_tensor(r0[:, 4, :, :], r0[:, 2, :, :],
                                                 r0[:, 3, 1, :].unsqueeze(1).to_broadcast(shape), ALU.mult))
                    src = r0[:, 4, :, :]
            iota = K("iota8").unsqueeze(1).to_broadcast(shape)
            oh1, oh2 = oh0[:, :, 0:E0], oh0[:, :, E0:2 * E0]
            top2_onehots(link, r0[:, 2, :, :], oh1, oh2, r0[:, 5, :, :], r0s[:, 0, :], iota, shape)
            for k, oh in enumerate((oh1, oh2)):
                link(nc.vector.tensor_tensor(r0[:, 6, :, :], oh, r0[:, 2, :, :], ALU.mult))
                link(nc.vector.tensor_reduce(r0s[:, 4 + k, :], r0[:, 6, :, :], AX.X, ALU.add))
            nc.vector.tensor_tensor(r0s[:, 2, :], r0s[:, 5, :], r0s[:, 4, :], ALU.subtract).then_inc(*ph.mark("exp_in"))
            dve.wait_ge(*ph.after("exp_out", 3))
            link(nc.vector.tensor_scalar(r0s[:, 4, :], r0s[:, 3, :], 1.0, None, ALU.add))
            link(nc.vector.reciprocal(r0s[:, 5, :], r0s[:, 4, :]))
            link(nc.vector.tensor_tensor(r0s[:, 6, :], r0s[:, 3, :], r0s[:, 5, :], ALU.mult))
            for k, oh in enumerate((oh1, oh2)):
                link(nc.vector.tensor_tensor(wt0[:, :, k * E0:(k + 1) * E0], oh, bc(r0s[:, 5 + k, :], shape), ALU.mult))
            ph.leave(dve)
            led.end_pass(dve, B + 1)

            with dve.Fori(0, B) as b:
                ph = Phase(led, "moe0")
                link = chain(ph, dve)
                nc.vector.tensor_copy(ohb[:, :].unsqueeze(1), oh0[:, bass.ds(b, 1), :])
                nc.vector.tensor_copy(wtb[:, :].unsqueeze(1), wt0[:, bass.ds(b, 1), :])
                link(nc.vector.tensor_copy(h[:, :, :].rearrange("p t d -> p (t d)").unsqueeze(1), hall[:, bass.ds(b, 1), :]))
                norm_vec(ph, dve, h[:, :, :], x[:, :, :], 1)
                ready_vec(ph, dve)
                for k in range(2):
                    sel = big[0:65, 0:E0 * F0].rearrange("p (f e) -> p f e", e=E0)
                    link(nc.vector.tensor_tensor(sel, K("w1_0").rearrange("p (e f) -> p f e", e=E0),
                                                 ohb[0:65, k * E0:(k + 1) * E0].unsqueeze(1).to_broadcast([65, F0, E0]), ALU.mult))
                    link(nc.vector.tensor_reduce(w1s[0:65, k, :], sel, AX.X, ALU.add))
                    for table, dst in (("w2_0", w2s), ("b2_0", b2s)):
                        sel = big[:, 0:E0 * D].rearrange("p (f e) -> p f e", e=E0)
                        link(nc.vector.tensor_tensor(sel, K(table).rearrange("p (e f) -> p f e", e=E0),
                                                     wtb[:, k * E0:(k + 1) * E0].unsqueeze(1).to_broadcast([P, D, E0]), ALU.mult))
                        link(nc.vector.tensor_reduce(dst[:, k, :], sel, AX.X, ALU.add))
                nc.vector.tensor_tensor(b2s[:, 0, :], b2s[:, 0, :], b2s[:, 1, :], ALU.add).then_inc(*ph.mark("weights_ready"))
                dve.wait_ge(*ph.own("weights_ready"))
                for i in range(2):
                    dve.wait_ge(*ph.after("out_psum", i + 1))
                    link(nc.vector.tensor_tensor(y[:, 6 * i:6 * i + 6, :], rows_bank([6, 7], i), x[:, 6 * i:6 * i + 6, :], ALU.add))
                link(nc.vector.tensor_tensor(y[:, :, :], y[:, :, :], per_token(b2s[:, 0, :]), ALU.add))
                norm_vec(ph, dve, y[:, :, :], x[:, :, :], 2)
                link(nc.vector.tensor_tensor(x[:, :, :], x[:, :, :], per_token(K("gamma0")), ALU.mult))
                link(nc.vector.tensor_tensor(x[:, :, :], x[:, :, :], per_token(K("beta0")), ALU.add))
                link(nc.vector.tensor_tensor(h[:, :, :], h[:, :, :], x[:, :, :], ALU.add))
                ph.leave(dve)

                ph = Phase(led, "qkv1")
                norm_vec(ph, dve, h[:, :, :], x[:, :, :], 1)
                ready_vec(ph, dve)
                qkv_vec(ph, dve, float(32 ** -0.5))
                ph.leave(dve)
                ph = Phase(led, "attn1")
                attn_vec(ph, dve, "attn1", to_ctxt(32))
                ph.leave(dve)

                ph = Phase(led, "moe1")
                link = chain(ph, dve)
                dve.wait_ge(weights_in, (b + 1) * (16 * 2 * NG))
                for layer in range(2):
                    ins = nc.vector.tensor_scalar(bias1[:, layer, :], rw[:, layer, :, HID1], K("bs1")[:, layer:layer + 1], None, ALU.add)
                ins.then_inc(*ph.mark("bias_ready"))
                for i in range(2):
                    dve.wait_ge(*ph.after("proj_psum", i + 1))
                    link(nc.vector.tensor_tensor(h[:, 6 * i:6 * i + 6, :], rows_bank([3, 4], i), h[:, 6 * i:6 * i + 6, :], ALU.add))
                norm_vec(ph, dve, h[:, :, :], x[:, :, :], 1)
                ready_vec(ph, dve)
                link(nc.vector.tensor_tensor(h[:, :, :], h[:, :, :], per_token(K("bo1")), ALU.add))
                for i in range(2):
                    dve.wait_ge(*ph.after("out_psum", i + 1))
                    nc.vector.tensor_tensor(h[:, 6 * i:6 * i + 6, :], rows_bank([0, 1], i), h[:, 6 * i:6 * i + 6, :], ALU.add)
                ph.leave(dve)

                ph = Phase(led, "sim2")
                link = chain(ph, dve)
                norm_vec(ph, dve, h[:, :, :], x[:, :, :], 1)
                ready_vec(ph, dve)
                link(nc.vector.tensor_tensor(sq[:, :, :], x[:, :, :], x[:, :, :], ALU.mult))
                nc.vector.tensor_reduce(st[:, 3, :], sq[:, :, :], AX.X, ALU.add).then_inc(*ph.mark("var_ready"))
                dve.wait_ge(*ph.after("rstd_ready", 2))
                link(nc.vector.tensor_scalar(st[:, 5, :], st[:, 4, :], 1e-12, None, ALU.max))
                link(nc.vector.reciprocal(st[:, 6, :], st[:, 5, :]))
                link(nc.vector.tensor_tensor(y[:, :, :], x[:, :, :], bc(st[:, 6, :], [P, T, D]), ALU.mult))
                ready_vec(ph, dve)
                for i in range(2):
                    dve.wait_ge(*ph.after("v_psum", i + 1))
                    nc.vector.tensor_copy(v[:, 6 * i:6 * i + 6, :], rows_bank([3, 4], i))
                for j in range(NB):
                    dve.wait_ge(*ph.after("xt_copied", NB + j + 1))
                    nc.vector.tensor_copy(kt[0:D, 512 * j:512 * (j + 1)], qt[0:D, 512 * j:512 * (j + 1)])
                ph.leave(dve)
                ph = Phase(led, "attn2")
                attn_vec(ph, dve, "attn2", add_to_h)
                ph.leave(dve)

                ph = Phase(led, "moe2")
                link = chain(ph, dve)
                norm_vec(ph, dve, h[:, :, :], xa[:, :, 0:D], 1)
                ready_vec(ph, dve)
                dve.wait_ge(*ph.after("logit_psum", 1))
                logits = ps[:, 3, 0:T * E2].rearrange("p (t e) -> p t e", e=E2)
                oh = xa[:, :, D:D + E2]
                iota = K("iota32").unsqueeze(1).to_broadcast([P, T, E2])
                top2_onehots(link, logits, oh, None, None, st[:, 7, :], iota, [P, T, E2])
                link(nc.vector.tensor_scalar(xa[:, :, D + E2:P], oh, -1.0, None, ALU.add))
                ready_vec(ph, dve)
                for i in range(2):
                    dve.wait_ge(*ph.after("out_psum", i + 1))
                    nc.vector.scalar_tensor_tensor(h[:, 6 * i:6 * i + 6, :], rows_bank([4, 5], i), 0.0, h[:, 6 * i:6 * i + 6, :],
                                                   ALU.max, ALU.add)
                ph.leave(dve)

                for half, name in enumerate(("rel3a", "rel3b")):
                    ph = Phase(led, name)
                    link = chain(ph, dve)
                    if half == 0:
                        link(nc.vector.tensor_tensor(bias3[:, :], K("bq3"), K("uv3"), ALU.add))
                        nc.vector.tensor_scalar(bias3[:, :], bias3[:, :], 0.125, None, ALU.mult).then_inc(*ph.mark("bias_ready"))
                        norm_vec(ph, dve, h[:, :, :], x[:, :, :], 1)
                        norm_vec(ph, dve, x[:, :, :], y[:, :, :], 2)
                        link(nc.vector.tensor_tensor(y[:, :, :], y[:, :, :], per_token(K("gamma3")), ALU.mult))
                        link(nc.vector.tensor_tensor(x[:, :, :], y[:, :, :], per_token(K("beta3")), ALU.add))
                        ready_vec(ph, dve)
                        for i in range(2):
                            dve.wait_ge(*ph.after("v_psum", i + 1))
                            ins = nc.vector.tensor_copy(v[:, 6 * i:6 * i + 6, :], rows_bank([6, 7], i))
                        ins.then_inc(*ph.mark("v_copied"))
                    for i in range(2 * NB):
                        s, j = i // NB, i % NB
                        bank, cols = 4 * (i % 2), slice(512 * j, 512 * (j + 1))
                        dve.wait_ge(*ph.after("k_psum", i + 1))
                        if i >= 2:
                            dve.wait_ge(*ph.after("rot_used", i - 1))
                        for keys in (klo, kup):
                            ins = nc.vector.tensor_copy(keys[64:80, s, cols], ps[64:80, bank + 1, :])
                        ins.then_inc(*ph.mark("k_copied"))
                        dve.wait_ge(*ph.after("rot_psum", i + 1))
                        nc.vector.tensor_tensor(rt1[:, i % 2, :], ps[0:D, bank + 2, :], K("rot_c")[:, cols], ALU.mult)
                        nc.vector.tensor_tensor(rt2[:, i % 2, :], ps[0:D, bank + 3, :], K("rot_s")[:, cols], ALU.mult)\
                            .then_inc(*ph.mark("rot_ready"))
                    ph.leave(dve)
                    ph = Phase(led, "attn3" + "ab"[half])
                    attn_vec(ph, dve, "attn3" + "ab"[half], to_ctxt(DH))
                    ph.leave(dve)

                ph = Phase(led, "rope4")
                link = chain(ph, dve)
                for i in range(2):
                    dve.wait_ge(*ph.after("proj_psum", i + 1))
                    link(nc.vector.tensor_tensor(h[:, 6 * i:6 * i + 6, :], rows_bank([3, 4], i), h[:, 6 * i:6 * i + 6, :], ALU.add))
                norm_vec(ph, dve, h[:, :, :], y[:, :, :], 1)
                norm_vec(ph, dve, y[:, :, :], x[:, :, :], 2, centre=False, eps=RMS_EPS)
                link(nc.vector.tensor_tensor(x[:, :, :], x[:, :, :], per_token(K("rms1")), ALU.mult))
                ready_vec(ph, dve)
                for i in range(2 * NB):
                    j = i // 2
                    bank, o, cols = 4 + 2 * (i % 2), (i % 2) * 512, slice(512 * j, 512 * (j + 1))
                    dve.wait_ge(*ph.after("rope_psum", i + 1))
                    if i >= 2:
                        dve.wait_ge(*ph.after("rope_used", i - 1))
                    nc.vector.tensor_tensor(rp1[:, o:o + 512], ps[:, bank, :], K("rope_c")[:, cols], ALU.mult)
                    nc.vector.tensor_tensor(rp2[:, o:o + 512], ps[:, bank + 1, :], K("rope_s")[:, cols], ALU.mult)\
                        .then_inc(*ph.mark("rope_ready"))
                ph.leave(dve)
                ph = Phase(led, "attn4")
                attn_vec(ph, dve, "attn4", to_ctxt(DH))
                ph.leave(dve)

                ph = Phase(led, "moe4")
                link = chain(ph, dve)
                for i in range(2):
                    dve.wait_ge(*ph.after("proj_psum", i + 1))
                    ins = nc.vector.tensor_tensor(y[:, 6 * i:6 * i + 6, :], rows_bank([3, 4], i), y[:, 6 * i:6 * i + 6, :], ALU.add)
                ins.then_inc(*ph.mark("proj_read"))
                dve.wait_ge(*ph.own("proj_read"))
                norm_vec(ph, dve, y[:, :, :], x[:, :, :], 1, centre=False, eps=RMS_EPS)
                link(nc.vector.tensor_tensor(x[:, :, :], x[:, :, :], per_token(K("rms2")), ALU.mult))
                ready_vec(ph, dve)
                link(nc.vector.tensor_tensor(y[:, :, :], y[:, :, :], h[:, :, :], ALU.add))
                dve.wait_ge(*ph.after("logit_psum", 1))
                shape = [P, T, E3]
                L = [lg[:, i, :].rearrange("p (t e) -> p t e", e=E3) for i in range(5)]
                logits = ps[:, 3, 0:T * E3].rearrange("p (t e) -> p t e", e=E3)
                link(nc.vector.tensor_reduce(st[:, 7, :], logits, AX.X, ALU.max))
                nc.vector.tensor_tensor(L[0], logits, bc(st[:, 7, :], shape), ALU.subtract).then_inc(*ph.mark("exp_in"))
                dve.wait_ge(*ph.after("exp_out", 1))
                link(nc.vector.tensor_reduce(st[:, 7, :], L[1], AX.X, ALU.add))
                link(nc.vector.reciprocal(st[:, 8, :], st[:, 7, :]))
                link(nc.vector.tensor_tensor(L[1], L[1], bc(st[:, 8, :], shape), ALU.mult))
                iota = K("iota8").unsqueeze(1).to_broadcast(shape)
                top2_onehots(link, L[1], L[2], L[3], L[4], st[:, 7, :], iota, shape)
                link(nc.vector.tensor_tensor(L[2], L[2], L[3], ALU.add))
                link(nc.vector.tensor_tensor(L[2], L[2], L[1], ALU.mult))
                link(nc.vector.tensor_reduce(st[:, 7, :], L[2], AX.X, ALU.add))
                link(nc.vector.tensor_scalar(st[:, 8, :], st[:, 7, :], 1e-9, None, ALU.add))
                link(nc.vector.reciprocal(st[:, 9, :], st[:, 8, :]))
                link(nc.vector.tensor_tensor(wt4[:, :, :], L[2], bc(st[:, 9, :], shape), ALU.mult))
                dve.wait_ge(led.sems["res_free"], 1)
                for n in range(NB * E3):
                    j, e = n // E3, n % E3
                    for c in range(2):
                        i = 2 * n + c
                        dve.wait_ge(*ph.after("silu_ready", i + 1))
                        dve.wait_ge(*ph.after("up_psum", i + 1))
                        if n >= 2:
                            dve.wait_ge(*ph.after("down_psum", n - 1))
                        nc.vector.tensor_tensor(hh[:, n % 2, c, :], sg[:, i % 2, :], ps[0:HC3, 2 * (i % 2) + 1, :], ALU.mult)\
                            .then_inc(*ph.mark("gated"))
                    if e == E3 - 1:
                        dve.wait_ge(*ph.after("down_psum", n + 1))
                        for t in range(4):
                            tt = 4 * j + t
                            link(nc.vector.tensor_tensor(moe_w.rearrange("p (e d) -> p e d", e=E3),
                                                         ps[:, 4 + t, :].rearrange("p (e d) -> p e d", e=E3),
                                                         bc(wt4[:, tt, :], [P, E3, D]), ALU.mult))
                            link(nc.vector.tensor_reduce(sq[:, tt, :], moe_w.rearrange("p (e d) -> p d e", e=E3), AX.X, ALU.add))
                            nc.vector.tensor_tensor(res[:, tt, :], sq[:, tt, :], y[:, tt, :], ALU.add).then_inc(*ph.mark("mixed"))
                ph.leave(dve)
                led.end_pass(dve, b + (B + 2))

        return led



def _tables():
    c = {}
    i = np.arange(P)
    c["ident"] = np.eye(P)
    c["mask_low"] = (i[None, :] <= i[:, None]).astype(np.int32)
    c["mask_line"] = (np.arange(P + 1)[None, :] == i[:, None] + 1).astype(np.int32)
    c["mask_future"] = (i[None, :] > i[:, None]).astype(np.int32)
    c["neg"] = np.full((P, 1), NEG)
    c["mean"] = np.full((P, P), 1.0 / S)
    c["half"] = np.repeat(np.array([[-0.5] * T + [0.5] * T]), P, 0)
    c["iota8"] = np.repeat(np.arange(8, 0, -1)[None].astype(float), P, 0)
    c["iota32"] = np.repeat(np.arange(32, 0, -1)[None].astype(float), P, 0)
    w = np.exp(np.arange(0, D, 2) * (-np.log(10000.0) / D))
    m = np.arange(S)

    def pe(pos):
        t = np.zeros((D, len(pos)))
        t[0::2], t[1::2] = np.sin(w[:, None] * pos), np.cos(w[:, None] * pos)
        return t
    a = -(m + 1.0)
    c["rot_c"] = np.repeat(np.cos(w[:, None] * a), 2, 0)
    s = np.sin(w[:, None] * a)
    c["rot_s"] = np.stack([-s, s], 1).reshape(D, S)
    inv = 1.0 / 10000.0 ** (np.arange(0, DH, 2) / DH)
    f = np.outer(np.concatenate([inv, inv]), m)
    c["rope_c"], c["rope_s"] = np.zeros((P, S)), np.zeros((P, S))
    for hd in range(HEADS):
        c["rope_c"][32 * hd:32 * hd + DH] = np.cos(f)
        c["rope_s"][32 * hd:32 * hd + DH] = np.sin(f) * np.where(np.arange(DH) < DH // 2, -1.0, 1.0)[:, None]
    return c, pe(m + S).astype(np.float32), pe(m).astype(np.float32)


def _layout(a):
    c, pe_low, pe_up = _tables()

    def aug(w, bias):
        return np.concatenate([w.T, bias[None, :]], 0)

    def rep(vec):
        return np.repeat(vec.reshape(1, -1), P, 0)
    c["tok_w"] = aug(a["L0_tok_W"], a["L0_tok_b"])
    c["pos"] = a["L0_tok_pos_embed"][0].reshape(TP, P, D).transpose(1, 0, 2).reshape(P, TP * D)
    for n in "qkv":
        c[n + "0"] = aug(a["L0_attn_W" + n], a["L0_attn_b" + n])
    c["wr0"] = np.concatenate([a["L0_ffn_Wr"], a["L0_ffn_br"][None]], 0)
    c["w1_0"] = np.concatenate([a["L0_ffn_W1"], a["L0_ffn_b1"][:, None, :]], 1).transpose(1, 0, 2).reshape(65, E0 * F0)
    c["w2_0"] = a["L0_ffn_W2"].transpose(1, 0, 2).reshape(P, E0 * D)
    c["b2_0"] = rep(a["L0_ffn_b2"])
    c["gamma0"], c["beta0"] = rep(a["L0_ffn_gamma"]), rep(a["L0_ffn_beta"])
    wq, bq = a["L1_attn_w_qkv"].reshape(2, 3, 32, D), a["L1_attn_b_qkv"].reshape(2, 3, 32)
    for i, n in enumerate("qkv"):
        c[n + "1"] = aug(wq[:, i].reshape(D, D), bq[:, i].reshape(D))
    c["proj1"] = aug(a["L1_attn_w_proj"], a["L1_attn_b_proj"])
    c["wi1"] = aug(a["L1_ffn_Wi"], a["L1_ffn_bi"])
    c["ws1"] = a["L1_ffn_Ws"][:, 0].transpose(2, 0, 1).reshape(P, 2 * HID1)
    c["bs1"] = a["L1_ffn_bs"][:, 0].T
    c["wo1"], c["bo1"] = a["L1_ffn_Wo"].T, rep(a["L1_ffn_bo"])
    c["w2a"] = aug(a["L2_attn_W"], a["L2_attn_b"])
    c["rw2"] = aug(a["L2_ffn_router_w"], a["L2_ffn_router_b"])
    c["w1_2"] = np.zeros((P, E2 * H2), np.float32)
    c["w1_2"][0:D] = a["L2_ffn_W1"].transpose(1, 0, 2).reshape(D, E2 * H2)
    for e in range(E2):
        c["w1_2"][D + e, H2 * e:H2 * (e + 1)] = a["L2_ffn_b1"][e]
        c["w1_2"][D + E2 + e, H2 * e:H2 * (e + 1)] = BIG
    c["w2_2"] = a["L2_ffn_W2"].reshape(C2, P, D).transpose(1, 0, 2).reshape(P, C2 * D)
    c["b2_2"] = np.zeros((P, D), np.float32)
    c["b2_2"][D:D + E2] = a["L2_ffn_b2"]
    c["gamma3"], c["beta3"] = rep(a["L3_attn_ln_gamma"]), rep(a["L3_attn_ln_beta"])
    c["wq3"], c["bq3"], c["uv3"] = np.zeros((D, HEADS, 80), np.float32), np.zeros((80, HEADS), np.float32), np.zeros((80, HEADS), np.float32)
    for hd in range(HEADS):
        sl = slice(DH * hd, DH * hd + DH)
        for r in (0, 64):
            c["wq3"][:, hd, r:r + DH] = a["L3_attn_Wq"][:, sl]
            c["bq3"][r:r + DH, hd] = a["L3_attn_bq"][sl]
        c["uv3"][0:DH, hd] = a["L3_attn_v_bias"][hd]
        c["uv3"][64:80, hd] = a["L3_attn_u_bias"][hd]
    c["wq3"] = c["wq3"].reshape(D, HEADS * 80)
    c["wk3"] = np.concatenate([a["L3_attn_Wk"], a["L3_attn_bk"][None]], 0)
    c["v3"] = np.concatenate([a["L3_attn_Wv"], a["L3_attn_bv"][None]], 0)
    swap = np.arange(D) ^ 1
    wp = a["L3_attn_Wpos"].reshape(D, HEADS, DH).transpose(2, 1, 0)
    c["wpos3"] = np.stack([wp, wp[:, :, swap]], 2).reshape(DH, HEADS * 2 * D)
    c["wout3"] = np.concatenate([a["L3_attn_Wout"], a["L3_attn_bout"][None]], 0)
    c["rms1"], c["rms2"] = rep(a["L3_ffn_ln1_w"]), rep(a["L3_ffn_ln2_w"])
    turned = np.concatenate([np.arange(DH // 2, DH), np.arange(DH // 2)])
    for n, kv in (("wq", HEADS), ("wk", 2)):
        w = a["L3_ffn_" + n].reshape(kv, DH, D)
        w = np.repeat(w, HEADS // kv, 0)
        z = np.zeros((2, HEADS, 32, D), np.float32)
        z[0, :, 0:DH], z[1, :, 0:DH] = w, w[:, turned]
        c[n + "4"] = z.reshape(2 * P, D).T
    c["wv4"], c["wo4"] = a["L3_ffn_wv"].T, a["L3_ffn_wo"].T
    c["rt4"] = a["L3_ffn_router_w"].T
    for n in (1, 3):
        c[f"w{n}_4"] = a[f"L3_ffn_w{n}"].reshape(E3 * 2 * HC3, D).T
    c["w2_4"] = a["L3_ffn_w2"].reshape(E3, D, 2, HC3).transpose(3, 0, 2, 1).reshape(HC3, E3 * 2 * D)

    pack = np.zeros((P, CONST_COLS), np.float32)
    for name, (rows, at, cols) in CONST_AT.items():
        assert c[name].shape == (rows, cols), (name, c[name].shape)
        part = c[name]
        pack[0:rows, at:at + cols] = part.view(np.float32) if part.dtype == np.int32 else part
    x = a["x"][:, 0].reshape(B, P // 8, 8, 512 // 8, 8).transpose(0, 2, 4, 1, 3).reshape(B, D, NP_)
    patches = np.concatenate([x, np.ones((B, 1, NP_), np.float32)], 1)
    w_route = np.concatenate([a["L1_ffn_Wr"].transpose(0, 1, 3, 2), a["L1_ffn_br"][..., None]], 3)
    return {"consts": pack, "patches": patches, "txt": a["txt"], "route": a["L1_ffn_route_id"].reshape(1, B * NG),
            "w_route": w_route, "pe_low": pe_low, "pe_up": pe_up}


def kernel(**inputs):
    import numpy as _np
    import concourse.bacc as _bacc
    from concourse import mybir as _mybir
    from concourse.bass_utils import run_bass_kernel_spmd as _run

    arrays = _layout({k: _np.asarray(a) for k, a in inputs.items()})
    arrays = {f"in_{k}": _np.ascontiguousarray(a) for k, a in arrays.items()}
    nc = _bacc.Bacc("TRN2", target_bir_lowering=False, num_devices=1)
    args = {k[3:]: nc.dram_tensor(k, a.shape, _mybir.dt.from_np(a.dtype), kind="ExternalInput").ap() for k, a in arrays.items()}
    out = nc.dram_tensor("out_dram", (B, S, D), F32, kind="ExternalOutput").ap()
    build(nc, out=out, **args)
    r = _run(nc, [arrays], core_ids=[0])
    return r.results[0]["out_dram"]
```

```python
import concourse.bass as bass
from concourse import mybir
from contextlib import ExitStack
import numpy as np

F32 = mybir.dt.float32
I32 = mybir.dt.int32
F32R = mybir.dt.float32r
ALU = mybir.AluOpType
ACT = mybir.ActivationFunctionType
AX = mybir.AxisListType

B, D, P = 4, 64, 128
NP_, NT = 1024, 512
S = NP_ + NT
T = S // P
TP = NP_ // P
NB = S // 512
E0, F0 = 8, 128
E1, HID1, GRP = 16, 128, 96
NG = S // GRP
GPB = 4
E2, H2 = 32, 16
C2 = E2 * H2 // P
HEADS, DH = 4, 16
E3, HC3 = 8, 85
TOPK = 64
CHUNKS, PER_CHUNK = 16, 16
CAND_OPS = 3 * CHUNKS
BIG = float(2.0 ** 100)
NEG = -4e30
LN_EPS, RMS_EPS = 1e-5, 1e-6
CAP0 = float(-(-(B * S * 5 // 4) // E0))

ENGINES = 4

SIGNALS = {
    "embed": {"pool_step": 1, "rstd_ready": 2, "xt_copied": 3, "emb_psum": 1, "xt_psum": 3, "q_psum": 3, "k_psum": 3,
        "v_psum": 2, "vec_step": 13, "var_ready": 2, "normed": 1},
    "attn0": {"probs_ready": 12, "pt_by_act": 24, "scores_ready": 12, "pt_psum": 36, "ctx_ready": 12,
        "max_ready": 12, "pt_by_vec": 12, "vec_step": 12, "ctx_copied": 12},
    "mean0": {"rstd_ready": 2, "mean_psum": 1, "logit_psum": 1, "vec_step": 12, "var_ready": 2, "normed": 1,
        "mean_ready": 1},
    "route0": {"exp_out": 3, "vec_step": 33, "exp_in": 3},
    "moe0": {"rstd_ready": 4, "xt_copied": 3, "hid_ready": 6, "xt_psum": 3, "hid_psum": 6, "out_psum": 2,
        "vec_step": 43, "var_ready": 4, "normed": 1, "weights_ready": 1},
    "qkv1": {"weights_spread": 4, "rstd_ready": 2, "xt_copied": 3, "high_ready": 12, "xt_psum": 3, "stack_psum": 12,
        "v_psum": 2, "vec_step": 12, "var_ready": 2, "normed": 1, "low_ready": 12},
    "attn1": {"probs_ready": 24, "pt_by_act": 48, "scores_ready": 24, "pt_psum": 72, "ctx_ready": 24,
        "max_ready": 24, "pt_by_vec": 24, "vec_step": 24, "ctx_copied": 24},
    "moe1": {"rstd_ready": 2, "xt_copied": 6, "hid_ready": 3, "expert_ready": 8, "xt_psum": 6, "proj_psum": 2,
        "hid_psum": 3, "expert_psum": 8, "out_psum": 2, "bias_ready": 1, "vec_step": 15, "var_ready": 2, "normed": 1},
    "sim2": {"pool_step": 1, "rstd_ready": 3, "xt_copied": 6, "xt_psum": 6, "v_psum": 2, "vec_step": 16,
        "var_ready": 3, "normed": 2},
    "attn2": {"row_copied": 12, "probs_ready": 12, "pt_by_act": 36, "scores_ready": 12, "unsure_summed": 12,
        "pt_psum": 36, "ctx_ready": 12, "cand_step": 576, "vec_step": 264, "unsure_ready": 12, "sparse_ready": 12,
        "ctx_copied": 12},
    "moe2": {"rstd_ready": 2, "xt_copied": 6, "hid_ready": 12, "xt_psum": 6, "logit_psum": 1, "hid_psum": 12,
        "out_psum": 2, "vec_step": 18, "var_ready": 2, "normed": 2},
    "rel3a": {"pool_step": 7, "upper_cleared": 1, "rstd_ready": 4, "rot_used": 6, "xt_copied": 3, "qv_ready": 6,
        "content_ready": 6, "xt_psum": 3, "v_psum": 2, "q_psum": 6, "k_psum": 6, "rot_psum": 6, "vec_step": 27,
        "bias_ready": 1, "var_ready": 4, "normed": 1, "v_copied": 1, "k_copied": 6, "rot_ready": 6},
    "attn3a": {"queries_alone": 24, "probs_ready": 24, "pt_by_act": 48, "scores_ready": 24, "side_ready": 24,
        "pt_psum": 72, "ctx_ready": 24, "vec_step": 48, "side_read": 24, "max_ready": 24, "pt_by_vec": 24,
        "ctx_copied": 24},
    "rel3b": {"pool_step": 6, "rot_used": 6, "qv_ready": 6, "content_ready": 6, "q_psum": 6, "k_psum": 6,
        "rot_psum": 6, "k_copied": 6, "rot_ready": 6},
    "attn3b": {"queries_alone": 24, "probs_ready": 24, "pt_by_act": 48, "scores_ready": 24, "side_ready": 24,
        "pt_psum": 72, "ctx_ready": 24, "vec_step": 48, "side_read": 24, "max_ready": 24, "pt_by_vec": 24,
        "ctx_copied": 24},
    "rope4": {"rstd_ready": 4, "rope_used": 6, "xt_copied": 6, "xt_psum": 6, "proj_psum": 2, "v_psum": 1,
        "rope_psum": 6, "vec_step": 21, "var_ready": 4, "normed": 1, "rope_ready": 6},
    "attn4": {"queries_alone": 48, "probs_ready": 48, "pt_by_act": 48, "scores_ready": 48, "pt_psum": 96,
        "ctx_ready": 48, "vec_step": 144, "max_ready": 48, "ctx_copied": 48, "pt_by_vec": 48},
    "moe4": {"rstd_ready": 2, "xt_copied": 6, "high_ready": 3, "exp_out": 1, "silu_ready": 48, "xt_psum": 6,
        "proj_psum": 2, "logit_psum": 1, "gate_psum": 48, "up_psum": 48, "down_psum": 24, "proj_read": 1,
        "vec_step": 54, "var_ready": 2, "normed": 1, "low_ready": 3, "exp_in": 1, "gated": 48, "mixed": 12},
}


def const_layout():
    return [
        ("ident", P, P), ("mask_low", P, P), ("mask_line", P, P + 1), ("mask_future", P, P), ("neg", P, 1),
        ("mean", P, P), ("half", P, 2 * T), ("iota8", P, 8), ("iota32", P, 32),
        ("tok_w", 65, D), ("pos", P, TP * D),
        ("q0", 65, D), ("k0", 65, D), ("v0", 65, D),
        ("wr0", 65, E0), ("w1_0", 65, E0 * F0), ("w2_0", P, E0 * D), ("b2_0", P, E0 * D), ("gamma0", P, D), ("beta0", P, D),
        ("q1", 65, D), ("k1", 65, D), ("v1", 65, D), ("proj1", 65, D),
        ("wi1", 65, HID1), ("ws1", P, 2 * HID1), ("bs1", P, 2), ("wo1", P, D), ("bo1", P, D),
        ("w2a", 65, D), ("rw2", 65, E2), ("w1_2", P, C2 * P), ("w2_2", P, C2 * D), ("b2_2", P, D),
        ("gamma3", P, D), ("beta3", P, D), ("wq3", 64, HEADS * 80), ("bq3", 80, HEADS), ("uv3", 80, HEADS),
        ("v3", 65, D), ("wk3", 65, HEADS * DH), ("wpos3", DH, HEADS * 2 * D), ("wout3", 65, D),
        ("rot_c", 64, S), ("rot_s", 64, S),
        ("rms1", P, D), ("rms2", P, D), ("wq4", 64, 2 * P), ("wk4", 64, 2 * P), ("wv4", 64, 32), ("wo4", 64, D),
        ("rope_c", P, S), ("rope_s", P, S),
        ("rt4", 64, E3), ("w2_4", HC3, E3 * 2 * D), ("w1_4", P, E3 * 2 * HC3), ("w3_4", P, E3 * 2 * HC3),
    ]


CONST_AT = {}
_at = 0
for _name, _rows, _cols in const_layout():
    CONST_AT[_name] = (_rows, _at, _cols)
    _at += _cols
CONST_COLS = _at
EXPERT_AT = CONST_AT["w1_4"][1]


class Ledger:

    def __init__(self, nc, ctx):
        self.nc, self.seen = nc, {}
        names = ["phase_left", "res_free"] + sorted({n for p in SIGNALS.values() for n in p})
        self.sems = {n: ctx.enter_context(nc.semaphore(n)) for n in names}
        self.pass_ended, self.pass_opened, self.turn = (ctx.enter_context(nc.semaphore(n))
                                                        for n in ("pass_ended", "pass_opened", "turn"))

    def phases(self, phase):
        return [p for p in PLAN if phase in p][0]

    def before(self, phase, name):
        phases = self.phases(phase)
        return sum(SIGNALS[p].get(name, 0) for p in phases[:phases.index(phase)])

    def ended(self, phase):
        return (self.phases(phase).index(phase) + 1) * ENGINES

    def end_pass(self, eng, passes):
        eng.drain().then_inc(self.pass_ended, 1)
        if eng is self.nc.gpsimd:
            eng.wait_ge(self.pass_ended, passes * (ENGINES + 1))
            eng.sem_inc(self.turn, 1)
            nums = sorted(s.num for s in self.sems.values())
            assert nums == list(range(nums[0], nums[0] + len(nums)))
            eng.sem_clear(range(nums[0], nums[0] + len(nums)))
            eng.drain().then_inc(self.pass_opened, 1)
        else:
            eng.wait_ge(self.pass_opened, passes)
            eng.sem_inc(self.turn, 1)


class Phase:

    def __init__(self, ledger, name):
        self.led, self.name, self.mine = ledger, name, {}

    def mark(self, name):
        self.mine[name] = self.mine.get(name, 0) + 1
        seen = self.led.seen.setdefault(self.name, {})
        seen[name] = seen.get(name, 0) + 1
        return self.led.sems[name], 1

    def after(self, name, k):
        return self.led.sems[name], self.led.before(self.name, name) + k

    def own(self, name):
        return self.after(name, self.mine[name])

    def leave(self, eng):
        eng.drain().then_inc(self.led.sems["phase_left"], 1)
        eng.wait_ge(self.led.sems["phase_left"], self.led.ended(self.name))


PLAN = [
    ["embed", "attn0", "mean0"],
    ["route0"],
    ["moe0", "qkv1", "attn1", "moe1", "sim2", "attn2", "moe2", "rel3a", "attn3a", "rel3b", "attn3b",
     "rope4", "attn4", "moe4"],
]


def units_of(kind):
    heads = {"attn0": [0], "attn1": [0, 1], "attn2": [0], "attn3a": [0, 1], "attn3b": [2, 3], "attn4": [0, 1, 2, 3]}[kind]
    return [(h, q) for h in heads for q in range(T)]


def build(nc, consts, patches, txt, route, w_route, pe_low, pe_up, out):
    with ExitStack() as ctx:
        def sb(name, shape, dt=F32):
            return ctx.enter_context(nc.sbuf_tensor(name, shape, dt))

        cst = sb("cst", [P, EXPERT_AT])
        with nc.sbuf_tensor("experts_in", [P, CONST_COLS - EXPERT_AT], F32) as experts_in:
            pass
        experts = sb("experts", [P, CONST_COLS - EXPERT_AT])
        h = sb("h", [P, T, D])
        x = sb("x", [P, T, D])
        y = sb("y", [P, T, D])
        sq = sb("sq", [P, T, D])
        ctxt = sb("ctxt", [P, T, D])
        res = sb("res", [P, T, D])
        v = sb("v", [P, T, D])
        hall = sb("hall", [P, B, T * D])
        xt = sb("xt", [P, S])
        with nc.sbuf_tensor("qlo", [P, 2, S], F32) as qlo, nc.sbuf_tensor("qup", [P, 2, S], F32) as qup:
            pass
        q_stack = sb("q_stack", [P, 2, S])
        k_stack = sb("k_stack", [P, 2, S])
        x_high, x_low = q_stack[:, 0, :], q_stack[:, 1, :]
        klo = sb("klo", [P, 2, S])
        kup = sb("kup", [P, 2, S])
        big = sb("big", [P, 4 * S])
        rw = sb("rw", [P, 2, NG, HID1 + 1])
        st = sb("st", [P, 16, T])
        negmax = sb("negmax", [P, 48])
        rowsum = sb("rowsum", [P, 48])
        qz = sb("qz", [P, HEADS, 2, P])
        rinv = sb("rinv", [P, 48])
        lg0 = sb("lg0", [P, B, E0])
        r0 = sb("r0", [P, 8, B, E0])
        r0s = sb("r0s", [P, 8, B])
        oh0 = sb("oh0", [P, B, 2 * E0])
        wt0 = sb("wt0", [P, B, 2 * E0])
        ohb = sb("ohb", [P, 2 * E0])
        wtb = sb("wtb", [P, 2 * E0])
        mean_t = sb("mean_t", [P, P])
        w1s = sb("w1s", [P, 2, F0])
        w2s = sb("w2s", [P, 2, D])
        b2s = sb("b2s", [P, 2, D])
        bias1 = sb("bias1", [P, 2, NG])
        bias3 = sb("bias3", [80, HEADS])
        lg = sb("lg", [P, 5, T * E3])
        wt4 = sb("wt4", [P, T, E3])
        route_sb = sb("route_sb", [1, B * NG], I32)
        ps = ctx.enter_context(nc.psum_tensor("ps", [P, 8, 512], F32))

        xp = qup[0:65, 0, 0:NP_]
        txt_in = qup[:, 1, 0:(T - TP) * D].rearrange("p (t d) -> p t d", d=D)
        prob = big[:, 0:2 * S].rearrange("p (s n) -> p s n", s=2)
        pt = big[:, 2 * S:4 * S].rearrange("p (s g n) -> p s g n", s=2, g=NB)
        hid = big[:, :].rearrange("p (c n) -> p c n", c=4)
        xt2 = qup[:, 0, :]
        xa = big[:, 0:S].rearrange("p (t n) -> p t n", n=P)
        work = qup[:, 0, :]
        spread = big[:, 0:4 * P].rearrange("p (w h r d) -> p w h r d", w=2, h=2, r=4)
        row_copy = (big[:, S:2 * S], big[:, 3 * S:4 * S])
        sparse = qup[:, 1, :]
        qt = qlo[:, 0, :]
        kt = qlo[:, 1, :]
        qv = big[:, 0:2 * 512].rearrange("p (s n) -> p s n", s=2)
        rt1 = big[0:D, 1024:2048].rearrange("p (s n) -> p s n", s=2)
        rt2 = big[0:D, 2048:3072].rearrange("p (s n) -> p s n", s=2)
        rp1 = big[:, 0:S]
        rp2 = big[:, S:2 * S]
        sg = big[0:HC3, 0:1024].rearrange("p (s n) -> p s n", s=2)
        hh = big[0:HC3, 1024:1024 + 2048].rearrange("p (s c n) -> p s c n", s=2, c=2)
        moe_w = big[:, 4096:4096 + 512]
        xx = big[:, 4608:4608 + T * P].rearrange("p (t r d) -> p t r d", r=2, d=D)

        def K(name):
            rows, at, cols = CONST_AT[name]
            return cst[0:rows, at:at + cols]

        def W(name):
            _, at, cols = CONST_AT[name]
            return cst[:, at:at + cols]

        ident = K("ident")
        wsi = K("ws1").rearrange("p (l n) -> p l n", l=2)
        spare = ctxt[:, :, :].rearrange("p t d -> p (t d)")
        n_cand = CHUNKS * PER_CHUNK
        cand_left = spare[:, n_cand:2 * n_cand]
        cand = [x[:, :, :].rearrange("p t d -> p (t d)")[:, k * n_cand:(k + 1) * n_cand] for k in range(2)]
        top8 = spare[:, 2 * n_cand:2 * n_cand + TOPK + 8].rearrange("p (r e) -> p r e", e=8)
        limit = spare[:, 2 * n_cand + TOPK + 8:2 * n_cand + TOPK + 9]
        unsure = spare[:, 2 * n_cand + TOPK + 9:2 * n_cand + TOPK + 10]
        unsure_any = spare[0:1, 2 * n_cand + TOPK + 10:2 * n_cand + TOPK + 11].bitcast(I32)
        led = Ledger(nc, ctx)

        def dsem(name):
            return ctx.enter_context(nc.semaphore(name))

        consts_in = dsem("consts_in")
        patches_in = dsem("patches_in")
        route_in = dsem("route_in")
        weights_in = dsem("weights_in")
        stored = dsem("stored")
        CONST_DMAS = 16 * 7


        def chain(ph, eng):
            def link(ins):
                ins.then_inc(*ph.mark("vec_step"))
                eng.wait_ge(*ph.own("vec_step"))
            return link

        def pool_chain(ph, pool):
            def link(ins):
                ins.then_inc(*ph.mark("pool_step"))
                pool.wait_ge(*ph.own("pool_step"))
            return link

        def bc(ap, shape):
            return ap.unsqueeze(2).to_broadcast(shape)

        def per_token(ap):
            return ap.unsqueeze(1).to_broadcast([P, T, D])

        def norm_vec(ph, dve, src, dst, n, centre=True, eps=LN_EPS):
            done = [0, 0]
            tiles_of = [slice(0, T // 2), slice(T // 2, T)]

            def in_turn(step):
                for k, t in enumerate(tiles_of):
                    if done[k]:
                        dve.wait_ge(*ph.after("vec_step", done[k]))
                    step(t).then_inc(*ph.mark("vec_step"))
                    done[k] = ph.mine["vec_step"]

            def each(ap, t):
                return bc(ap[:, t], [P, T // 2, D])

            xc = src
            if centre:
                in_turn(lambda t: nc.vector.tensor_reduce(st[:, 0, t], src[:, t, :], AX.X, ALU.add))
                in_turn(lambda t: nc.vector.tensor_scalar(st[:, 1, t], st[:, 0, t], -1.0 / D, None, ALU.mult))
                in_turn(lambda t: nc.vector.tensor_tensor(dst[:, t, :], src[:, t, :], each(st[:, 1, :], t), ALU.add))
                xc = dst
            in_turn(lambda t: nc.vector.tensor_tensor(sq[:, t, :], xc[:, t, :], xc[:, t, :], ALU.mult))
            in_turn(lambda t: nc.vector.tensor_reduce(st[:, 2, t], sq[:, t, :], AX.X, ALU.add))
            for k, t in enumerate(tiles_of):
                dve.wait_ge(*ph.after("vec_step", done[k]))
                nc.vector.tensor_scalar(st[:, 3, t], st[:, 2, t], 1.0 / D, eps, ALU.mult, ALU.add)\
                    .then_inc(*ph.mark("var_ready"))
            for k, t in enumerate(tiles_of):
                dve.wait_ge(*ph.after("rstd_ready", 2 * n - 1 + k))
                nc.vector.tensor_tensor(dst[:, t, :], xc[:, t, :], each(st[:, 4, :], t), ALU.mult)\
                    .then_inc(*ph.mark("vec_step"))
            dve.wait_ge(*ph.own("vec_step"))

        def norm_pool(ph, pool, n):
            for k, t in enumerate((slice(0, T // 2), slice(T // 2, T))):
                pool.wait_ge(*ph.after("var_ready", 2 * n - 1 + k))
                nc.gpsimd.tensor_tensor(st[:, 4, t], st[:, 3, t], K("half")[:, t], ALU.pow).then_inc(*ph.mark("rstd_ready"))
                pool.wait_ge(*ph.own("rstd_ready"))

        def clear_upper(ph, pool):
            nc.gpsimd.memset(qlo[D:P, :, :], 0.0).then_inc(*ph.mark("pool_step"))
            pool.wait_ge(*ph.own("pool_step"))

        def ready_vec(ph, dve, name="normed"):
            nc.vector.tensor_copy(st[:, 15, 0:1], st[:, 4, 0:1]).then_inc(*ph.mark(name))

        def transpose_pe(ph, src, banks, width=D):
            for t in range(T):
                ins = nc.tensor.transpose(ps[0:width, banks[t // 4], (t % 4) * P:(t % 4 + 1) * P], src[:, t, :], ident)
                if t % 4 == 3:
                    ins.then_inc(*ph.mark("xt_psum"))

        def transpose_act(ph, act, dst, banks, n0=0, width=D):
            for j in range(NB):
                act.wait_ge(*ph.after("xt_psum", n0 + j + 1))
                nc.scalar.copy(dst[0:width, 512 * j:512 * (j + 1)], ps[0:width, banks[j], :]).then_inc(*ph.mark("xt_copied"))

        def rows_pe(ph, w, src, banks, name, n=D):
            for t in range(T):
                ins = nc.tensor.matmul(ps[:, banks[t // 6], (t % 6) * n:(t % 6 + 1) * n], src[:, t * P:(t + 1) * P], w,
                                       start=True, stop=True)
                if t % 6 == 5:
                    ins.then_inc(*ph.mark(name))

        def rows_bank(banks, i, n=D):
            return ps[:, banks[i], 0:6 * n].rearrange("p (t d) -> p t d", d=n)

        def qkv_pe(ph, pe, wq, wk, wv):
            pe.wait_ge(*ph.after("normed", 1))
            transpose_pe(ph, x, [0, 1, 2])
            for j in range(NB):
                pe.wait_ge(*ph.after("xt_copied", j + 1))
                nc.tensor.matmul(ps[0:D, 3 + j, :], W(wq), xt[:, 512 * j:512 * (j + 1)], start=True, stop=True)\
                    .then_inc(*ph.mark("q_psum"))
            for j in range(NB):
                nc.tensor.matmul(ps[0:D, (6 + j) % 8, :], W(wk), xt[:, 512 * j:512 * (j + 1)], start=True, stop=True)\
                    .then_inc(*ph.mark("k_psum"))
            rows_pe(ph, W(wv), xt, [1, 2], "v_psum")

        def qkv_act(ph, act):
            transpose_act(ph, act, xt, [0, 1, 2])
            for j in range(NB):
                act.wait_ge(*ph.after("k_psum", j + 1))
                nc.scalar.copy(kt[0:D, 512 * j:512 * (j + 1)], ps[0:D, (6 + j) % 8, :])

        def qkv_vec(ph, dve, scale):
            for j in range(NB):
                dve.wait_ge(*ph.after("q_psum", j + 1))
                nc.vector.tensor_scalar(qt[0:D, 512 * j:512 * (j + 1)], ps[0:D, 3 + j, :], scale, None, ALU.mult)
            for i in range(2):
                dve.wait_ge(*ph.after("v_psum", i + 1))
                nc.vector.tensor_copy(v[:, 6 * i:6 * i + 6, :], rows_bank([1, 2], i))

        def stack_blocks():
            return [(hd, j, w) for hd in range(2) for j in range(NB) for w in range(2)]

        def stack_pool(ph, pool):
            for w, name in enumerate(("q1", "k1")):
                for hd in range(2):
                    nc.gpsimd.tensor_copy(spread[:, w, hd, :, :],
                                          W(name)[:, 32 * hd:32 * hd + 32].unsqueeze(1).to_broadcast([P, 4, 32]))\
                        .then_inc(*ph.mark("weights_spread"))
                    pool.wait_ge(*ph.own("weights_spread"))

        def stack_pe(ph, pe):
            pe.wait_ge(*ph.after("normed", 1))
            transpose_pe(ph, x, [0, 1, 2])
            pe.wait_ge(*ph.after("weights_spread", 4))
            for i, (hd, j, w) in enumerate(stack_blocks()):
                if i < 2 * NB:
                    pe.wait_ge(*ph.after("xt_copied", j + 1))
                if i >= 5:
                    pe.wait_ge(*ph.after("low_ready", i - 4))
                nc.tensor.matmul(ps[:, 3 + i % 5, :], spread[:, w, hd, :, :].rearrange("p r d -> p (r d)"),
                                 xt[:, 512 * j:512 * (j + 1)], start=True, stop=True).then_inc(*ph.mark("stack_psum"))
                if i == 2 * NB - 1:
                    rows_pe(ph, W("v1"), xt, [1, 2], "v_psum")

        def stack_act(ph, act):
            transpose_act(ph, act, xt, [0, 1, 2])
            for i, (hd, j, w) in enumerate(stack_blocks()):
                act.wait_ge(*ph.after("stack_psum", i + 1))
                nc.scalar.activation((q_stack, k_stack)[w][:, hd, 512 * j:512 * (j + 1)].bitcast(F32R), ps[:, 3 + i % 5, :],
                                     ACT.Identity, scale=(float(32 ** -0.5), 1.0)[w]).then_inc(*ph.mark("high_ready"))

        def stack_vec(ph, dve):
            for i, (hd, j, w) in enumerate(stack_blocks()):
                dve.wait_ge(*ph.after("high_ready", i + 1))
                for a, b in (((64, 128),), ((32, 64), (96, 128)))[w]:
                    part = (q_stack, k_stack)[w][a:b, hd, 512 * j:512 * (j + 1)]
                    ins = nc.vector.scalar_tensor_tensor(part.bitcast(F32R), ps[a:b, 3 + i % 5, :],
                                                         (float(32 ** -0.5), 1.0)[w], part, ALU.mult, ALU.subtract)
                ins.then_inc(*ph.mark("low_ready"))
            for i in range(2):
                dve.wait_ge(*ph.after("v_psum", i + 1))
                nc.vector.tensor_copy(v[:, 6 * i:6 * i + 6, :], rows_bank([1, 2], i))


        def tiles(kind, q):
            return q + 1 if kind == "attn4" else T

        def groups(kind, q):
            return -(-tiles(kind, q) // 4)

        def before_groups(kind, u):
            return sum(groups(kind, q) for _, q in units_of(kind)[:u])

        def slot_of(kind, u):
            return 0 if kind == "attn2" else u % 2

        def early(kind):
            return kind in ("attn0", "attn1")

        def copier(kind, g):
            return "pt_by_vec" if kind != "attn2" and (g == 1 or (g == 2 and kind == "attn4")) else "pt_by_act"

        def copied(kind, u, g):
            name = copier(kind, g)
            last = sum(copier(kind, i) == name for i in range(g + 1))
            return name, last + sum(copier(kind, i) == name for _, q in units_of(kind)[:u] for i in range(groups(kind, q)))

        def context_of(kind, hd):
            w, at = {"attn0": (D, 0), "attn1": (32, 32 * hd), "attn2": (D, 0), "attn4": (DH, DH * (hd // 2))}.get(
                kind, (DH, DH * hd))
            return ps[:, 7, 448 + at:448 + at + w]

        def alone(kind):
            return kind == "attn4" or kind.startswith("attn3")

        def head_rows(kind, hd):
            return (2, slice(64, 80)) if kind.startswith("attn3") else (hd, slice(32 * hd, 32 * hd + 32))

        def attn_pool(ph, pool, kind):
            link = pool_chain(ph, pool)
            for u, (hd, q) in enumerate(units_of(kind)):
                slot, rows = head_rows(kind, hd)
                if u >= 2:
                    pool.wait_ge(*ph.after("side_ready" if kind.startswith("attn3") else "scores_ready", u - 1))
                src = qlo[rows, hd % 2, :] if kind.startswith("attn3") else qt[rows, :]
                nc.gpsimd.tensor_copy(qz[rows, slot, u % 2, :], src[:, q * P:(q + 1) * P]).then_inc(*ph.mark("queries_alone"))
                pool.wait_ge(*ph.own("queries_alone"))

        def attn_pe(ph, pe, kind):
            units = units_of(kind)

            def scores(u, j):
                hd, q = units[u]
                if u >= len(units) or 4 * j >= tiles(kind, q):
                    return
                if j == 0 and u >= 2:
                    pe.wait_ge(*ph.after("row_copied" if kind == "attn2" else "probs_ready", u - 1))
                bank = ps[:, 3 * (u % 2) + j, :]
                lo, hi = 4 * j, min(4 * j + 4, tiles(kind, q))
                qs = slice(q * P, (q + 1) * P)
                if kind.startswith("attn3"):
                    s = hd % 2
                    cut = min(max(q, lo), hi)
                    parts = [(lo, cut, qlo, klo), (cut, hi, qup, kup)]
                    parts = [(a, b, qq, kk) for a, b, qq, kk in parts if a < b]
                    for a, b, qq, kk in parts:
                        ins = nc.tensor.matmul(bank[:, (a - lo) * P:(b - lo) * P], qq[:, s, qs], kk[:, s, a * P:b * P],
                                               start=True, stop=True)
                elif kind == "attn1":
                    ins = nc.tensor.matmul(bank, q_stack[:, hd, qs].bitcast(F32R), k_stack[:, hd, lo * P:hi * P].bitcast(F32R),
                                           start=True, stop=True)
                else:
                    qq = qt[:, qs]
                    if alone(kind):
                        pe.wait_ge(*ph.after("queries_alone", u + 1))
                        qq = qz[:, hd, u % 2, :]
                    ins = nc.tensor.matmul(bank[:, 0:(hi - lo) * P], qq, kt[:, lo * P:hi * P], start=True, stop=True)
                if hi == tiles(kind, q):
                    ins.then_inc(*ph.mark("scores_ready"))

            def side(u):
                hd, q = units[u]
                s = hd % 2
                if u >= 2:
                    pe.wait_ge(*ph.after("ctx_copied", u - 1))
                qs = slice(q * P, (q + 1) * P)
                n = min(P + 1, S - q * P)
                nc.tensor.matmul(ps[:, 7, 0:P], qlo[:, s, qs], klo[:, s, qs], start=True, stop=True)
                pe.wait_ge(*ph.after("queries_alone", u + 1))
                nc.tensor.matmul(ps[:, 7, P:P + n], qz[:, 2, u % 2, :], klo[:, s, q * P:q * P + n], start=True, stop=True)\
                    .then_inc(*ph.mark("side_ready"))

            def turn(u, g):
                if g == 0:
                    pe.wait_ge(*ph.after("probs_ready", u + 1))
                if g > 0:
                    pe.wait_ge(*ph.after(*copied(kind, u, g - 1)))
                elif u > 0:
                    pe.wait_ge(*ph.after(*copied(kind, u - 1, groups(kind, units[u - 1][1]) - 1)))
                n = min(4, tiles(kind, units[u][1]) - 4 * g)
                for i in range(n):
                    ins = nc.tensor.transpose(ps[:, 6, i * P:(i + 1) * P], prob[:, slot_of(kind, u), (4 * g + i) * P:(4 * g + i + 1) * P],
                                              ident)
                ins.then_inc(*ph.mark("pt_psum"))

            def context(u, g):
                hd, q = units[u]
                pe.wait_ge(*ph.after(*copied(kind, u, g)))
                if g == 0:
                    if u > 0:
                        pe.wait_ge(*ph.after("ctx_copied", u))
                    if kind.startswith("attn3") and u + 1 < len(units):
                        pe.wait_ge(*ph.after("side_read", u + 2))
                n = tiles(kind, q)
                for i in range(4 * g, min(4 * g + 4, n)):
                    ins = nc.tensor.matmul(ps[:, 7, 448:448 + D], pt[:, slot_of(kind, u), g, (i % 4) * P:(i % 4 + 1) * P],
                                           v[:, i, :], start=(i == 0), stop=(i == n - 1))
                if g == groups(kind, q) - 1:
                    ins.then_inc(*ph.mark("ctx_ready"))

            for u in (0, 1):
                for j in range(NB):
                    scores(u, j)
            if kind.startswith("attn3"):
                side(0)
            for u in range(len(units)):
                more = groups(kind, units[u][1])
                ahead = u + 2 < len(units)
                if kind == "attn2":
                    for j in range(NB if ahead else 0):
                        scores(u + 2, j)
                    ahead = False
                    pe.wait_ge(*ph.after("unsure_ready", u + 1))
                    nc.tensor.matmul(ps[:, 7, 0:1], K("mean"), unsure, start=True, stop=True).then_inc(*ph.mark("unsure_summed"))
                turn(u, 0)
                if ahead:
                    scores(u + 2, 0)
                if kind.startswith("attn3") and u + 1 < len(units):
                    if u == 0:
                        pe.wait_ge(*ph.after("side_read", 1))
                    else:
                        pe.wait_ge(*ph.after("ctx_copied", u))
                    side(u + 1)
                if more > 1:
                    turn(u, 1)
                context(u, 0)
                if ahead:
                    scores(u + 2, 1)
                if more > 2:
                    turn(u, 2)
                if more > 1:
                    context(u, 1)
                if ahead:
                    scores(u + 2, 2)
                if more > 2:
                    context(u, 2)

        def copy_group(ph, eng, kind, u, g, copy):
            q = units_of(kind)[u][1]
            n = min(4, tiles(kind, q) - 4 * g) * P
            eng.wait_ge(*ph.after("pt_psum", before_groups(kind, u) + g + 1))
            if u >= 2 or (u == 1 and kind == "attn2"):
                eng.wait_ge(*ph.after("ctx_ready", u if kind == "attn2" else u - 1))
            copy(pt[:, slot_of(kind, u), g, 0:n], ps[:, 6, 0:n]).then_inc(*ph.mark(copier(kind, g)))

        def attn_act(ph, act, kind):
            units = units_of(kind)

            def exps(u):
                q = units[u][1]
                n = tiles(kind, q) * P
                if kind == "attn2":
                    act.wait_ge(*ph.after("sparse_ready", u + 1))
                    src, bias = sparse, 0.0
                else:
                    act.wait_ge(*ph.after("max_ready", u + 1))
                    src = ps[:, 3 * (u % 2):3 * (u % 2) + NB, :].rearrange("p b n -> p (b n)")[:, 0:n]
                    bias = negmax[:, u:u + 1]
                if kind == "attn2" and u >= 1:
                    act.wait_ge(*ph.after("pt_psum", before_groups(kind, u)))
                elif u >= 2:
                    act.wait_ge(*ph.after("pt_psum", before_groups(kind, u - 1)))
                scale = 0.25 if kind == "attn4" else 1.0
                nc.scalar.activation(prob[:, slot_of(kind, u), 0:n], src, ACT.Exp, bias=bias, scale=scale,
                                     accum_out=rowsum[:, u:u + 1]).then_inc(*ph.mark("probs_ready"))

            def copy_row(u):
                act.wait_ge(*ph.after("scores_ready", u + 1))
                if u >= 2:
                    act.wait_ge(*ph.after("sparse_ready", u - 1))
                nc.scalar.copy(row_copy[u % 2], ps[:, 3 * (u % 2):3 * (u % 2) + NB, :].rearrange("p b n -> p (b n)"))\
                    .then_inc(*ph.mark("row_copied"))

            if kind == "attn2":
                copy_row(0)
                copy_row(1)
            else:
                exps(0)
            for u in range(len(units)):
                if kind == "attn2":
                    if u + 2 < len(units):
                        copy_row(u + 2)
                    exps(u)
                for g in range(groups(kind, units[u][1])):
                    if copier(kind, g) == "pt_by_act":
                        copy_group(ph, act, kind, u, g, nc.scalar.copy)
                    if g == 0 and u + 1 < len(units) and kind != "attn2" and not kind.startswith("attn3"):
                        exps(u + 1)
                if u + 1 < len(units) and kind.startswith("attn3"):
                    exps(u + 1)

        def attn_vec(ph, dve, kind, dest):
            units = units_of(kind)
            link = chain(ph, dve)

            def candidates(u, i):
                r, c = divmod(i, CHUNKS)
                row_c = row_copy[u % 2].rearrange("p (n c) -> p c n", c=CHUNKS)[:, c, :]
                work_c = work.rearrange("p (n c) -> p c n", c=CHUNKS)[:, c, :]
                best = cand[u % 2].rearrange("p (c k) -> p c k", c=CHUNKS)[:, c, :]
                if i >= CHUNKS:
                    dve.wait_ge(*ph.after("cand_step", CAND_OPS * u + i - CHUNKS + 1))
                if r == 0:
                    ins = nc.vector.max(best[:, 0:8], row_c)
                elif r == 1:
                    ins = nc.vector.match_replace(work_c, best[:, 0:8], row_c, -4.0)
                else:
                    ins = nc.vector.max(best[:, 8:16], work_c)
                ins.then_inc(*ph.mark("cand_step"))

            def place_side(u):
                hd, q = units[u]
                flat = ps[:, 3 * (u % 2):3 * (u % 2) + NB, :].rearrange("p b n -> p (b n)")
                dve.wait_ge(*ph.after("scores_ready", u + 1))
                dve.wait_ge(*ph.after("side_ready", u + 1))
                m = min(P + 1, S - q * P)
                link(nc.vector.copy_predicated(flat[:, q * P:(q + 1) * P], K("mask_low").bitcast(I32), ps[:, 7, 0:P]))
                ins = nc.vector.copy_predicated(flat[:, q * P:q * P + m], K("mask_line")[:, 0:m].bitcast(I32),
                                                ps[:, 7, P:P + m])
                ins.then_inc(*ph.mark("side_read"))
                dve.wait_ge(*ph.own("side_read"))

            def maxima(u):
                hd, q = units[u]
                n = tiles(kind, q) * P
                flat = ps[:, 3 * (u % 2):3 * (u % 2) + NB, :].rearrange("p b n -> p (b n)")
                if kind != "attn2":
                    dve.wait_ge(*ph.after("scores_ready", u + 1))
                if kind == "attn4":
                    link(nc.vector.copy_predicated(flat[:, q * P:(q + 1) * P], K("mask_future").bitcast(I32),
                                                   K("neg").to_broadcast([P, P])))
                if kind == "attn2":
                    row, cand_c = row_copy[u % 2], cand[u % 2].rearrange("p (c k) -> p c k", c=CHUNKS)
                    ahead = u + 1 < len(units)

                    def beside(step):
                        if ahead and step == 4:
                            dve.wait_ge(*ph.after("row_copied", u + 2))
                        if ahead and step >= 4:
                            for i in range(4 * (step - 4), 4 * (step - 3)):
                                candidates(u + 1, i)

                    src = cand[u % 2]
                    for r in range(TOPK // 8):
                        nc.vector.max(top8[:, r, :], src).then_inc(*ph.mark("vec_step"))
                        k = ph.mine["vec_step"]
                        beside(2 * r)
                        dve.wait_ge(*ph.after("vec_step", k))
                        nc.vector.match_replace(cand_left, top8[:, r, :], src, -4.0).then_inc(*ph.mark("vec_step"))
                        k = ph.mine["vec_step"]
                        beside(2 * r + 1)
                        dve.wait_ge(*ph.after("vec_step", k))
                        src = cand_left
                    link(nc.vector.max(top8[:, TOPK // 8, :], src))
                    last = top8[:, TOPK // 8 - 1, 7:8]
                    if u >= 1:
                        dve.wait_ge(*ph.after("probs_ready", u))
                    link(nc.vector.tensor_reduce(limit, cand_c[:, :, PER_CHUNK - 1], AX.X, ALU.max))
                    link(nc.vector.tensor_tensor(limit, limit, top8[:, TOPK // 8, 0:1], ALU.max))
                    nc.vector.tensor_tensor(unsure, limit, last, ALU.is_ge).then_inc(*ph.mark("unsure_ready"))
                    link(nc.vector.scalar_tensor_tensor(sparse, row, last, row, ALU.is_ge, ALU.mult))
                    dve.wait_ge(*ph.after("unsure_summed", u + 1))
                    link(nc.vector.tensor_scalar(unsure_any, ps[0:1, 7, 0:1], 0.0, None, ALU.is_gt))
                    any_row = dve.value_load(unsure_any, min_val=0, max_val=1)
                    with dve.If(any_row > 0):
                        src = row
                        for r in range(TOPK // 8):
                            nc.vector.max(top8[:, r, :], src)
                            dve.drain()
                            nc.vector.match_replace(sparse, top8[:, r, :], src, -4.0)
                            dve.drain()
                            src = sparse
                        nc.vector.scalar_tensor_tensor(sparse, sparse, -3.0, row, ALU.is_lt, ALU.mult)
                        dve.drain()
                    nc.vector.tensor_copy(limit, last).then_inc(*ph.mark("sparse_ready"))
                    return
                if kind == "attn4":
                    link(nc.vector.tensor_reduce(st[:, 14, u % T:u % T + 1], flat[:, 0:n], AX.X, ALU.max, negate=True))
                    nc.vector.tensor_scalar(negmax[:, u:u + 1], st[:, 14, u % T:u % T + 1], 0.25, None, ALU.mult)\
                        .then_inc(*ph.mark("max_ready"))
                else:
                    nc.vector.tensor_reduce(negmax[:, u:u + 1], flat[:, 0:n], AX.X, ALU.max, negate=True)\
                        .then_inc(*ph.mark("max_ready"))

            if kind == "attn2":
                dve.wait_ge(*ph.after("row_copied", 1))
                for i in range(CAND_OPS):
                    candidates(0, i)
                dve.wait_ge(*ph.own("cand_step"))
            if kind.startswith("attn3"):
                place_side(0)
            maxima(0)
            if early(kind):
                maxima(1)
            for u in range(len(units)):
                hd, q = units[u]
                if u + 1 < len(units):
                    if kind.startswith("attn3"):
                        place_side(u + 1)
                    elif not early(kind):
                        maxima(u + 1)
                for g in range(groups(kind, q)):
                    if copier(kind, g) == "pt_by_vec":
                        copy_group(ph, dve, kind, u, g, nc.vector.tensor_copy)
                if u + 1 < len(units) and kind.startswith("attn3"):
                    maxima(u + 1)
                if u + 2 < len(units) and early(kind):
                    maxima(u + 2)
                dve.wait_ge(*ph.after("probs_ready", u + 1))
                link(nc.vector.reciprocal(rinv[:, u:u + 1], rowsum[:, u:u + 1]))
                dve.wait_ge(*ph.after("ctx_ready", u + 1))
                dest(u, hd, q, context_of(kind, hd), rinv[:, u:u + 1]).then_inc(*ph.mark("ctx_copied"))

        def add_to_h(u, hd, q, o, r):
            return nc.vector.scalar_tensor_tensor(h[:, q, :], o, r, h[:, q, :], ALU.mult, ALU.add)

        def to_ctxt(w):
            def put(u, hd, q, o, r):
                return nc.vector.tensor_scalar(ctxt[:, q, w * hd:w * hd + w], o, r, None, ALU.mult)
            return put

        def top2_onehots(link, src, oh1, oh2, tmp, m, iota, shape):
            for oh, s in ((oh1, src), (oh2, tmp)):
                link(nc.vector.tensor_reduce(m, s, AX.X, ALU.max))
                link(nc.vector.tensor_tensor(oh, s, bc(m, shape), ALU.is_equal))
                link(nc.vector.tensor_tensor(oh, oh, iota, ALU.mult))
                link(nc.vector.tensor_reduce(m, oh, AX.X, ALU.max))
                link(nc.vector.tensor_tensor(oh, oh, bc(m, shape), ALU.is_equal))
                if oh is oh1 and oh2 is not None:
                    link(nc.vector.scalar_tensor_tensor(tmp, oh, -BIG, src, ALU.mult, ALU.add))
                if oh2 is None:
                    return

        block = ctx.enter_context(nc.Block())

        @block.sync
        def _(sp):
            half = EXPERT_AT // 2
            sp.dma_start(cst[:, 0:half], consts[:, 0:half]).then_inc(consts_in, 16)
            sp.dma_start(cst[:, half:EXPERT_AT], consts[:, half:EXPERT_AT]).then_inc(consts_in, 16)
            sp.dma_start(experts_in[:, :], consts[:, EXPERT_AT:CONST_COLS]).then_inc(consts_in, 16)
            sp.dma_start(route_sb[:, :], route).then_inc(route_in, 16)
            for s in range(2):
                sp.dma_start(klo[0:D, s, :], pe_low).then_inc(consts_in, 16)
            sp.dma_start(kup[0:D, 0, :], pe_up).then_inc(consts_in, 16)
            sp.dma_start(kup[0:D, 1, :], pe_up).then_inc(consts_in, 16)

            def load_tokens(b):
                sp.dma_start(xp, patches[bass.ds(b, 1), :, :].rearrange("a p n -> (a p) n")).then_inc(patches_in, 16)
                sp.dma_start(txt_in, txt[bass.ds(b, 1), :, :].rearrange("a (t p) d -> (a p) t d", p=P)).then_inc(patches_in, 16)

            def load_experts(b):
                for g in range(NG):
                    e = sp.value_load(route_sb[0:1, bass.ds(b * NG + g, 1)], min_val=0, max_val=E1 - 1)
                    for layer in range(2):
                        sp.dma_start(rw[:, layer, g, :], w_route[layer, bass.ds(e, 1), :, :].rearrange("a p n -> (a p) n"))\
                            .then_inc(weights_in, 16)

            load_tokens(0)
            with sp.Fori(0, B - 1) as b:
                sp.wait_ge(led.sems["phase_left"], led.ended("embed"))
                load_tokens(b + 1)
                sp.wait_ge(led.sems["phase_left"], led.ended("mean0"))
                led.end_pass(sp, b + 1)
            sp.wait_ge(led.sems["phase_left"], led.ended("mean0"))
            led.end_pass(sp, B)
            sp.wait_ge(route_in, 16)
            load_experts(0)
            sp.wait_ge(led.sems["phase_left"], led.ended("route0"))
            led.end_pass(sp, B + 1)

            sp.sem_inc(led.sems["res_free"], 1)

            def store_row(b):
                sp.wait_ge(led.sems["phase_left"], led.ended("moe4"))
                sp.dma_start(out[bass.ds(b, 1), :, :].rearrange("a (t p) d -> (a p) t d", p=P), res[:, :, :])\
                    .then_inc(stored, 16)

            with sp.Fori(0, B - 1) as b:
                sp.wait_ge(led.sems["phase_left"], led.ended("moe1"))
                load_experts(b + 1)
                store_row(b)
                led.end_pass(sp, b + (B + 2))
                sp.wait_ge(stored, 16 * (b + 1))
                sp.sem_inc(led.sems["res_free"], 1)
            store_row(B - 1)
            led.end_pass(sp, 2 * B + 1)
            sp.wait_ge(stored, 16 * B)

        @block.gpsimd
        def _(pool):
            with pool.Fori(0, B) as b:
                ph = Phase(led, "embed")
                pool.wait_ge(consts_in, CONST_DMAS)
                clear_upper(ph, pool)
                norm_pool(ph, pool, 1)
                ph.leave(pool)
                Phase(led, "attn0").leave(pool)
                ph = Phase(led, "mean0")
                norm_pool(ph, pool, 1)
                ph.leave(pool)
                led.end_pass(pool, b + 1)
            Phase(led, "route0").leave(pool)
            led.end_pass(pool, B + 1)
            with pool.Fori(0, B) as b:
                ph = Phase(led, "moe0")
                norm_pool(ph, pool, 1)
                norm_pool(ph, pool, 2)
                ph.leave(pool)
                ph = Phase(led, "qkv1")
                stack_pool(ph, pool)
                norm_pool(ph, pool, 1)
                ph.leave(pool)
                Phase(led, "attn1").leave(pool)
                ph = Phase(led, "moe1")
                norm_pool(ph, pool, 1)
                ph.leave(pool)
                ph = Phase(led, "sim2")
                clear_upper(ph, pool)
                norm_pool(ph, pool, 1)
                pool.wait_ge(*ph.after("var_ready", 3))
                nc.gpsimd.tensor_tensor(st[:, 4, :], st[:, 3, :], K("half")[:, T:2 * T], ALU.pow).then_inc(*ph.mark("rstd_ready"))
                ph.leave(pool)
                Phase(led, "attn2").leave(pool)
                ph = Phase(led, "moe2")
                norm_pool(ph, pool, 1)
                ph.leave(pool)
                for half, name in enumerate(("rel3a", "rel3b")):
                    ph = Phase(led, name)
                    link = pool_chain(ph, pool)
                    if half == 0:
                        link(nc.gpsimd.memset(qup[0:D, :, S - 1:S], 0.0))
                        nc.gpsimd.memset(qup[D:P, :, :], 0.0).then_inc(*ph.mark("upper_cleared"))
                        pool.wait_ge(*ph.own("upper_cleared"))
                        norm_pool(ph, pool, 1)
                        norm_pool(ph, pool, 2)
                    for i in range(2 * NB):
                        s, j = i // NB, i % NB
                        c = 512 * j
                        pool.wait_ge(*ph.after("rot_ready", i + 1))
                        link(nc.gpsimd.tensor_tensor(qlo[0:D, s, c:c + 512], rt1[:, i % 2, :], rt2[:, i % 2, :], ALU.add))
                        o = 1 if j == 0 else 0
                        nc.gpsimd.tensor_tensor(qup[0:D, s, c - 1 + o:c + 511], rt1[:, i % 2, o:512], rt2[:, i % 2, o:512],
                                                ALU.add).then_inc(*ph.mark("rot_used"))
                        pool.wait_ge(*ph.own("rot_used"))
                    ph.leave(pool)
                    ph = Phase(led, "attn3" + "ab"[half])
                    attn_pool(ph, pool, "attn3" + "ab"[half])
                    ph.leave(pool)
                ph = Phase(led, "rope4")
                norm_pool(ph, pool, 1)
                norm_pool(ph, pool, 2)
                for i in range(2 * NB):
                    j = i // 2
                    dst = (qt, kt)[i % 2]
                    cols = slice(512 * j, 512 * (j + 1))
                    pool.wait_ge(*ph.after("rope_ready", i + 1))
                    nc.gpsimd.tensor_tensor(dst[:, cols], rp1[:, (i % 2) * 512:(i % 2) * 512 + 512],
                                            rp2[:, (i % 2) * 512:(i % 2) * 512 + 512], ALU.add).then_inc(*ph.mark("rope_used"))
                    pool.wait_ge(*ph.own("rope_used"))
                ph.leave(pool)
                ph = Phase(led, "attn4")
                attn_pool(ph, pool, "attn4")
                ph.leave(pool)
                ph = Phase(led, "moe4")
                norm_pool(ph, pool, 1)
                ph.leave(pool)
                led.end_pass(pool, b + (B + 2))

        @block.scalar
        def _(act):
            with act.Fori(0, B) as b:
                ph = Phase(led, "embed")
                qkv_act(ph, act)
                ph.leave(act)
                ph = Phase(led, "attn0")
                attn_act(ph, act, "attn0")
                ph.leave(act)
                Phase(led, "mean0").leave(act)
                led.end_pass(act, b + 1)
            ph = Phase(led, "route0")
            for n in (1, 2):
                act.wait_ge(*ph.after("exp_in", n))
                nc.scalar.activation(r0[:, 1, :, :], r0[:, 0, :, :], ACT.Exp).then_inc(*ph.mark("exp_out"))
            act.wait_ge(*ph.after("exp_in", 3))
            nc.scalar.activation(r0s[:, 3, :], r0s[:, 2, :], ACT.Exp).then_inc(*ph.mark("exp_out"))
            ph.leave(act)
            led.end_pass(act, B + 1)
            with act.Fori(0, B) as b:
                ph = Phase(led, "moe0")
                transpose_act(ph, act, xt, [0, 1, 2])
                for i in range(2 * NB):
                    k, j = i // NB, i % NB
                    act.wait_ge(*ph.after("hid_psum", i + 1))
                    nc.scalar.activation(hid[:, k, 512 * j:512 * (j + 1)], ps[:, 3 + i % 3, :], ACT.Gelu)\
                        .then_inc(*ph.mark("hid_ready"))
                ph.leave(act)
                ph = Phase(led, "qkv1")
                stack_act(ph, act)
                ph.leave(act)
                ph = Phase(led, "attn1")
                attn_act(ph, act, "attn1")
                ph.leave(act)
                ph = Phase(led, "moe1")
                transpose_act(ph, act, xt, [0, 1, 2])
                transpose_act(ph, act, xt, [0, 1, 2], n0=NB)
                for j in range(NB):
                    act.wait_ge(*ph.after("hid_psum", j + 1))
                    nc.scalar.activation(hid[:, 0, 512 * j:512 * (j + 1)], ps[:, 5 + j, :], ACT.Relu)\
                        .then_inc(*ph.mark("hid_ready"))
                act.wait_ge(*ph.after("bias_ready", 1))
                for layer in range(2):
                    for j in range(NG // GPB):
                        act.wait_ge(*ph.after("expert_psum", layer * (NG // GPB) + j + 1))
                        for i in range(GPB):
                            g = GPB * j + i
                            ins = nc.scalar.activation(hid[:, 1 - layer, GRP * g:GRP * (g + 1)],
                                                       ps[:, 4 * layer + j, GRP * i:GRP * (i + 1)], ACT.Relu,
                                                       bias=bias1[:, layer, g:g + 1])
                        ins.then_inc(*ph.mark("expert_ready"))
                ph.leave(act)
                ph = Phase(led, "sim2")
                transpose_act(ph, act, xt, [0, 1, 2])
                transpose_act(ph, act, qt, [5, 6, 7], n0=NB)
                ph.leave(act)
                ph = Phase(led, "attn2")
                attn_act(ph, act, "attn2")
                ph.leave(act)
                ph = Phase(led, "moe2")
                transpose_act(ph, act, xt, [0, 1, 2])
                transpose_act(ph, act, xt2, [4, 5, 6], n0=NB, width=P)
                for i in range(NB * C2):
                    j, c = i // C2, i % C2
                    act.wait_ge(*ph.after("hid_psum", i + 1))
                    nc.scalar.activation(hid[:, c, 512 * j:512 * (j + 1)], ps[:, i % 4, :], ACT.Relu)\
                        .then_inc(*ph.mark("hid_ready"))
                ph.leave(act)
                for half, name in enumerate(("rel3a", "rel3b")):
                    ph = Phase(led, name)
                    if half == 0:
                        transpose_act(ph, act, xt, [0, 1, 2])
                        act.wait_ge(*ph.after("bias_ready", 1))
                    for i in range(2 * NB):
                        s, j = i // NB, i % NB
                        hd = 2 * half + s
                        bank, cols = 4 * (i % 2), slice(512 * j, 512 * (j + 1))
                        act.wait_ge(*ph.after("q_psum", i + 1))
                        if i >= 2:
                            act.wait_ge(*ph.after("rot_psum", i - 1))
                        nc.scalar.activation(qv[0:DH, i % 2, :], ps[0:DH, bank, :], ACT.Identity,
                                             bias=bias3[0:DH, hd:hd + 1], scale=0.125).then_inc(*ph.mark("qv_ready"))
                        if half == 0 and i == 0:
                            act.wait_ge(*ph.after("upper_cleared", 1))
                        for content in (qlo, qup):
                            ins = nc.scalar.activation(content[64:80, s, cols], ps[64:80, bank, :], ACT.Identity,
                                                       bias=bias3[64:80, hd:hd + 1], scale=0.125)
                        ins.then_inc(*ph.mark("content_ready"))
                    ph.leave(act)
                    ph = Phase(led, "attn3" + "ab"[half])
                    attn_act(ph, act, "attn3" + "ab"[half])
                    ph.leave(act)
                ph = Phase(led, "rope4")
                transpose_act(ph, act, xt, [0, 1, 2])
                transpose_act(ph, act, xt, [0, 1, 2], n0=NB)
                act.wait_ge(*ph.after("v_psum", 1))
                nc.scalar.copy(v[:, :, 0:32], ps[:, 3, 0:T * 32].rearrange("p (t d) -> p t d", d=32))
                ph.leave(act)
                ph = Phase(led, "attn4")
                attn_act(ph, act, "attn4")
                ph.leave(act)
                ph = Phase(led, "moe4")
                transpose_act(ph, act, xt, [0, 1, 2])
                transpose_act(ph, act, xt, [0, 1, 2], n0=NB)
                for j in range(NB):
                    nc.scalar.copy(x_high[:, 512 * j:512 * (j + 1)].bitcast(F32R), ps[:, j, :]).then_inc(*ph.mark("high_ready"))
                act.wait_ge(*ph.after("exp_in", 1))
                nc.scalar.activation(lg[:, 1, :], lg[:, 0, :], ACT.Exp).then_inc(*ph.mark("exp_out"))
                for i in range(NB * E3 * 2):
                    act.wait_ge(*ph.after("gate_psum", i + 1))
                    if i >= 2:
                        act.wait_ge(*ph.after("gated", i - 1))
                    nc.scalar.activation(sg[:, i % 2, :], ps[0:HC3, 2 * (i % 2), :], ACT.Silu).then_inc(*ph.mark("silu_ready"))
                ph.leave(act)
                led.end_pass(act, b + (B + 2))

        @block.tensor
        def _(pe):
            with pe.Fori(0, B) as b:
                ph = Phase(led, "embed")
                pe.wait_ge(consts_in, CONST_DMAS)
                pe.wait_ge(patches_in, 32 * (b + 1))
                for t in range(TP):
                    ins = nc.tensor.matmul(ps[:, 0, t * D:(t + 1) * D], xp[:, t * P:(t + 1) * P], K("tok_w"), start=True, stop=True)
                ins.then_inc(*ph.mark("emb_psum"))
                qkv_pe(ph, pe, "q0", "k0", "v0")
                ph.leave(pe)
                ph = Phase(led, "attn0")
                attn_pe(ph, pe, "attn0")
                ph.leave(pe)
                ph = Phase(led, "mean0")
                pe.wait_ge(*ph.after("normed", 1))
                for t in range(T):
                    ins = nc.tensor.matmul(ps[0:D, 0, 0:P], x[:, t, :], K("mean"), start=(t == 0), stop=(t == T - 1))
                ins.then_inc(*ph.mark("mean_psum"))
                pe.wait_ge(*ph.after("mean_ready", 1))
                nc.tensor.matmul(ps[:, 1, 0:E0], mean_t[:, :], W("wr0"), start=True, stop=True).then_inc(*ph.mark("logit_psum"))
                ph.leave(pe)
                led.end_pass(pe, b + 1)
            Phase(led, "route0").leave(pe)
            led.end_pass(pe, B + 1)
            with pe.Fori(0, B) as b:
                ph = Phase(led, "moe0")
                pe.wait_ge(*ph.after("normed", 1))
                transpose_pe(ph, x, [0, 1, 2])
                pe.wait_ge(*ph.after("weights_ready", 1))
                for i in range(2 * NB):
                    k, j = i // NB, i % NB
                    if k == 0:
                        pe.wait_ge(*ph.after("xt_copied", j + 1))
                    if i >= 3:
                        pe.wait_ge(*ph.after("hid_ready", i - 2))
                    nc.tensor.matmul(ps[:, 3 + i % 3, :], w1s[:, k, :], xt[:, 512 * j:512 * (j + 1)], start=True, stop=True)\
                        .then_inc(*ph.mark("hid_psum"))
                pe.wait_ge(*ph.after("hid_ready", 2 * NB))
                for t in range(T):
                    for k in range(2):
                        ins = nc.tensor.matmul(ps[:, 6 + t // 6, (t % 6) * D:(t % 6 + 1) * D], hid[:, k, t * P:(t + 1) * P],
                                               w2s[:, k, :], start=(k == 0), stop=(k == 1))
                    if t % 6 == 5:
                        ins.then_inc(*ph.mark("out_psum"))
                ph.leave(pe)
                ph = Phase(led, "qkv1")
                stack_pe(ph, pe)
                ph.leave(pe)
                ph = Phase(led, "attn1")
                attn_pe(ph, pe, "attn1")
                ph.leave(pe)
                ph = Phase(led, "moe1")
                transpose_pe(ph, ctxt, [0, 1, 2])
                pe.wait_ge(*ph.after("xt_copied", NB))
                rows_pe(ph, W("proj1"), xt, [3, 4], "proj_psum")
                pe.wait_ge(*ph.after("normed", 1))
                transpose_pe(ph, x, [0, 1, 2])
                for j in range(NB):
                    pe.wait_ge(*ph.after("xt_copied", NB + j + 1))
                    nc.tensor.matmul(ps[:, 5 + j, :], W("wi1"), xt[:, 512 * j:512 * (j + 1)], start=True, stop=True)\
                        .then_inc(*ph.mark("hid_psum"))
                pe.wait_ge(*ph.after("bias_ready", 1))
                pe.wait_ge(weights_in, (b + 1) * (16 * 2 * NG))
                for layer in range(2):
                    if layer == 0:
                        pe.wait_ge(*ph.after("hid_ready", NB))
                    else:
                        pe.wait_ge(*ph.after("expert_ready", NG // GPB))
                    for j in range(NG // GPB):
                        bank = ps[:, 4 * layer + j, :]
                        w = GRP * GPB
                        nc.tensor.matmul(bank[:, 0:w], wsi[:, layer, :], hid[:, layer, w * j:w * (j + 1)], start=True, stop=False,
                                         skip_group_check=True)
                        for i in range(GPB):
                            g = GPB * j + i
                            ins = nc.tensor.matmul(bank[:, GRP * i:GRP * (i + 1)], rw[:, layer, g, 0:HID1],
                                                   hid[:, layer, GRP * g:GRP * (g + 1)], start=False, stop=(i == GPB - 1),
                                                   skip_group_check=True)
                        ins.then_inc(*ph.mark("expert_psum"))
                pe.wait_ge(*ph.after("expert_ready", 2 * (NG // GPB)))
                rows_pe(ph, W("wo1"), hid[:, 0, :], [0, 1], "out_psum")
                ph.leave(pe)
                ph = Phase(led, "sim2")
                pe.wait_ge(*ph.after("normed", 1))
                transpose_pe(ph, x, [0, 1, 2])
                pe.wait_ge(*ph.after("xt_copied", NB))
                rows_pe(ph, W("w2a"), xt, [3, 4], "v_psum")
                pe.wait_ge(*ph.after("normed", 2))
                transpose_pe(ph, y, [5, 6, 7])
                ph.leave(pe)
                ph = Phase(led, "attn2")
                attn_pe(ph, pe, "attn2")
                ph.leave(pe)
                ph = Phase(led, "moe2")
                pe.wait_ge(*ph.after("normed", 1))
                transpose_pe(ph, xa[:, :, 0:D], [0, 1, 2])
                pe.wait_ge(*ph.after("xt_copied", NB))
                for t in range(T):
                    ins = nc.tensor.matmul(ps[:, 3, t * E2:(t + 1) * E2], xt[:, t * P:(t + 1) * P], W("rw2"), start=True, stop=True)
                ins.then_inc(*ph.mark("logit_psum"))
                pe.wait_ge(*ph.after("normed", 2))
                transpose_pe(ph, xa, [4, 5, 6], width=P)
                for i in range(NB * C2):
                    j, c = i // C2, i % C2
                    if c == 0:
                        pe.wait_ge(*ph.after("xt_copied", NB + j + 1))
                    if i >= 4:
                        pe.wait_ge(*ph.after("hid_ready", i - 3))
                    nc.tensor.matmul(ps[:, i % 4, :], K("w1_2")[:, c * P:(c + 1) * P], xt2[:, 512 * j:512 * (j + 1)],
                                     start=True, stop=True).then_inc(*ph.mark("hid_psum"))
                pe.wait_ge(*ph.after("hid_ready", NB * C2))
                for t in range(T):
                    o = ps[:, 4 + t // 6, (t % 6) * D:(t % 6 + 1) * D]
                    for c in range(C2):
                        nc.tensor.matmul(o, hid[:, c, t * P:(t + 1) * P], K("w2_2")[:, c * D:(c + 1) * D], start=(c == 0), stop=False)
                    ins = nc.tensor.matmul(o, xt2[64:96, t * P:(t + 1) * P], K("b2_2")[64:96, :], start=False, stop=True)
                    if t % 6 == 5:
                        ins.then_inc(*ph.mark("out_psum"))
                ph.leave(pe)
                for half, name in enumerate(("rel3a", "rel3b")):
                    ph = Phase(led, name)
                    if half == 0:
                        pe.wait_ge(*ph.after("normed", 1))
                        transpose_pe(ph, x, [0, 1, 2])
                        pe.wait_ge(*ph.after("xt_copied", NB))
                        rows_pe(ph, W("v3"), xt, [6, 7], "v_psum")
                        pe.wait_ge(*ph.after("v_copied", 1))
                    def content(i):
                        s, j = i // NB, i % NB
                        hd = 2 * half + s
                        bank, cols = 4 * (i % 2), slice(512 * j, 512 * (j + 1))
                        if i >= 2:
                            pe.wait_ge(*ph.after("k_copied", i - 1))
                            pe.wait_ge(*ph.after("content_ready", i - 1))
                        nc.tensor.matmul(ps[0:80, bank, :], W("wq3")[:, 80 * hd:80 * hd + 80], xt[:, cols], start=True, stop=True)\
                            .then_inc(*ph.mark("q_psum"))
                        at = CONST_AT["wk3"][1] + DH * hd
                        nc.tensor.matmul(ps[0:80, bank + 1, :], cst[:, at - D:at + DH], xt[:, cols], start=True, stop=True)\
                            .then_inc(*ph.mark("k_psum"))

                    content(0)
                    for i in range(2 * NB):
                        hd, bank = 2 * half + i // NB, 4 * (i % 2)
                        if i + 1 < 2 * NB:
                            content(i + 1)
                        pe.wait_ge(*ph.after("qv_ready", i + 1))
                        if i >= 2:
                            pe.wait_ge(*ph.after("rot_ready", i - 1))
                        for r in range(2):
                            w = W("wpos3")[:, (2 * hd + r) * D:(2 * hd + r + 1) * D]
                            ins = nc.tensor.matmul(ps[0:D, bank + 2 + r, :], w, qv[:, i % 2, :], start=True, stop=True)
                        ins.then_inc(*ph.mark("rot_psum"))
                    ph.leave(pe)
                    ph = Phase(led, "attn3" + "ab"[half])
                    attn_pe(ph, pe, "attn3" + "ab"[half])
                    ph.leave(pe)
                ph = Phase(led, "rope4")
                transpose_pe(ph, ctxt, [0, 1, 2])
                pe.wait_ge(*ph.after("xt_copied", NB))
                rows_pe(ph, W("wout3"), xt, [3, 4], "proj_psum")
                pe.wait_ge(*ph.after("normed", 1))
                transpose_pe(ph, x, [0, 1, 2])
                pe.wait_ge(*ph.after("xt_copied", 2 * NB))
                for t in range(T):
                    ins = nc.tensor.matmul(ps[:, 3, t * 32:(t + 1) * 32], xt[:, t * P:(t + 1) * P], W("wv4"), start=True, stop=True)
                ins.then_inc(*ph.mark("v_psum"))
                for i in range(2 * NB):
                    j, w = i // 2, ("wq4", "wk4")[i % 2]
                    bank = 4 + 2 * (i % 2)
                    if i >= 2:
                        pe.wait_ge(*ph.after("rope_ready", i - 1))
                    for r in range(2):
                        ins = nc.tensor.matmul(ps[:, bank + r, :], W(w)[:, r * P:(r + 1) * P], xt[:, 512 * j:512 * (j + 1)],
                                               start=True, stop=True)
                    ins.then_inc(*ph.mark("rope_psum"))
                ph.leave(pe)
                ph = Phase(led, "attn4")
                attn_pe(ph, pe, "attn4")
                ph.leave(pe)
                ph = Phase(led, "moe4")
                transpose_pe(ph, ctxt, [0, 1, 2])
                pe.wait_ge(*ph.after("xt_copied", NB))
                rows_pe(ph, W("wo4"), xt, [3, 4], "proj_psum")
                pe.wait_ge(*ph.after("normed", 1))
                transpose_pe(ph, xx.rearrange("p t r d -> p t (r d)"), [0, 1, 2], width=P)
                pe.wait_ge(*ph.after("xt_copied", 2 * NB))
                for t in range(T):
                    ins = nc.tensor.matmul(ps[:, 7, t * E3:(t + 1) * E3], xt[:, t * P:(t + 1) * P], W("rt4"), start=True, stop=True)
                ins.then_inc(*ph.mark("logit_psum"))

                def down(n):
                    j, e = n // E3, n % E3
                    pe.wait_ge(*ph.after("gated", 2 * n + 2))
                    if n == 0:
                        pe.wait_ge(*ph.after("exp_in", 1))
                    if e == 0 and j > 0:
                        pe.wait_ge(*ph.after("mixed", 4 * j))
                    for t in range(4):
                        for c in range(2):
                            ins = nc.tensor.matmul(ps[:, 4 + t, e * D:(e + 1) * D], hh[:, n % 2, c, t * P:(t + 1) * P],
                                                   K("w2_4")[:, (2 * e + c) * D:(2 * e + c + 1) * D], start=(c == 0), stop=(c == 1))
                    ins.then_inc(*ph.mark("down_psum"))

                for n in range(NB * E3):
                    j, e = n // E3, n % E3
                    for c in range(2):
                        i = 2 * n + c
                        if i >= 2:
                            pe.wait_ge(*ph.after("gated", i - 1))
                        if n == 0 and c == 0:
                            pe.wait_ge(*ph.after("low_ready", NB))
                        for k, name in enumerate(("gate_psum", "up_psum")):
                            at = (k * E3 * 2 + 2 * e + c) * HC3
                            for xs in (x_high, x_low):
                                ins = nc.tensor.matmul(ps[0:HC3, 2 * (i % 2) + k, :], experts[:, at:at + HC3].bitcast(F32R),
                                                       xs[:, 512 * j:512 * (j + 1)].bitcast(F32R),
                                                       start=(xs is x_high), stop=(xs is x_low))
                            ins.then_inc(*ph.mark(name))
                    if n > 0:
                        down(n - 1)
                down(NB * E3 - 1)
                ph.leave(pe)
                led.end_pass(pe, b + (B + 2))

        @block.vector
        def _(dve):
            dve.wait_ge(consts_in, CONST_DMAS)
            for layer in range(2):
                nc.vector.tensor_tensor(wsi[:, layer, :], wsi[:, layer, :], ident, ALU.add)
            rough = big[:, 0:CONST_COLS - EXPERT_AT]
            nc.vector.tensor_copy(rough.bitcast(F32R), experts_in[:, :])
            nc.vector.drain()
            nc.vector.tensor_tensor(experts[D:P, :].bitcast(F32R), experts_in[D:P, :], rough[D:P, :], ALU.subtract)
            nc.vector.tensor_copy(experts[0:D, :].bitcast(F32R), experts_in[0:D, :])
            for rows in (xt[D:P, :], mean_t[D:P, :], w1s[D:P, :, :], klo[D:P, :, :], kup[D:P, :, :], qz[:, :, :, :]):
                nc.vector.memset(rows, 0.0)
            nc.vector.drain()
            nc.vector.memset(xt[D:D + 1, :], 1.0)
            nc.vector.memset(mean_t[D:D + 1, :], 1.0)
            with dve.Fori(0, B) as b:
                ph = Phase(led, "embed")
                link = chain(ph, dve)
                dve.wait_ge(patches_in, 32 * (b + 1))
                nc.vector.tensor_copy(h[:, TP:T, :], txt_in)
                dve.wait_ge(*ph.after("emb_psum", 1))
                link(nc.vector.tensor_tensor(h[:, 0:TP, :].rearrange("p t d -> p (t d)"), ps[:, 0, :], K("pos"), ALU.add))
                norm_vec(ph, dve, h[:, :, :], x[:, :, :], 1)
                ready_vec(ph, dve)
                qkv_vec(ph, dve, 1.0)
                ph.leave(dve)
                ph = Phase(led, "attn0")
                attn_vec(ph, dve, "attn0", add_to_h)
                ph.leave(dve)
                ph = Phase(led, "mean0")
                link = chain(ph, dve)
                norm_vec(ph, dve, h[:, :, :], x[:, :, :], 1)
                ready_vec(ph, dve)
                nc.vector.tensor_copy(hall[:, bass.ds(b, 1), :], h[:, :, :].rearrange("p t d -> p (t d)").unsqueeze(1))
                dve.wait_ge(*ph.after("mean_psum", 1))
                nc.vector.tensor_copy(mean_t[0:D, :], ps[0:D, 0, 0:P]).then_inc(*ph.mark("mean_ready"))
                dve.wait_ge(*ph.after("logit_psum", 1))
                nc.vector.tensor_copy(lg0[:, bass.ds(b, 1), :], ps[:, 1, 0:E0].unsqueeze(1))
                ph.leave(dve)
                led.end_pass(dve, b + 1)

            ph = Phase(led, "route0")
            link = chain(ph, dve)
            shape = [P, B, E0]
            src = lg0[:, :, :]
            for n in (1, 2):
                link(nc.vector.tensor_reduce(r0s[:, 0, :], src, AX.X, ALU.max))
                nc.vector.tensor_tensor(r0[:, 0, :, :], src, bc(r0s[:, 0, :], shape), ALU.subtract).then_inc(*ph.mark("exp_in"))
                dve.wait_ge(*ph.after("exp_out", n))
                link(nc.vector.tensor_reduce(r0s[:, 0, :], r0[:, 1, :, :], AX.X, ALU.add))
                link(nc.vector.reciprocal(r0s[:, 1, :], r0s[:, 0, :]))
                link(nc.vector.tensor_tensor(r0[:, 2, :, :], r0[:, 1, :, :], bc(r0s[:, 1, :], shape), ALU.mult))
                if n == 1:
                    load = r0[:, 3, 0, :]
                    link(nc.vector.tensor_reduce(load, r0[:, 2, :, :].rearrange("p b e -> p e b"), AX.X, ALU.add))
                    link(nc.vector.tensor_scalar(load, load, float(S), None, ALU.mult))
                    link(nc.vector.reciprocal(r0[:, 3, 1, :], load))
                    link(nc.vector.tensor_scalar(r0[:, 3, 1, :], r0[:, 3, 1, :], CAP0, 1.0, ALU.mult, ALU.min))
                    link(nc.vector.tensor_tensor(r0[:, 4, :, :], r0[:, 2, :, :],
                                                 r0[:, 3, 1, :].unsqueeze(1).to_broadcast(shape), ALU.mult))
                    src = r0[:, 4, :, :]
            iota = K("iota8").unsqueeze(1).to_broadcast(shape)
            oh1, oh2 = oh0[:, :, 0:E0], oh0[:, :, E0:2 * E0]
            top2_onehots(link, r0[:, 2, :, :], oh1, oh2, r0[:, 5, :, :], r0s[:, 0, :], iota, shape)
            for k, oh in enumerate((oh1, oh2)):
                link(nc.vector.tensor_tensor(r0[:, 6, :, :], oh, r0[:, 2, :, :], ALU.mult))
                link(nc.vector.tensor_reduce(r0s[:, 4 + k, :], r0[:, 6, :, :], AX.X, ALU.add))
            nc.vector.tensor_tensor(r0s[:, 2, :], r0s[:, 5, :], r0s[:, 4, :], ALU.subtract).then_inc(*ph.mark("exp_in"))
            dve.wait_ge(*ph.after("exp_out", 3))
            link(nc.vector.tensor_scalar(r0s[:, 4, :], r0s[:, 3, :], 1.0, None, ALU.add))
            link(nc.vector.reciprocal(r0s[:, 5, :], r0s[:, 4, :]))
            link(nc.vector.tensor_tensor(r0s[:, 6, :], r0s[:, 3, :], r0s[:, 5, :], ALU.mult))
            for k, oh in enumerate((oh1, oh2)):
                link(nc.vector.tensor_tensor(wt0[:, :, k * E0:(k + 1) * E0], oh, bc(r0s[:, 5 + k, :], shape), ALU.mult))
            ph.leave(dve)
            led.end_pass(dve, B + 1)

            with dve.Fori(0, B) as b:
                ph = Phase(led, "moe0")
                link = chain(ph, dve)
                nc.vector.tensor_copy(ohb[:, :].unsqueeze(1), oh0[:, bass.ds(b, 1), :])
                nc.vector.tensor_copy(wtb[:, :].unsqueeze(1), wt0[:, bass.ds(b, 1), :])
                link(nc.vector.tensor_copy(h[:, :, :].rearrange("p t d -> p (t d)").unsqueeze(1), hall[:, bass.ds(b, 1), :]))
                norm_vec(ph, dve, h[:, :, :], x[:, :, :], 1)
                ready_vec(ph, dve)
                for k in range(2):
                    sel = big[0:65, 0:E0 * F0].rearrange("p (f e) -> p f e", e=E0)
                    link(nc.vector.tensor_tensor(sel, K("w1_0").rearrange("p (e f) -> p f e", e=E0),
                                                 ohb[0:65, k * E0:(k + 1) * E0].unsqueeze(1).to_broadcast([65, F0, E0]), ALU.mult))
                    link(nc.vector.tensor_reduce(w1s[0:65, k, :], sel, AX.X, ALU.add))
                    for table, dst in (("w2_0", w2s), ("b2_0", b2s)):
                        sel = big[:, 0:E0 * D].rearrange("p (f e) -> p f e", e=E0)
                        link(nc.vector.tensor_tensor(sel, K(table).rearrange("p (e f) -> p f e", e=E0),
                                                     wtb[:, k * E0:(k + 1) * E0].unsqueeze(1).to_broadcast([P, D, E0]), ALU.mult))
                        link(nc.vector.tensor_reduce(dst[:, k, :], sel, AX.X, ALU.add))
                nc.vector.tensor_tensor(b2s[:, 0, :], b2s[:, 0, :], b2s[:, 1, :], ALU.add).then_inc(*ph.mark("weights_ready"))
                dve.wait_ge(*ph.own("weights_ready"))
                for i in range(2):
                    dve.wait_ge(*ph.after("out_psum", i + 1))
                    link(nc.vector.tensor_tensor(y[:, 6 * i:6 * i + 6, :], rows_bank([6, 7], i), x[:, 6 * i:6 * i + 6, :], ALU.add))
                link(nc.vector.tensor_tensor(y[:, :, :], y[:, :, :], per_token(b2s[:, 0, :]), ALU.add))
                norm_vec(ph, dve, y[:, :, :], x[:, :, :], 2)
                link(nc.vector.tensor_tensor(x[:, :, :], x[:, :, :], per_token(K("gamma0")), ALU.mult))
                link(nc.vector.tensor_tensor(x[:, :, :], x[:, :, :], per_token(K("beta0")), ALU.add))
                link(nc.vector.tensor_tensor(h[:, :, :], h[:, :, :], x[:, :, :], ALU.add))
                ph.leave(dve)

                ph = Phase(led, "qkv1")
                norm_vec(ph, dve, h[:, :, :], x[:, :, :], 1)
                ready_vec(ph, dve)
                stack_vec(ph, dve)
                ph.leave(dve)
                ph = Phase(led, "attn1")
                attn_vec(ph, dve, "attn1", to_ctxt(32))
                ph.leave(dve)

                ph = Phase(led, "moe1")
                link = chain(ph, dve)
                dve.wait_ge(weights_in, (b + 1) * (16 * 2 * NG))
                for layer in range(2):
                    ins = nc.vector.tensor_scalar(bias1[:, layer, :], rw[:, layer, :, HID1], K("bs1")[:, layer:layer + 1], None, ALU.add)
                ins.then_inc(*ph.mark("bias_ready"))
                for i in range(2):
                    dve.wait_ge(*ph.after("proj_psum", i + 1))
                    link(nc.vector.tensor_tensor(h[:, 6 * i:6 * i + 6, :], rows_bank([3, 4], i), h[:, 6 * i:6 * i + 6, :], ALU.add))
                norm_vec(ph, dve, h[:, :, :], x[:, :, :], 1)
                ready_vec(ph, dve)
                link(nc.vector.tensor_tensor(h[:, :, :], h[:, :, :], per_token(K("bo1")), ALU.add))
                for i in range(2):
                    dve.wait_ge(*ph.after("out_psum", i + 1))
                    nc.vector.tensor_tensor(h[:, 6 * i:6 * i + 6, :], rows_bank([0, 1], i), h[:, 6 * i:6 * i + 6, :], ALU.add)
                ph.leave(dve)

                ph = Phase(led, "sim2")
                link = chain(ph, dve)
                norm_vec(ph, dve, h[:, :, :], x[:, :, :], 1)
                ready_vec(ph, dve)
                link(nc.vector.tensor_tensor(sq[:, :, :], x[:, :, :], x[:, :, :], ALU.mult))
                nc.vector.tensor_reduce(st[:, 3, :], sq[:, :, :], AX.X, ALU.add).then_inc(*ph.mark("var_ready"))
                dve.wait_ge(*ph.after("rstd_ready", 3))
                link(nc.vector.tensor_scalar(st[:, 5, :], st[:, 4, :], 1e-12, None, ALU.max))
                link(nc.vector.reciprocal(st[:, 6, :], st[:, 5, :]))
                link(nc.vector.tensor_tensor(y[:, :, :], x[:, :, :], bc(st[:, 6, :], [P, T, D]), ALU.mult))
                ready_vec(ph, dve)
                for i in range(2):
                    dve.wait_ge(*ph.after("v_psum", i + 1))
                    nc.vector.tensor_copy(v[:, 6 * i:6 * i + 6, :], rows_bank([3, 4], i))
                for j in range(NB):
                    dve.wait_ge(*ph.after("xt_copied", NB + j + 1))
                    nc.vector.tensor_copy(kt[0:D, 512 * j:512 * (j + 1)], qt[0:D, 512 * j:512 * (j + 1)])
                ph.leave(dve)
                ph = Phase(led, "attn2")
                attn_vec(ph, dve, "attn2", add_to_h)
                ph.leave(dve)

                ph = Phase(led, "moe2")
                link = chain(ph, dve)
                norm_vec(ph, dve, h[:, :, :], xa[:, :, 0:D], 1)
                ready_vec(ph, dve)
                dve.wait_ge(*ph.after("logit_psum", 1))
                logits = ps[:, 3, 0:T * E2].rearrange("p (t e) -> p t e", e=E2)
                oh = xa[:, :, D:D + E2]
                iota = K("iota32").unsqueeze(1).to_broadcast([P, T, E2])
                top2_onehots(link, logits, oh, None, None, st[:, 7, :], iota, [P, T, E2])
                link(nc.vector.tensor_scalar(xa[:, :, D + E2:P], oh, -1.0, None, ALU.add))
                ready_vec(ph, dve)
                for i in range(2):
                    dve.wait_ge(*ph.after("out_psum", i + 1))
                    nc.vector.scalar_tensor_tensor(h[:, 6 * i:6 * i + 6, :], rows_bank([4, 5], i), 0.0, h[:, 6 * i:6 * i + 6, :],
                                                   ALU.max, ALU.add)
                ph.leave(dve)

                for half, name in enumerate(("rel3a", "rel3b")):
                    ph = Phase(led, name)
                    link = chain(ph, dve)
                    if half == 0:
                        link(nc.vector.tensor_tensor(bias3[:, :], K("bq3"), K("uv3"), ALU.add))
                        nc.vector.tensor_scalar(bias3[:, :], bias3[:, :], 0.125, None, ALU.mult).then_inc(*ph.mark("bias_ready"))
                        norm_vec(ph, dve, h[:, :, :], x[:, :, :], 1)
                        norm_vec(ph, dve, x[:, :, :], y[:, :, :], 2)
                        link(nc.vector.tensor_tensor(y[:, :, :], y[:, :, :], per_token(K("gamma3")), ALU.mult))
                        link(nc.vector.tensor_tensor(x[:, :, :], y[:, :, :], per_token(K("beta3")), ALU.add))
                        ready_vec(ph, dve)
                        for i in range(2):
                            dve.wait_ge(*ph.after("v_psum", i + 1))
                            ins = nc.vector.tensor_copy(v[:, 6 * i:6 * i + 6, :], rows_bank([6, 7], i))
                        ins.then_inc(*ph.mark("v_copied"))
                    for i in range(2 * NB):
                        s, j = i // NB, i % NB
                        bank, cols = 4 * (i % 2), slice(512 * j, 512 * (j + 1))
                        dve.wait_ge(*ph.after("k_psum", i + 1))
                        if i >= 2:
                            dve.wait_ge(*ph.after("rot_used", i - 1))
                        for keys in (klo, kup):
                            ins = nc.vector.tensor_copy(keys[64:80, s, cols], ps[64:80, bank + 1, :])
                        ins.then_inc(*ph.mark("k_copied"))
                        dve.wait_ge(*ph.after("rot_psum", i + 1))
                        nc.vector.tensor_tensor(rt1[:, i % 2, :], ps[0:D, bank + 2, :], K("rot_c")[:, cols], ALU.mult)
                        nc.vector.tensor_tensor(rt2[:, i % 2, :], ps[0:D, bank + 3, :], K("rot_s")[:, cols], ALU.mult)\
                            .then_inc(*ph.mark("rot_ready"))
                    ph.leave(dve)
                    ph = Phase(led, "attn3" + "ab"[half])
                    attn_vec(ph, dve, "attn3" + "ab"[half], to_ctxt(DH))
                    ph.leave(dve)

                ph = Phase(led, "rope4")
                link = chain(ph, dve)
                for i in range(2):
                    dve.wait_ge(*ph.after("proj_psum", i + 1))
                    link(nc.vector.tensor_tensor(h[:, 6 * i:6 * i + 6, :], rows_bank([3, 4], i), h[:, 6 * i:6 * i + 6, :], ALU.add))
                norm_vec(ph, dve, h[:, :, :], y[:, :, :], 1)
                norm_vec(ph, dve, y[:, :, :], x[:, :, :], 2, centre=False, eps=RMS_EPS)
                link(nc.vector.tensor_tensor(x[:, :, :], x[:, :, :], per_token(K("rms1")), ALU.mult))
                ready_vec(ph, dve)
                for i in range(2 * NB):
                    j = i // 2
                    bank, o, cols = 4 + 2 * (i % 2), (i % 2) * 512, slice(512 * j, 512 * (j + 1))
                    dve.wait_ge(*ph.after("rope_psum", i + 1))
                    if i >= 2:
                        dve.wait_ge(*ph.after("rope_used", i - 1))
                    nc.vector.tensor_tensor(rp1[:, o:o + 512], ps[:, bank, :], K("rope_c")[:, cols], ALU.mult)
                    nc.vector.tensor_tensor(rp2[:, o:o + 512], ps[:, bank + 1, :], K("rope_s")[:, cols], ALU.mult)\
                        .then_inc(*ph.mark("rope_ready"))
                ph.leave(dve)
                ph = Phase(led, "attn4")
                attn_vec(ph, dve, "attn4", to_ctxt(DH))
                ph.leave(dve)

                ph = Phase(led, "moe4")
                link = chain(ph, dve)
                for i in range(2):
                    dve.wait_ge(*ph.after("proj_psum", i + 1))
                    ins = nc.vector.tensor_tensor(y[:, 6 * i:6 * i + 6, :], rows_bank([3, 4], i), y[:, 6 * i:6 * i + 6, :], ALU.add)
                ins.then_inc(*ph.mark("proj_read"))
                dve.wait_ge(*ph.own("proj_read"))
                norm_vec(ph, dve, y[:, :, :], x[:, :, :], 1, centre=False, eps=RMS_EPS)
                for half in range(2):
                    link(nc.vector.tensor_tensor(xx[:, :, half, :], x[:, :, :], per_token(K("rms2")), ALU.mult))
                ready_vec(ph, dve)
                link(nc.vector.tensor_tensor(y[:, :, :], y[:, :, :], h[:, :, :], ALU.add))
                for j in range(NB):
                    cols = slice(512 * j, 512 * (j + 1))
                    dve.wait_ge(*ph.after("high_ready", j + 1))
                    nc.vector.tensor_tensor(x_low[:, cols].bitcast(F32R), ps[:, j, :], x_high[:, cols], ALU.subtract)\
                        .then_inc(*ph.mark("low_ready"))
                dve.wait_ge(*ph.after("logit_psum", 1))
                shape = [P, T, E3]
                L = [lg[:, i, :].rearrange("p (t e) -> p t e", e=E3) for i in range(5)]
                logits = ps[:, 7, 0:T * E3].rearrange("p (t e) -> p t e", e=E3)
                link(nc.vector.tensor_reduce(st[:, 7, :], logits, AX.X, ALU.max))
                nc.vector.tensor_tensor(L[0], logits, bc(st[:, 7, :], shape), ALU.subtract).then_inc(*ph.mark("exp_in"))
                iota = K("iota8").unsqueeze(1).to_broadcast(shape)

                def router(step):
                    if step == 0:
                        dve.wait_ge(*ph.after("exp_out", 1))
                        link(nc.vector.tensor_reduce(st[:, 7, :], L[1], AX.X, ALU.add))
                        link(nc.vector.reciprocal(st[:, 8, :], st[:, 7, :]))
                        link(nc.vector.tensor_tensor(L[1], L[1], bc(st[:, 8, :], shape), ALU.mult))
                    if step == 1:
                        top2_onehots(link, L[1], L[2], None, None, st[:, 7, :], iota, shape)
                        link(nc.vector.scalar_tensor_tensor(L[4], L[2], -BIG, L[1], ALU.mult, ALU.add))
                    if step == 2:
                        top2_onehots(link, L[4], L[3], None, None, st[:, 7, :], iota, shape)
                    if step == 3:
                        link(nc.vector.tensor_tensor(L[2], L[2], L[3], ALU.add))
                        link(nc.vector.tensor_tensor(L[2], L[2], L[1], ALU.mult))
                        link(nc.vector.tensor_reduce(st[:, 7, :], L[2], AX.X, ALU.add))
                        link(nc.vector.tensor_scalar(st[:, 8, :], st[:, 7, :], 1e-9, None, ALU.add))
                        link(nc.vector.reciprocal(st[:, 9, :], st[:, 8, :]))
                        link(nc.vector.tensor_tensor(wt4[:, :, :], L[2], bc(st[:, 9, :], shape), ALU.mult))

                def mix(j):
                    dve.wait_ge(*ph.after("down_psum", E3 * (j + 1)))
                    if j == 0:
                        dve.wait_ge(led.sems["res_free"], 1)
                    for t in range(4):
                        tt = 4 * j + t
                        link(nc.vector.tensor_tensor(moe_w.rearrange("p (e d) -> p e d", e=E3),
                                                     ps[:, 4 + t, :].rearrange("p (e d) -> p e d", e=E3),
                                                     bc(wt4[:, tt, :], [P, E3, D]), ALU.mult))
                        link(nc.vector.tensor_reduce(sq[:, tt, :], moe_w.rearrange("p (e d) -> p d e", e=E3), AX.X, ALU.add))
                        nc.vector.tensor_tensor(res[:, tt, :], sq[:, tt, :], y[:, tt, :], ALU.add).then_inc(*ph.mark("mixed"))

                for n in range(NB * E3):
                    for c in range(2):
                        i = 2 * n + c
                        dve.wait_ge(*ph.after("silu_ready", i + 1))
                        dve.wait_ge(*ph.after("up_psum", i + 1))
                        if n >= 2:
                            dve.wait_ge(*ph.after("down_psum", n - 1))
                        nc.vector.tensor_tensor(hh[:, n % 2, c, :], sg[:, i % 2, :], ps[0:HC3, 2 * (i % 2) + 1, :], ALU.mult)\
                            .then_inc(*ph.mark("gated"))
                    if n < 4:
                        router(n)
                    if n % E3 == 0 and n > 0:
                        mix(n // E3 - 1)
                mix(NB - 1)
                ph.leave(dve)
                led.end_pass(dve, b + (B + 2))

        return led



def _tables():
    c = {}
    i = np.arange(P)
    c["ident"] = np.eye(P)
    c["mask_low"] = (i[None, :] <= i[:, None]).astype(np.int32)
    c["mask_line"] = (np.arange(P + 1)[None, :] == i[:, None] + 1).astype(np.int32)
    c["mask_future"] = (i[None, :] > i[:, None]).astype(np.int32)
    c["neg"] = np.full((P, 1), NEG)
    c["mean"] = np.full((P, P), 1.0 / S)
    c["half"] = np.repeat(np.array([[-0.5] * T + [0.5] * T]), P, 0)
    c["iota8"] = np.repeat(np.arange(8, 0, -1)[None].astype(float), P, 0)
    c["iota32"] = np.repeat(np.arange(32, 0, -1)[None].astype(float), P, 0)
    w = np.exp(np.arange(0, D, 2) * (-np.log(10000.0) / D))
    m = np.arange(S)

    def pe(pos):
        t = np.zeros((D, len(pos)))
        t[0::2], t[1::2] = np.sin(w[:, None] * pos), np.cos(w[:, None] * pos)
        return t
    a = -(m + 1.0)
    c["rot_c"] = np.repeat(np.cos(w[:, None] * a), 2, 0)
    s = np.sin(w[:, None] * a)
    c["rot_s"] = np.stack([-s, s], 1).reshape(D, S)
    inv = 1.0 / 10000.0 ** (np.arange(0, DH, 2) / DH)
    f = np.outer(np.concatenate([inv, inv]), m)
    c["rope_c"], c["rope_s"] = np.zeros((P, S)), np.zeros((P, S))
    for hd in range(HEADS):
        c["rope_c"][32 * hd:32 * hd + DH] = np.cos(f)
        c["rope_s"][32 * hd:32 * hd + DH] = np.sin(f) * np.where(np.arange(DH) < DH // 2, -1.0, 1.0)[:, None]
    return c, pe(m + S).astype(np.float32), pe(m).astype(np.float32)


def _layout(a):
    c, pe_low, pe_up = _tables()

    def aug(w, bias):
        return np.concatenate([w.T, bias[None, :]], 0)

    def rep(vec):
        return np.repeat(vec.reshape(1, -1), P, 0)
    c["tok_w"] = aug(a["L0_tok_W"], a["L0_tok_b"])
    c["pos"] = a["L0_tok_pos_embed"][0].reshape(TP, P, D).transpose(1, 0, 2).reshape(P, TP * D)
    for n in "qkv":
        c[n + "0"] = aug(a["L0_attn_W" + n], a["L0_attn_b" + n])
    c["wr0"] = np.concatenate([a["L0_ffn_Wr"], a["L0_ffn_br"][None]], 0)
    c["w1_0"] = np.concatenate([a["L0_ffn_W1"], a["L0_ffn_b1"][:, None, :]], 1).transpose(1, 0, 2).reshape(65, E0 * F0)
    c["w2_0"] = a["L0_ffn_W2"].transpose(1, 0, 2).reshape(P, E0 * D)
    c["b2_0"] = rep(a["L0_ffn_b2"])
    c["gamma0"], c["beta0"] = rep(a["L0_ffn_gamma"]), rep(a["L0_ffn_beta"])
    wq, bq = a["L1_attn_w_qkv"].reshape(2, 3, 32, D), a["L1_attn_b_qkv"].reshape(2, 3, 32)
    for i, n in enumerate("qkv"):
        c[n + "1"] = aug(wq[:, i].reshape(D, D), bq[:, i].reshape(D))
    c["proj1"] = aug(a["L1_attn_w_proj"], a["L1_attn_b_proj"])
    c["wi1"] = aug(a["L1_ffn_Wi"], a["L1_ffn_bi"])
    c["ws1"] = a["L1_ffn_Ws"][:, 0].transpose(2, 0, 1).reshape(P, 2 * HID1)
    c["bs1"] = a["L1_ffn_bs"][:, 0].T
    c["wo1"], c["bo1"] = a["L1_ffn_Wo"].T, rep(a["L1_ffn_bo"])
    c["w2a"] = aug(a["L2_attn_W"], a["L2_attn_b"])
    c["rw2"] = aug(a["L2_ffn_router_w"], a["L2_ffn_router_b"])
    c["w1_2"] = np.zeros((P, E2 * H2), np.float32)
    c["w1_2"][0:D] = a["L2_ffn_W1"].transpose(1, 0, 2).reshape(D, E2 * H2)
    for e in range(E2):
        c["w1_2"][D + e, H2 * e:H2 * (e + 1)] = a["L2_ffn_b1"][e]
        c["w1_2"][D + E2 + e, H2 * e:H2 * (e + 1)] = BIG
    c["w2_2"] = a["L2_ffn_W2"].reshape(C2, P, D).transpose(1, 0, 2).reshape(P, C2 * D)
    c["b2_2"] = np.zeros((P, D), np.float32)
    c["b2_2"][D:D + E2] = a["L2_ffn_b2"]
    c["gamma3"], c["beta3"] = rep(a["L3_attn_ln_gamma"]), rep(a["L3_attn_ln_beta"])
    c["wq3"], c["bq3"], c["uv3"] = np.zeros((D, HEADS, 80), np.float32), np.zeros((80, HEADS), np.float32), np.zeros((80, HEADS), np.float32)
    for hd in range(HEADS):
        sl = slice(DH * hd, DH * hd + DH)
        for r in (0, 64):
            c["wq3"][:, hd, r:r + DH] = a["L3_attn_Wq"][:, sl]
            c["bq3"][r:r + DH, hd] = a["L3_attn_bq"][sl]
        c["uv3"][0:DH, hd] = a["L3_attn_v_bias"][hd]
        c["uv3"][64:80, hd] = a["L3_attn_u_bias"][hd]
    c["wq3"] = c["wq3"].reshape(D, HEADS * 80)
    c["wk3"] = np.concatenate([a["L3_attn_Wk"], a["L3_attn_bk"][None]], 0)
    c["v3"] = np.concatenate([a["L3_attn_Wv"], a["L3_attn_bv"][None]], 0)
    swap = np.arange(D) ^ 1
    wp = a["L3_attn_Wpos"].reshape(D, HEADS, DH).transpose(2, 1, 0)
    c["wpos3"] = np.stack([wp, wp[:, :, swap]], 2).reshape(DH, HEADS * 2 * D)
    c["wout3"] = np.concatenate([a["L3_attn_Wout"], a["L3_attn_bout"][None]], 0)
    c["rms1"], c["rms2"] = rep(a["L3_ffn_ln1_w"]), rep(a["L3_ffn_ln2_w"])
    turned = np.concatenate([np.arange(DH // 2, DH), np.arange(DH // 2)])
    for n, kv in (("wq", HEADS), ("wk", 2)):
        w = a["L3_ffn_" + n].reshape(kv, DH, D)
        w = np.repeat(w, HEADS // kv, 0)
        z = np.zeros((2, HEADS, 32, D), np.float32)
        z[0, :, 0:DH], z[1, :, 0:DH] = w, w[:, turned]
        c[n + "4"] = z.reshape(2 * P, D).T
    c["wv4"], c["wo4"] = a["L3_ffn_wv"].T, a["L3_ffn_wo"].T
    c["rt4"] = a["L3_ffn_router_w"].T
    for n in (1, 3):
        c[f"w{n}_4"] = np.concatenate([a[f"L3_ffn_w{n}"].reshape(E3 * 2 * HC3, D).T] * 2, 0)
    c["w2_4"] = a["L3_ffn_w2"].reshape(E3, D, 2, HC3).transpose(3, 0, 2, 1).reshape(HC3, E3 * 2 * D)

    pack = np.zeros((P, CONST_COLS), np.float32)
    for name, (rows, at, cols) in CONST_AT.items():
        assert c[name].shape == (rows, cols), (name, c[name].shape)
        part = c[name]
        pack[0:rows, at:at + cols] = part.view(np.float32) if part.dtype == np.int32 else part
    x = a["x"][:, 0].reshape(B, P // 8, 8, 512 // 8, 8).transpose(0, 2, 4, 1, 3).reshape(B, D, NP_)
    patches = np.concatenate([x, np.ones((B, 1, NP_), np.float32)], 1)
    w_route = np.concatenate([a["L1_ffn_Wr"].transpose(0, 1, 3, 2), a["L1_ffn_br"][..., None]], 3)
    return {"consts": pack, "patches": patches, "txt": a["txt"], "route": a["L1_ffn_route_id"].reshape(1, B * NG),
            "w_route": w_route, "pe_low": pe_low, "pe_up": pe_up}


def kernel(**inputs):
    import numpy as _np
    import concourse.bacc as _bacc
    from concourse import mybir as _mybir
    from concourse.bass_utils import run_bass_kernel_spmd as _run

    arrays = _layout({k: _np.asarray(a) for k, a in inputs.items()})
    arrays = {f"in_{k}": _np.ascontiguousarray(a) for k, a in arrays.items()}
    nc = _bacc.Bacc("TRN2", target_bir_lowering=False, num_devices=1)
    args = {k[3:]: nc.dram_tensor(k, a.shape, _mybir.dt.from_np(a.dtype), kind="ExternalInput").ap() for k, a in arrays.items()}
    out = nc.dram_tensor("out_dram", (B, S, D), F32, kind="ExternalOutput").ap()
    build(nc, out=out, **args)
    r = _run(nc, [arrays], core_ids=[0])
    return r.results[0]["out_dram"]
```
